# Optimizing a Trainium2 kernel written in Bass

```python
import numpy as np
import jax
import jax.numpy as jnp

def _softmax(x, axis=-1):
    return jax.nn.softmax(x, axis=axis)

def _gelu(x):
    return jax.nn.gelu(x, approximate=True)

def _silu(x):
    return jax.nn.silu(x)

def _sigmoid(x):
    return jax.nn.sigmoid(x)

def _layernorm(x, axis=-1, eps=1e-05):
    m = jnp.mean(x, axis=axis, keepdims=True)
    v = jnp.var(x, axis=axis, keepdims=True)
    return (x - m) / jnp.sqrt(v + eps)

def _scatter_add(tgt, idx, src, axis=0):
    return tgt.at[idx].add(src)

def _segment_sum(src, seg, n):
    return jax.ops.segment_sum(src, seg, n)
kernel_name = 'mk_perceiver_d1_seqx_r4_193983'

def setup_inputs(seed: int=0):
    np.random.seed(seed)
    _w = jnp.asarray

    def _rec_inputs():
        import jax
        import jax.numpy as jnp
        _rk = jax.random.key(seed)
        x = -1.394e-06 + 0.9999 * jax.random.normal(jax.random.fold_in(_rk, 1), (64, 64, 256), jnp.float32)
        _lenS = 64 - jax.random.randint(jax.random.fold_in(_rk, 7), (64,), 0, max(1, 64 // 4) + 1, jnp.int32)
        _lenS2 = 256 - jax.random.randint(jax.random.fold_in(_rk, 8), (64,), 0, max(1, 256 // 4) + 1, jnp.int32)
        _ctx_1024P = jax.random.normal(jax.random.fold_in(_rk, 11), (64, 16, 256), jnp.float32)
        _ctx_1024c = jax.random.dirichlet(jax.random.fold_in(_rk, 511), 0.3 * jnp.ones((16,), jnp.float32), (64, 256))
        _ctx_1024t = jnp.einsum('bsk,bkd->bsd', _ctx_1024c, _ctx_1024P)
        _ctx_1024t = _ctx_1024t * jax.lax.rsqrt(jnp.mean(jnp.square(_ctx_1024t)) + 1e-12) * 0.953939
        ctx_1024 = 7.22013e-05 + 1.00017 * (_ctx_1024t + 0.3 * jax.random.normal(jax.random.fold_in(_rk, 611), (64, 256, 256), jnp.float32))
        _validS = jnp.arange(64)[None, :] < _lenS[:, None]
        _validS2 = jnp.arange(256)[None, :] < _lenS2[:, None]
        _causal = jnp.tril(jnp.ones((64, 64), dtype=bool))
        mask_Bx1x1xS2_bk0 = jnp.logical_not(jnp.broadcast_to(_validS2[:, None, None, :], (64, 1, 1, 256)))
        return (x, ctx_1024, mask_Bx1x1xS2_bk0)
    x, ctx_1024, mask_Bx1x1xS2_bk0 = _rec_inputs()

    def _L0_xattn_setup():
        import math
        import jax, jax.numpy as jnp
        import numpy as np
        NUM_BUCKETS = 32
        MAX_DISTANCE = 128
        H = 16
        D_MODEL = 256
        D_K = D_MODEL // H

        def _relative_position_bucket(relative_position):
            nb = NUM_BUCKETS // 2
            buckets = (relative_position > 0).astype(jnp.int32) * nb
            rp = jnp.abs(relative_position)
            max_exact = nb // 2
            is_small = rp < max_exact
            rp_large = max_exact + (jnp.log(jnp.maximum(rp, 1).astype(jnp.float32) / max_exact) / math.log(MAX_DISTANCE / max_exact) * (nb - max_exact)).astype(jnp.int32)
            rp_large = jnp.minimum(rp_large, nb - 1)
            return buckets + jnp.where(is_small, rp, rp_large)
        key = jax.random.key(seed)
        ks = jax.random.split(key, 8)
        B, T_k, T_q = (4, 512, 256)
        std = D_MODEL ** (-0.5)
        inp = {'src': jax.random.normal(ks[0], (B, T_k, D_MODEL), dtype=jnp.float32), 'dst': jax.random.normal(ks[1], (B, T_q, D_MODEL), dtype=jnp.float32), 'mask': jax.random.randint(ks[2], (B, 1, 1, T_k), 0, 2).astype(bool), 'Wq': jax.random.normal(ks[3], (D_MODEL, D_MODEL), dtype=jnp.float32) * std, 'Wk': jax.random.normal(ks[4], (D_MODEL, D_MODEL), dtype=jnp.float32) * std, 'Wv': jax.random.normal(ks[5], (D_MODEL, D_MODEL), dtype=jnp.float32) * std, 'Wo': jax.random.normal(ks[6], (D_MODEL, D_MODEL), dtype=jnp.float32) * std, 'rel_bias': jax.random.normal(ks[7], (H, NUM_BUCKETS), dtype=jnp.float32) * NUM_BUCKETS ** (-0.5)}
        return inp
    _L0_xattn_all = _L0_xattn_setup()
    _L0_xattn_in = {k: v for k, v in _L0_xattn_all.items() if k in ('Wq', 'Wk', 'Wv', 'Wo', 'rel_bias')}
    del _L0_xattn_all

    def _L0_attn_setup():
        import jax, jax.numpy as jnp
        import numpy as np
        import math
        B, N, DIM, H, DH, NNULL = (2, 512, 256, 16, 64, 2)
        SCALE = 8.0
        LN_EPS = 1e-05

        def _alibi_slopes(heads):
            start = 2.0 ** (-2.0 ** (-(math.log2(heads) - 3)))
            return np.array([start * start ** i for i in range(heads)], dtype=np.float32)

        def _l2norm(t):
            n = jnp.sqrt(jnp.sum(t * t, axis=-1, keepdims=True))
            return t / jnp.maximum(n, 1e-12)
        key = jax.random.key(seed)
        ks = jax.random.split(key, 6)
        inner = H * DH
        return {'x': jax.random.normal(ks[0], (B, N, DIM), dtype=jnp.float32), 'norm_g': jnp.ones((DIM,), jnp.float32), 'norm_b': jnp.zeros((DIM,), jnp.float32), 'Wq': jax.random.normal(ks[1], (DIM, inner), jnp.float32) * 0.02, 'Wkv': jax.random.normal(ks[2], (DIM, 2 * inner), jnp.float32) * 0.02, 'q_scale': jnp.ones((DH,), jnp.float32), 'k_scale': jnp.ones((DH,), jnp.float32), 'null_kv': jax.random.normal(ks[3], (H, 2 * NNULL, DH), jnp.float32), 'Wout': jax.random.normal(ks[4], (inner, DIM), jnp.float32) * 0.02}
    _L0_attn_all = _L0_attn_setup()
    _L0_attn_in = {k: v for k, v in _L0_attn_all.items() if k in ('norm_g', 'norm_b', 'Wq', 'Wkv', 'q_scale', 'k_scale', 'null_kv', 'Wout')}
    del _L0_attn_all

    def _L0_ffn_setup():
        import jax, jax.numpy as jnp
        import numpy as np
        B, S, D_MODEL, D_FF, E, R, TOP_K = (4, 512, 256, 1024, 8, 16, 2)
        key = jax.random.key(seed)
        ks = jax.random.split(key, 9)
        sd = 1.0 / np.sqrt(D_MODEL)
        return {'hidden_states': jax.random.normal(ks[0], (B, S, D_MODEL), jnp.float32), 'wi': jax.random.normal(ks[1], (D_FF, D_MODEL), jnp.float32) * sd, 'bi': jax.random.normal(ks[2], (D_FF,), jnp.float32) * 0.01, 'wo': jax.random.normal(ks[3], (D_MODEL, D_FF), jnp.float32) * (1.0 / np.sqrt(D_FF)), 'bo': jax.random.normal(ks[4], (D_MODEL,), jnp.float32) * 0.01, 'lora_A': jax.random.normal(ks[5], (E, R, D_MODEL), jnp.float32) * sd, 'lora_B': jax.random.normal(ks[6], (E, D_FF, R), jnp.float32) * 0.02, 'gate_w': jax.random.normal(ks[7], (E, D_MODEL), jnp.float32) * sd, 'gate_b': jax.random.normal(ks[8], (E,), jnp.float32) * 0.01}
    _L0_ffn_all = _L0_ffn_setup()
    _L0_ffn_in = {k: v for k, v in _L0_ffn_all.items() if k in ('wi', 'bi', 'wo', 'bo', 'lora_A', 'lora_B', 'gate_w', 'gate_b')}
    del _L0_ffn_all
    return {'x': x, 'ctx_1024': ctx_1024, 'mask_Bx1x1xS2_bk0': mask_Bx1x1xS2_bk0, 'L0_xattn_Wq': _L0_xattn_in['Wq'], 'L0_xattn_Wk': _L0_xattn_in['Wk'], 'L0_xattn_Wv': _L0_xattn_in['Wv'], 'L0_xattn_Wo': _L0_xattn_in['Wo'], 'L0_xattn_rel_bias': _L0_xattn_in['rel_bias'], 'L0_attn_norm_g': _L0_attn_in['norm_g'], 'L0_attn_norm_b': _L0_attn_in['norm_b'], 'L0_attn_Wq': _L0_attn_in['Wq'], 'L0_attn_Wkv': _L0_attn_in['Wkv'], 'L0_attn_q_scale': _L0_attn_in['q_scale'], 'L0_attn_k_scale': _L0_attn_in['k_scale'], 'L0_attn_null_kv': _L0_attn_in['null_kv'], 'L0_attn_Wout': _L0_attn_in['Wout'], 'L0_ffn_wi': _L0_ffn_in['wi'], 'L0_ffn_bi': _L0_ffn_in['bi'], 'L0_ffn_wo': _L0_ffn_in['wo'], 'L0_ffn_bo': _L0_ffn_in['bo'], 'L0_ffn_lora_A': _L0_ffn_in['lora_A'], 'L0_ffn_lora_B': _L0_ffn_in['lora_B'], 'L0_ffn_gate_w': _L0_ffn_in['gate_w'], 'L0_ffn_gate_b': _L0_ffn_in['gate_b']}

def reference(x, ctx_1024, mask_Bx1x1xS2_bk0, L0_xattn_Wq, L0_xattn_Wk, L0_xattn_Wv, L0_xattn_Wo, L0_xattn_rel_bias, L0_attn_norm_g, L0_attn_norm_b, L0_attn_Wq, L0_attn_Wkv, L0_attn_q_scale, L0_attn_k_scale, L0_attn_null_kv, L0_attn_Wout, L0_ffn_wi, L0_ffn_bi, L0_ffn_wo, L0_ffn_bo, L0_ffn_lora_A, L0_ffn_lora_B, L0_ffn_gate_w, L0_ffn_gate_b):
    import jax
    import jax.numpy as jnp

    def _L0_xattn_ref(src, dst, mask, Wq, Wk, Wv, Wo, rel_bias):
        import math
        import jax, jax.numpy as jnp
        import numpy as np
        NUM_BUCKETS = 32
        MAX_DISTANCE = 128
        H = 16
        D_MODEL = 256
        D_K = D_MODEL // H

        def _relative_position_bucket(relative_position):
            nb = NUM_BUCKETS // 2
            buckets = (relative_position > 0).astype(jnp.int32) * nb
            rp = jnp.abs(relative_position)
            max_exact = nb // 2
            is_small = rp < max_exact
            rp_large = max_exact + (jnp.log(jnp.maximum(rp, 1).astype(jnp.float32) / max_exact) / math.log(MAX_DISTANCE / max_exact) * (nb - max_exact)).astype(jnp.int32)
            rp_large = jnp.minimum(rp_large, nb - 1)
            return buckets + jnp.where(is_small, rp, rp_large)
        B, T_k, _ = src.shape
        T_q = dst.shape[1]
        q = (dst @ Wq.T).reshape(B, T_q, H, D_K)
        k = (src @ Wk.T).reshape(B, T_k, H, D_K)
        v = (src @ Wv.T).reshape(B, T_k, H, D_K)
        scores = jnp.einsum('bqhd,bkhd->bhqk', q, k)
        rel_pos = jnp.arange(T_k)[None, :] - jnp.arange(T_q)[:, None]
        rp_bucket = _relative_position_bucket(rel_pos)
        bias = rel_bias[:, rp_bucket]
        scores = scores + bias[None]
        scores = jnp.where(mask, scores, -1000000000.0)
        attn = jax.nn.softmax(scores, axis=-1)
        out = jnp.einsum('bhqk,bkhd->bqhd', attn, v).reshape(B, T_q, H * D_K)
        return out @ Wo.T

    def _L0_attn_ref(x, norm_g, norm_b, Wq, Wkv, q_scale, k_scale, null_kv, Wout):
        import jax, jax.numpy as jnp
        import numpy as np
        import math
        B, N, DIM, H, DH, NNULL = (2, 512, 256, 16, 64, 2)
        SCALE = 8.0
        LN_EPS = 1e-05

        def _alibi_slopes(heads):
            start = 2.0 ** (-2.0 ** (-(math.log2(heads) - 3)))
            return np.array([start * start ** i for i in range(heads)], dtype=np.float32)

        def _l2norm(t):
            n = jnp.sqrt(jnp.sum(t * t, axis=-1, keepdims=True))
            return t / jnp.maximum(n, 1e-12)
        b, n, dim = x.shape
        h, dh, nn = (H, DH, NNULL)
        j = n + nn
        mu = jnp.mean(x, axis=-1, keepdims=True)
        var = jnp.mean((x - mu) ** 2, axis=-1, keepdims=True)
        xn = (x - mu) * jax.lax.rsqrt(var + LN_EPS) * norm_g + norm_b
        q = (xn @ Wq).reshape(b, n, h, dh).transpose(0, 2, 1, 3)
        kv = x @ Wkv
        k, v = jnp.split(kv, 2, axis=-1)
        k = k.reshape(b, n, h, dh).transpose(0, 2, 1, 3)
        v = v.reshape(b, n, h, dh).transpose(0, 2, 1, 3)
        null = null_kv.reshape(h, nn, 2, dh)
        nk = jnp.broadcast_to(null[:, :, 0, :][None], (b, h, nn, dh))
        nv = jnp.broadcast_to(null[:, :, 1, :][None], (b, h, nn, dh))
        k = jnp.concatenate([nk, k], axis=2)
        v = jnp.concatenate([nv, v], axis=2)
        q = _l2norm(q) * q_scale
        k = _l2norm(k) * k_scale
        sim = jnp.einsum('bhid,bhjd->bhij', q, k) * SCALE
        irow = jnp.arange(j - n, j)
        jcol = jnp.arange(j)
        bias = -jnp.abs(jcol[None, :] - irow[:, None]).astype(sim.dtype)
        slopes = jnp.asarray(_alibi_slopes(h))[:, None, None]
        sim = sim + slopes * bias
        causal = jnp.triu(jnp.ones((n, j), dtype=bool), k=j - n + 1)
        neg = jnp.finfo(sim.dtype).max
        sim = jnp.where(causal[None, None], -neg, sim)
        attn = jax.nn.softmax(sim, axis=-1)
        out = jnp.einsum('bhij,bhjd->bhid', attn, v)
        out = out.transpose(0, 2, 1, 3).reshape(b, n, h * dh)
        return out @ Wout

    def _L0_ffn_ref(hidden_states, wi, bi, wo, bo, lora_A, lora_B, gate_w, gate_b):
        import jax, jax.numpy as jnp
        import numpy as np
        B, S, D_MODEL, D_FF, E, R, TOP_K = (4, 512, 256, 1024, 8, 16, 2)
        logits = jnp.einsum('bsd,ed->bse', hidden_states, gate_w) + gate_b
        scores = jax.nn.softmax(logits, axis=-1)
        top_v, top_i = jax.lax.top_k(scores, TOP_K)
        val_sum = top_v.sum(axis=-1)
        out = jnp.zeros_like(hidden_states)
        for e in range(E):
            count = (top_i == e).sum(axis=-1).astype(hidden_states.dtype)
            gate = count * val_sum
            inter = jnp.einsum('bsd,fd->bsf', hidden_states, wi) + bi + jnp.einsum('bsr,fr->bsf', jnp.einsum('bsd,rd->bsr', hidden_states, lora_A[e]), lora_B[e])
            h = jax.nn.relu(inter)
            expert_out = jnp.einsum('bsf,df->bsd', h, wo) + bo
            out = out + gate[..., None] * expert_out
        return out
    x = x + _L0_xattn_ref(ctx_1024, _layernorm(x, axis=-1), mask_Bx1x1xS2_bk0, L0_xattn_Wq, L0_xattn_Wk, L0_xattn_Wv, L0_xattn_Wo, L0_xattn_rel_bias)
    x = x + _L0_attn_ref(_layernorm(x, axis=-1), L0_attn_norm_g, L0_attn_norm_b, L0_attn_Wq, L0_attn_Wkv, L0_attn_q_scale, L0_attn_k_scale, L0_attn_null_kv, L0_attn_Wout)
    x = x + _L0_ffn_ref(_layernorm(x, axis=-1), L0_ffn_wi, L0_ffn_bi, L0_ffn_wo, L0_ffn_bo, L0_ffn_lora_A, L0_ffn_lora_B, L0_ffn_gate_w, L0_ffn_gate_b)
    return x

_drawn_inputs = setup_inputs


def setup_inputs(seed=0):
    import zlib

    import numpy as np

    out = dict(_drawn_inputs(seed))
    spreads = {'L0_attn_norm_g': (1.0, 0.6),
     'L0_attn_norm_b': (0.0, 0.8),
     'L0_attn_q_scale': (1.0, 0.6),
     'L0_attn_k_scale': (1.0, 0.6)}
    factors = {'L0_xattn_rel_bias': 8.0, 'L0_ffn_bi': 8.0, 'L0_ffn_bo': 8.0, 'L0_ffn_gate_b': 8.0}
    for name, (base, spread) in spreads.items():
        noise = np.random.default_rng([zlib.crc32(name.encode()), seed]).standard_normal(out[name].shape)
        drawn = base * np.exp(spread * noise) if base else spread * noise
        out[name] = jnp.asarray(drawn.astype(out[name].dtype))
    for name, factor in factors.items():
        out[name] = (out[name] * factor).astype(out[name].dtype)
    return out
```

```python
from contextlib import ExitStack

import numpy as np

import concourse.bass as bass
from concourse import mybir

F32 = mybir.dt.float32
I32, U8 = mybir.dt.int32, mybir.dt.uint8
ALU = mybir.AluOpType
ACT = mybir.ActivationFunctionType
AX = mybir.AxisListType.X

P = 128
B, TQ, TK, D = 64, 64, 256, 256
BU = P // TQ
UNITS = B // BU
KD = D // P
XH, XD = 16, D // 16
XPAIRS = XH // 2
XTILES = BU * XPAIRS
NBUCKET, DIAGS = 32, TQ + TK
AH, AD, NNULL = 16, 64, 2
INNER = AH * AD
AK = TQ + NNULL
APAIRS = AH // 2
FF, E, R = 1024, 8, 16
FC = FF // P
EPS = 1e-5
MASKED = float(2.0 ** 100)
BIG = 3.0e38

PER_UNIT = dict(
    x_loaded=16, ctx_loaded=16, mask_loaded=16, out_stored=16,
    x_stats=2, x_rstd=2, x_normed=1, x_kept=1, x_turned=1, x_turned_copied=1, q_done=1,
    q_spread=1, k_done=2, k_copied=2, v_done=2, v_copied=2, mask_scaled=1, bias_masked=2,
    scores_done=XTILES, biased=XTILES, exp_done=XTILES, recip_done=XTILES, probs_ready=XTILES,
    probs_turned=XTILES, probs_copied=XTILES, pv_done=XTILES, merge_a=1, merge_b=2, xo_done=1,
    x1_ready=1,
    a_kept=1, a_stats=4, a_rstd=4, a_normed=2, a_turned=1, a_turned_copied=2, aq_done=2, ak_done=2,
    av_done=2, aq_copied=2, ak_copied=2, av_copied=4, a_squared=2, a_sumsq=2, a_len=4, a_unit=2,
    aq_turned=2, aq_spread=2, ak_turned=2, ak_placed=2, as_done=4, as_biased=4, a_soft=5,
    a_exp=1, ap_turned=4, ap_copied=4, apv_done=2, apv_copied=2, ao_done=1, x2_ready=1,
    f_kept=1, f_stats=2, f_rstd=2, f_normed=1, f_turned=1, f_turned_copied=1, z_done=1,
    z_copied=1, f_exp=1, route=9, z_routed=3, z_turned=1, z_turned_copied=1,
    hid_first=2, relu_done=2, hid_second=2, hid_ready=2, y_done=1, y_sum=1, out_ready=1,
)
ONCE = ("consts", "table_stored", "table_loaded", "set_pe", "set_act", "set_dve", "set_pool",
        "half")


def constants():
    r = np.arange(DIAGS) - (TQ - 1)
    far = 8 + sum((np.abs(r) >= t).astype(np.int64) for t in (12, 16, 23, 32, 46, 64, 91))
    bucket = (r > 0) * 16 + np.where(np.abs(r) < 8, np.abs(r), far)
    onehot = (bucket[None, :] == np.arange(NBUCKET)[:, None]).astype(np.float32)
    start = 2.0 ** (-2.0 ** (-(np.log2(AH) - 3)))
    slopes = np.array([start * start ** i for i in range(AH)], dtype=np.float32)
    q = np.arange(TQ)[:, None]
    col = np.concatenate([NNULL + np.arange(TQ), np.arange(NNULL)])[None, :]
    dist = -np.abs(col - (q + NNULL)).astype(np.float32)
    alibi = slopes[None, :, None] * dist[:, None, :]
    alibi = np.where((col > q + NNULL)[:, None, :], np.float32(-MASKED), alibi)
    alibi = np.tile(alibi, (BU, 1, 1)).astype(np.float32)
    row = np.arange(P)
    headmask = (row[:, None] // XD == np.arange(8)[None, :]).astype(np.float32)
    parity = (row[:, None] // XD % 2 == np.arange(2)[None, :]).astype(np.float32)
    lower = np.tile((np.arange(E)[None, :] < np.arange(E)[:, None]).astype(np.float32)[None],
                    (P, 1, 1))
    return dict(c_ident=np.eye(P, dtype=np.float32), c_onehot=onehot, c_alibi=alibi,
                c_headmask=headmask, c_parity=parity, c_lower=lower)


def build(nc, io, out):
    with ExitStack() as ctx:
        def sb(name, shape, dt=F32):
            return ctx.enter_context(nc.sbuf_tensor(name, shape, dt))

        def bank(name):
            return ctx.enter_context(nc.psum_tensor(name, [P, 512], F32))

        sem = {n: ctx.enter_context(nc.semaphore(n)) for n in (*PER_UNIT, *ONCE)}

        def at(name, u, k):
            return u * PER_UNIT[name] + k

        def seen(u):
            return not isinstance(u, int) or u >= 0

        def lone(eng, name, u, k):
            value = at(name, u, k)
            if not isinstance(value, int):
                value = eng.to_reg(value)
                eng.wait_ge(sem["consts"], 16)
            return value

        wq, wk, wv, wo = (sb(n, [P, KD, D]) for n in ("wq", "wk", "wv", "wo"))
        a_wq, a_wkv = sb("a_wq", [P, KD, INNER]), sb("a_wkv", [P, KD, 2 * INNER])
        a_wo = sb("a_wo", [P, APAIRS, D])
        f_wi, f_wo = sb("f_wi", [P, KD, FF]), sb("f_wo", [P, FC, D])
        f_loraB, f_zw = sb("f_loraB", [P, FF]), sb("f_zw", [P, KD, P + E])
        f_bi, f_bo2, f_gb = sb("f_bi", [P, FC]), sb("f_bo2", [P, D]), sb("f_gb", [P, E])
        f_nbi = sb("f_nbi", [P, FC])
        ident, alibi = sb("ident", [P, P]), sb("alibi", [P, AH, AK])
        headmask, parity = sb("headmask", [P, 8]), sb("parity", [P, 2])
        lower = sb("lower", [P, E, E])
        a_g, a_b, a_qs, a_ks = sb("a_g", [P, KD]), sb("a_b", [P, KD]), sb("a_qs", [P, 1]), sb("a_ks", [P, 1])
        relT, onehot = sb("relT", [NBUCKET, XH]), sb("onehot", [NBUCKET, DIAGS])
        reltab = sb("reltab", [XH, DIAGS])
        bias = sb("bias", [P, XPAIRS, TK])
        nulls = sb("nulls", [AH * NNULL, AD])
        null_sq = sb("null_sq", [AH * NNULL, AD])
        null_len, half = sb("null_len", [AH * NNULL, 2]), sb("half", [P, 2 * AH])
        x_ld, x_res, x_n = sb("x_ld", [P, D]), sb("x_res", [P, D]), sb("x_n", [P, D])
        ctxT, mask32, negm = sb("ctxT", [P, KD, BU, TK]), sb("mask32", [P, BU * TK // 4], I32), sb("negm", [P, BU, TK])
        x_st, x_mv, x_rs = sb("x_st", [P, 6]), sb("x_mv", [P, 2]), sb("x_rs", [P, 2])
        xnT = sb("xnT", [P, KD, P])
        qbd = sb("qbd", [P, KD, BU, 8, TQ])
        kT, v = sb("kT", [P, KD, BU, TK]), sb("v", [P, BU * 2, D])
        bm = sb("bm", [P, BU, XPAIRS, TK])
        S = sb("S", [P, 4, TK])
        x_nmx, x_sum, x_inv = sb("x_nmx", [P, XTILES]), sb("x_sum", [P, XTILES]), sb("x_inv", [P, XTILES])
        pT = sb("pT", [P, 2, 2, P])
        o_half, oT = sb("o_half", [P, KD, BU, TQ]), sb("oT", [P, KD, BU, TQ])
        x1 = sb("x1", [P, D])
        a_res, a_x, a_n = sb("a_res", [P, D]), sb("a_x", [P, D]), sb("a_n", [P, D])
        a_st, a_mv, a_rs = sb("a_st", [P, 2, 6]), sb("a_mv", [P, 2, 2]), sb("a_rs", [P, 2, 2])
        aT = sb("aT", [P, 2, KD, P])
        a_raw = sb("a_raw", [P, 2, AH, AD])
        a_sq = sb("a_sq", [P, AH, AD])
        a_len = sb("a_len", [P, 2, AH])
        a_qk = sb("a_qk", [P, 1])
        qz = sb("qz", [P, AH, P])
        akT = sb("akT", [P, APAIRS, BU, AK])
        av = sb("av", [AK, BU, INNER])
        aS = sb("aS", [P, AH, AK])
        a_mx, a_sum = sb("a_mx", [P, AH]), sb("a_sum", [P, AH])
        apT, aoT = sb("apT", [AK, AH, P]), sb("aoT", [P, APAIRS, P])
        x2 = sb("x2", [P, D])
        f_res, f_n, f_out, f_t = (sb(n, [P, D]) for n in ("f_res", "f_n", "f_out", "f_t"))
        f_st, f_mv, f_rs = sb("f_st", [P, 6]), sb("f_mv", [P, 2]), sb("f_rs", [P, 2])
        fT = sb("fT", [P, KD, P])
        z = sb("z", [P, P + E])
        g_e, g_s, g_gt, g_eq = sb("g_e", [P, E]), sb("g_s", [P, E]), sb("g_gt", [P, E, E]), sb("g_eq", [P, E, E])
        g_rank, g_sel, g_1 = sb("g_rank", [P, E]), sb("g_sel", [P, 3, E]), sb("g_1", [P, 4])
        g_top = sb("g_top", [P, E])
        zr, zT = sb("zr", [P, 3, E, R]), sb("zT", [P, 2, P])
        f_r, f_h = sb("f_r", [P, FC, P]), sb("f_h", [P, FC, P])

        ps_s = [bank("ps_s0"), bank("ps_s1")]
        ps_t = [bank("ps_t0"), bank("ps_t1")]
        ps_o = bank("ps_o")
        ps_a = [bank("ps_a0"), bank("ps_a1")]
        ps_f = bank("ps_f")

        table = nc.dram_tensor("table", [XH, TQ, DIAGS], F32)
        table_ap = table.ap()

        block = ctx.enter_context(nc.Block())

        def tiles4(ap):
            return ap.rearrange("p (n c) -> p n c", n=4)

        def steps(eng, step):
            for i in range(3):
                step(i, True, i >= 1, i >= 2)
            with eng.Fori(3, UNITS - 1) as i:
                step(i, True, True, True)
            for i in range(UNITS - 1, UNITS + 2):
                step(i, i < UNITS, i - 1 < UNITS, True)

        N_CONST = 30

        @block.sync
        def _(sp):
            def load(u):
                if seen(u - 1):
                    sp.wait_ge(sem["x_normed"], lone(sp, "x_normed", u - 1, 1))
                if seen(u - 1):
                    sp.wait_ge(sem["x_kept"], lone(sp, "x_kept", u - 1, 1))
                sp.dma_start(x_ld[:], io["x"][bass.ts(u, P), :]).then_inc(sem["x_loaded"], 16)
                if seen(u - 1):
                    sp.wait_ge(sem["mask_scaled"], lone(sp, "mask_scaled", u - 1, 1))
                sp.dma_start(mask32[:], io["mask"][bass.ts(u, 1), :].broadcast_to([P, BU * TK // 4])).then_inc(sem["mask_loaded"], 16)
                if seen(u - 1):
                    sp.wait_ge(sem["k_done"], lone(sp, "k_done", u - 1, 2))
                if seen(u - 1):
                    sp.wait_ge(sem["v_done"], lone(sp, "v_done", u - 1, 2))
                sp.dma_start(ctxT[:].rearrange("p c b k -> p (c b k)"),
                             io["ctxT"][bass.ts(u, P), :]).then_inc(sem["ctx_loaded"], 16)

            def const(dst, src):
                sp.dma_start(dst, src).then_inc(sem["consts"], 16)
                const.n += 1
            const.n = 0

            def rows(name):
                return io[name].rearrange("(c p) n -> p c n", p=P)

            load(0)
            const(wk[:], rows("wkT"))
            const(wv[:], rows("wvT"))
            const(wq[:], rows("wqT"))
            const(ident[:], io["c_ident"])
            const(headmask[:], io["c_headmask"])
            const(parity[:], io["c_parity"])
            const(relT[:], io["relT"])
            const(onehot[:], io["c_onehot"])
            const(nulls[:], io["null_k"])
            const(av[TQ:AK, 0, :], io["null_v"])
            const(av[TQ:AK, 1, :], io["null_v"])
            const(wo[:], rows("woT"))
            const(a_wq[:], rows("a_wq"))
            const(a_wkv[:], rows("a_wkv"))
            const(alibi[:], io["c_alibi"])
            const(a_wo[:], rows("a_wo"))
            const(f_wi[:], rows("f_wiT"))
            const(f_wo[:], rows("f_woT"))
            const(f_loraB[:], io["f_loraB"])
            const(f_zw[:, :, 0:P], rows("f_loraA"))
            const(f_zw[:, :, P:P + E], rows("f_gateT"))
            const(f_bi[:], io["f_bi"])
            const(f_bo2[:], io["f_bo"].partition_broadcast(P))
            const(f_gb[:], io["f_gb"].partition_broadcast(P))
            const(lower[:], io["c_lower"])
            const(a_g[:], io["a_g"])
            const(a_b[:], io["a_b"])
            for h2 in range(2):
                const(a_qs[h2 * AD:(h2 + 1) * AD, :], io["a_qs"])
            const(a_ks[0:AD, :], io["a_ks"])
            assert const.n == N_CONST
            sp.dma_start(a_ks[AD:P, :], io["a_ks"]).then_inc(sem["consts"], 16)
            sp.wait_ge(sem["set_dve"], 1)
            sp.dma_start(table_ap, reltab[:].unsqueeze(1).broadcast_to([XH, TQ, DIAGS]))\
                .then_inc(sem["table_stored"], 16)
            sp.wait_ge(sem["table_stored"], 16)
            for h2 in range(2):
                src = bass.AP(table_ap.tensor, h2 * TQ * DIAGS + TQ - 1,
                              [[DIAGS - 1, TQ], [2 * TQ * DIAGS, XPAIRS], [1, TK]])
                sp.dma_start(bias[h2 * TQ:(h2 + 1) * TQ, :, :], src).then_inc(sem["table_loaded"], 16)

            def step(i, do_x, do_a, do_f):
                if do_x and not (isinstance(i, int) and i + 1 >= UNITS):
                    load(i + 1)
                if do_f:
                    u = i - 2
                    sp.wait_ge(sem["out_ready"], lone(sp, "out_ready", u, 1))
                    sp.dma_start(out[bass.ts(u, P), :], f_out[:]).then_inc(sem["out_stored"], 16)

            steps(sp, step)
            sp.wait_ge(sem["out_stored"], 16 * UNITS)

        ALL_CONST = 16 * (N_CONST + 1)

        @block.tensor
        def _(pe):
            mm, turn = nc.tensor.matmul, nc.tensor.transpose

            def setup():
                pe.wait_ge(sem["consts"], ALL_CONST)
                mm(ps_s[0][0:XH, 0:DIAGS], relT[:], onehot[:], start=True, stop=True)\
                    .then_inc(sem["set_pe"], 1)
                for c in range(FC):
                    last = mm(ps_f[:, 0:D], f_bi[:, c:c + 1].broadcast_to([P, P]), f_wo[:, c, :],
                              start=(c == 0), stop=(c == FC - 1))
                last.then_inc(sem["set_pe"], 1)
                pe.wait_ge(sem["set_pool"], 3)
                turn(ps_a[0][0:AD, 0:AH * NNULL], nulls[:], ident[0:32, 0:32])\
                    .then_inc(sem["set_pe"], 1)
                pe.wait_ge(sem["set_dve"], 2)
                pe.wait_ge(sem["set_act"], 1)

            def x_kv(u):
                pe.wait_ge(sem["ctx_loaded"], at("ctx_loaded", u, 16))
                for g in range(KD):
                    if seen(u - 1):
                        pe.wait_ge(sem["biased"], at("biased", u - 1, XTILES - 1 + g))
                    for c in range(KD):
                        last = mm(ps_s[g][:], wk[:, c, g * P:(g + 1) * P],
                                  ctxT[:, c].rearrange("p b k -> p (b k)"), start=(c == 0), stop=(c == KD - 1))
                    last.then_inc(sem["k_done"], 1)
                ct = ctxT[:].rearrange("p c b k -> p c (b k)")
                for n in range(2):
                    if seen(u - 1):
                        pe.wait_ge(sem["probs_copied"], at("probs_copied", u - 1, XTILES - 1 + n))
                    for j in range(2):
                        t = 2 * n + j
                        for c in range(KD):
                            last = mm(ps_t[n][:, j * D:(j + 1) * D], ct[:, c, t * P:(t + 1) * P],
                                      wv[:, c, :], start=(c == 0), stop=(c == KD - 1))
                    last.then_inc(sem["v_done"], 1)

            def x_turn(u):
                pe.wait_ge(sem["x_normed"], at("x_normed", u, 1))
                if seen(u - 1):
                    pe.wait_ge(sem["x1_ready"], at("x1_ready", u - 1, 1))
                for c in range(KD):
                    last = turn(ps_o[:, c * P:(c + 1) * P], x_n[:, c * P:(c + 1) * P], ident[:])
                last.then_inc(sem["x_turned"], 1)

            def x_q(u):
                pe.wait_ge(sem["x_turned_copied"], at("x_turned_copied", u, 1))
                for g in range(KD):
                    for c in range(KD):
                        last = mm(ps_o[:, 256 + g * P:256 + (g + 1) * P], wq[:, c, g * P:(g + 1) * P],
                                  xnT[:, c, :], start=(c == 0), stop=(c == KD - 1))
                last.then_inc(sem["q_done"], 1)

            def x_scores(u, t):
                b, pair = t // XPAIRS, t % XPAIRS
                g, p4 = pair // 4, pair % 4
                if t == 0:
                    pe.wait_ge(sem["q_spread"], at("q_spread", u, 1))
                    pe.wait_ge(sem["k_copied"], at("k_copied", u, 2))
                elif t >= 2:
                    pe.wait_ge(sem["biased"], at("biased", u, t - 1))
                mm(ps_s[t % 2][:, 0:TK], qbd[:, g, b, 2 * p4:2 * p4 + 2, :].rearrange("p h q -> p (h q)"),
                   kT[:, g, b, :], start=True, stop=True).then_inc(sem["scores_done"], 1)

            def x_turn_probs(u, t):
                pe.wait_ge(sem["probs_ready"], at("probs_ready", u, t + 1))
                if t < 2:
                    pe.wait_ge(sem["v_copied"], at("v_copied", u, t + 1))
                else:
                    pe.wait_ge(sem["probs_copied"], at("probs_copied", u, t - 1))
                for c in range(2):
                    last = turn(ps_t[t % 2][:, c * P:(c + 1) * P], S[:, t % 4, c * P:(c + 1) * P], ident[:])
                last.then_inc(sem["probs_turned"], 1)

            def x_pv(u, t):
                b, pair = t // XPAIRS, t % XPAIRS
                g, p4 = pair // 4, pair % 4
                pe.wait_ge(sem["probs_copied"], at("probs_copied", u, t + 1))
                if t == 0:
                    pe.wait_ge(sem["v_copied"], at("v_copied", u, 2))
                o = ps_o[32 * p4:32 * p4 + 32, (g * BU + b) * P:(g * BU + b + 1) * P]
                for c in range(2):
                    last = mm(o, v[:, 2 * b + c, pair * 32:(pair + 1) * 32], pT[:, t % 2, c, :],
                              start=(c == 0), stop=(c == 1))
                last.then_inc(sem["pv_done"], 1)

            def x_out(u):
                pe.wait_ge(sem["merge_b"], at("merge_b", u, 2))
                for g in range(KD):
                    last = mm(ps_o[:, 0:D], oT[:, g].rearrange("p b q -> p (b q)"), wo[:, g, :],
                              start=(g == 0), stop=(g == KD - 1))
                last.then_inc(sem["xo_done"], 1)

            def a_turn(u):
                pe.wait_ge(sem["a_normed"], at("a_normed", u, 2))
                if seen(u - 1):
                    pe.wait_ge(sem["apv_copied"], at("apv_copied", u - 1, 1))
                for n, src in enumerate((a_x, a_n)):
                    for c in range(KD):
                        last = turn(ps_a[0][:, (n * KD + c) * P:(n * KD + c + 1) * P],
                                    src[:, c * P:(c + 1) * P], ident[:])
                last.then_inc(sem["a_turned"], 1)

            def a_q(u):
                pe.wait_ge(sem["a_turned_copied"], at("a_turned_copied", u, 2))
                for n in range(2):
                    if n == 0:
                        if seen(u - 1):
                            pe.wait_ge(sem["x2_ready"], at("x2_ready", u - 1, 1))
                    for c in range(KD):
                        last = mm(ps_a[1 - n][:], aT[:, 1, c, :], a_wq[:, c, n * 512:(n + 1) * 512],
                                  start=(c == 0), stop=(c == KD - 1))
                    last.then_inc(sem["aq_done"], 1)

            def a_k(u):
                for n in range(2):
                    pe.wait_ge(sem["aq_copied"], at("aq_copied", u, n + 1))
                    for c in range(KD):
                        last = mm(ps_a[1 - n][:], aT[:, 0, c, :], a_wkv[:, c, n * 512:(n + 1) * 512],
                                  start=(c == 0), stop=(c == KD - 1))
                    last.then_inc(sem["ak_done"], 1)

            def a_v(u):
                for n in range(2):
                    pe.wait_ge(sem["ak_copied"], at("ak_copied", u, n + 1))
                    for c in range(KD):
                        last = mm(ps_a[1 - n][:], aT[:, 0, c, :],
                                  a_wkv[:, c, INNER + n * 512:INNER + (n + 1) * 512],
                                  start=(c == 0), stop=(c == KD - 1))
                    last.then_inc(sem["av_done"], 1)

            def a_turn_qk(u, which):
                pe.wait_ge(sem["a_unit"], at("a_unit", u, which + 1))
                for n in range(2):
                    if which == 0:
                        pe.wait_ge(sem["av_copied"], at("av_copied", u, 2 * n + 2))
                    else:
                        pe.wait_ge(sem["aq_spread"], at("aq_spread", u, n + 1))
                    for j in range(4):
                        pair = 4 * n + j
                        last = turn(ps_a[1 - n][:, j * P:(j + 1) * P],
                                    a_raw[:, which, 2 * pair:2 * pair + 2, :].rearrange("p h d -> p (h d)"),
                                    ident[:])
                    last.then_inc(sem["ak_turned" if which else "aq_turned"], 1)

            def a_scores(u, n):
                if n < 2:
                    pe.wait_ge(sem["ak_placed"], at("ak_placed", u, 2))
                else:
                    pe.wait_ge(sem["as_biased"], at("as_biased", u, n - 1))
                for j in range(4):
                    h = 4 * n + j
                    for b in range(BU):
                        last = mm(ps_a[(n + 1) % 2][b * TQ:(b + 1) * TQ, j * AK:(j + 1) * AK],
                                  qz[:, h, b * TQ:(b + 1) * TQ], akT[:, h // 2, b, :],
                                  start=True, stop=True)
                last.then_inc(sem["as_done"], 1)

            def a_turn_probs(u, n):
                if n < 2:
                    pe.wait_ge(sem["a_soft"], at("a_soft", u, 5))
                else:
                    pe.wait_ge(sem["ap_copied"], at("ap_copied", u, n - 1))
                for j in range(4):
                    last = turn(ps_a[(n + 1) % 2][0:AK, j * P:(j + 1) * P], aS[:, 4 * n + j, :], ident[:])
                last.then_inc(sem["ap_turned"], 1)

            def a_pv(u, n):
                pe.wait_ge(sem["ap_copied"], at("ap_copied", u, 4))
                for j in range(8):
                    h = 8 * n + j
                    for b in range(BU):
                        last = mm(ps_a[1 - n][(h % 2) * AD:(h % 2 + 1) * AD,
                                              (j // 2) * P + b * TQ:(j // 2) * P + (b + 1) * TQ],
                                  av[:, b, h * AD:(h + 1) * AD], apT[:, h, b * TQ:(b + 1) * TQ],
                                  start=True, stop=True)
                last.then_inc(sem["apv_done"], 1)

            def a_out(u):
                pe.wait_ge(sem["apv_copied"], at("apv_copied", u, 2))
                for c in range(APAIRS):
                    last = mm(ps_a[1][:, 0:D], aoT[:, c, :], a_wo[:, c, :],
                              start=(c == 0), stop=(c == APAIRS - 1))
                last.then_inc(sem["ao_done"], 1)

            def f_turn(u):
                pe.wait_ge(sem["f_normed"], at("f_normed", u, 1))
                if seen(u - 1):
                    pe.wait_ge(sem["y_sum"], at("y_sum", u - 1, 1))
                for c in range(KD):
                    last = turn(ps_f[:, c * P:(c + 1) * P], f_n[:, c * P:(c + 1) * P], ident[:])
                last.then_inc(sem["f_turned"], 1)

            def f_z(u):
                pe.wait_ge(sem["f_turned_copied"], at("f_turned_copied", u, 1))
                for c in range(KD):
                    last = mm(ps_f[:, 0:P + E], fT[:, c, :], f_zw[:, c, :], start=(c == 0), stop=(c == KD - 1))
                last.then_inc(sem["z_done"], 1)

            def f_turn_z(u):
                pe.wait_ge(sem["z_routed"], at("z_routed", u, 3))
                pe.wait_ge(sem["z_copied"], at("z_copied", u, 1))
                for n, m in enumerate((0, 2)):
                    last = turn(ps_f[:, n * P:(n + 1) * P], zr[:, m].rearrange("p e r -> p (e r)"), ident[:])
                last.then_inc(sem["z_turned"], 1)

            def f_first(u, n):
                if n == 0:
                    pe.wait_ge(sem["z_turned_copied"], at("z_turned_copied", u, 1))
                else:
                    pe.wait_ge(sem["hid_ready"], at("hid_ready", u, 1))
                for j in range(4):
                    f = (4 * n + j) * P
                    for c in range(KD):
                        mm(ps_f[:, j * P:(j + 1) * P], f_wi[:, c, f:f + P], fT[:, c, :],
                           start=(j == 0 and c == 0), stop=False, skip_group_check=True)
                    last = mm(ps_f[:, j * P:(j + 1) * P], f_loraB[:, f:f + P], zT[:, 0, :],
                              start=False, stop=False, skip_group_check=True)
                last.then_inc(sem["hid_first"], 1)

            def f_second(u, n):
                pe.wait_ge(sem["relu_done"], at("relu_done", u, n + 1))
                for j in range(4):
                    f = (4 * n + j) * P
                    last = mm(ps_f[:, j * P:(j + 1) * P], f_loraB[:, f:f + P], zT[:, 1, :],
                              start=False, stop=(j == 3), skip_group_check=True)
                last.then_inc(sem["hid_second"], 1)

            def f_y(u):
                pe.wait_ge(sem["hid_ready"], at("hid_ready", u, 2))
                for c in range(FC):
                    last = mm(ps_f[:, 0:D], f_h[:, c, :], f_wo[:, c, :], start=(c == 0), stop=(c == FC - 1))
                last.then_inc(sem["y_done"], 1)

            setup()

            def step(i, do_x, do_a, do_f):
                ua, uf = i - 1, i - 2
                if do_x:
                    x_kv(i)
                    x_turn(i)
                if do_a:
                    a_turn(ua)
                if do_f:
                    f_turn(uf)
                if do_x:
                    x_q(i)
                if do_f:
                    f_z(uf)
                if do_a:
                    a_q(ua)
                for t in range(XTILES + 3):
                    if do_x:
                        if t < XTILES:
                            x_scores(i, t)
                        if 2 <= t < XTILES + 2:
                            x_turn_probs(i, t - 2)
                        if t >= 3:
                            x_pv(i, t - 3)
                    if do_a:
                        if t == 0:
                            a_k(ua)
                        if t == 1:
                            a_v(ua)
                        if t == 4:
                            a_turn_qk(ua, 0)
                        if t == 5:
                            a_turn_qk(ua, 1)
                        if 6 <= t < 10:
                            a_scores(ua, t - 6)
                        if 13 <= t < 17:
                            a_turn_probs(ua, t - 13)
                        if t == 17:
                            a_pv(ua, 0)
                            a_pv(ua, 1)
                    if do_f:
                        if t == 3:
                            f_turn_z(uf)
                        if t in (8, 11):
                            f_first(uf, (t - 8) // 3)
                        if t in (9, 12):
                            f_second(uf, (t - 9) // 3)
                        if t == 14:
                            f_y(uf)
                if do_a:
                    a_out(ua)
                if do_x:
                    x_out(i)

            steps(pe, step)

        @block.scalar
        def _(act):
            go = nc.scalar.activation

            def setup():
                act.wait_ge(sem["set_pe"], 3)
                src = ps_a[0][0:AD, 0:AH * NNULL].rearrange("d (pair h n) -> d h pair n", h=2, n=NNULL)
                for h2 in range(2):
                    for b in range(BU):
                        last = go(akT[h2 * AD:(h2 + 1) * AD, :, b, TQ:AK], src[:, h2], ACT.Copy)
                last.then_inc(sem["set_act"], 1)

            def x_copy_turned(u):
                act.wait_ge(sem["x_turned"], at("x_turned", u, 1))
                go(xnT[:].rearrange("p c t -> p (c t)"), ps_o[:, 0:2 * P], ACT.Copy)\
                    .then_inc(sem["x_turned_copied"], 1)

            def x_copy_k(u):
                if seen(u - 1):
                    act.wait_ge(sem["scores_done"], at("scores_done", u - 1, XTILES))
                for g in range(KD):
                    act.wait_ge(sem["k_done"], at("k_done", u, g + 1))
                    go(kT[:, g].rearrange("p b k -> p (b k)"), ps_s[g][:], ACT.Copy)\
                        .then_inc(sem["k_copied"], 1)

            def x_exp(u, t):
                act.wait_ge(sem["biased"], at("biased", u, t + 1))
                go(S[:, t % 4, :], S[:, t % 4, :], ACT.Exp, bias=x_nmx[:, t:t + 1], scale=-1.0,
                   accum_out=x_sum[:, t:t + 1]).then_inc(sem["exp_done"], 1)

            def x_copy_probs(u, t):
                act.wait_ge(sem["probs_turned"], at("probs_turned", u, t + 1))
                if t < 2:
                    if seen(u - 1):
                        act.wait_ge(sem["pv_done"], at("pv_done", u - 1, XTILES - 1 + t))
                else:
                    act.wait_ge(sem["pv_done"], at("pv_done", u, t - 1))
                go(pT[:, t % 2].rearrange("p c m -> p (c m)"), ps_t[t % 2][:, 0:2 * P], ACT.Copy)\
                    .then_inc(sem["probs_copied"], 1)

            def x_merge(u):
                act.wait_ge(sem["pv_done"], at("pv_done", u, XTILES))
                if seen(u - 1):
                    act.wait_ge(sem["merge_b"], at("merge_b", u - 1, 2))
                o = ps_o[:].rearrange("p (g b h q) -> p g b h q", g=KD, b=BU, h=2)
                go(o_half[:].rearrange("p g b q -> p (g b) q"),
                   o.rearrange("p g b h q -> p (g b) h q")[:, :, 0, :],
                   ACT.Copy, scale=parity[:, 0:1]).then_inc(sem["merge_a"], 1)

            def a_copy_turned(u):
                act.wait_ge(sem["a_turned"], at("a_turned", u, 1))
                if seen(u - 1):
                    act.wait_ge(sem["av_done"], at("av_done", u - 1, 2))
                go(aT[:, 0].rearrange("p c t -> p (c t)"), ps_a[0][:, 0:2 * P], ACT.Copy)\
                    .then_inc(sem["a_turned_copied"], 1)
                for c in range(KD):
                    last = go(aT[:, 1, c, :], ps_a[0][:, (2 + c) * P:(3 + c) * P], ACT.Identity,
                              bias=a_b[:, c:c + 1], scale=a_g[:, c:c + 1])
                last.then_inc(sem["a_turned_copied"], 1)

            def a_copy_raw(u, which):
                done, copied = ("ak_done", "ak_copied") if which else ("aq_done", "aq_copied")
                if seen(u - 1):
                    act.wait_ge(sem["ak_turned" if which else "aq_turned"], at("ak_turned" if which else "aq_turned", u - 1, 2))
                for n in range(2):
                    act.wait_ge(sem[done], at(done, u, n + 1))
                    go(a_raw[:, which, 8 * n:8 * n + 8, :].rearrange("p h d -> p (h d)"),
                       ps_a[1 - n][:], ACT.Copy).then_inc(sem[copied], 1)

            def a_copy_v(u):
                if seen(u - 1):
                    act.wait_ge(sem["apv_done"], at("apv_done", u - 1, 2))
                for n in range(2):
                    act.wait_ge(sem["av_done"], at("av_done", u, n + 1))
                    for b in range(BU):
                        go(av[0:TQ, b, n * 512:(n + 1) * 512], ps_a[1 - n][b * TQ:(b + 1) * TQ, :],
                           ACT.Copy).then_inc(sem["av_copied"], 1)

            def a_exp(u):
                act.wait_ge(sem["a_soft"], at("a_soft", u, 2))
                s = aS[:].rearrange("p h k -> p (h k)")
                go(s, s, ACT.Exp).then_inc(sem["a_exp"], 1)

            def a_copy_probs(u, n):
                act.wait_ge(sem["ap_turned"], at("ap_turned", u, n + 1))
                if n == 0:
                    if seen(u - 1):
                        act.wait_ge(sem["apv_done"], at("apv_done", u - 1, 2))
                go(apT[:, 4 * n:4 * n + 4, :].rearrange("k h t -> k (h t)"), ps_a[(n + 1) % 2][0:AK, :],
                   ACT.Copy).then_inc(sem["ap_copied"], 1)

            def f_copy_turned(u):
                act.wait_ge(sem["f_turned"], at("f_turned", u, 1))
                if seen(u - 1):
                    act.wait_ge(sem["hid_first"], at("hid_first", u - 1, 2))
                go(fT[:].rearrange("p c t -> p (c t)"), ps_f[:, 0:2 * P], ACT.Copy)\
                    .then_inc(sem["f_turned_copied"], 1)

            def f_exp(u):
                act.wait_ge(sem["route"], at("route", u, 2))
                go(g_e[:], g_s[:], ACT.Exp, bias=g_1[:, 0:1], accum_out=g_1[:, 1:2])\
                    .then_inc(sem["f_exp"], 1)

            def f_copy_z(u):
                act.wait_ge(sem["z_turned"], at("z_turned", u, 1))
                if seen(u - 1):
                    act.wait_ge(sem["hid_second"], at("hid_second", u - 1, 2))
                go(zT[:].rearrange("p n t -> p (n t)"), ps_f[:, 0:2 * P], ACT.Copy)\
                    .then_inc(sem["z_turned_copied"], 1)

            def f_relu(u, n):
                act.wait_ge(sem["hid_first"], at("hid_first", u, n + 1))
                if seen(u - 1):
                    act.wait_ge(sem["hid_ready"], at("hid_ready", u - 1, n + 1))
                for j in range(4):
                    c = 4 * n + j
                    last = go(f_r[:, c, :], ps_f[:, j * P:(j + 1) * P], ACT.Relu, bias=f_bi[:, c:c + 1])
                last.then_inc(sem["relu_done"], 1)

            setup()

            def step(i, do_x, do_a, do_f):
                ua, uf = i - 1, i - 2
                if do_x:
                    x_copy_k(i)
                    x_copy_turned(i)
                if do_a:
                    a_copy_turned(ua)
                if do_f:
                    f_copy_turned(uf)
                if do_a:
                    a_copy_raw(ua, 0)
                for t in range(XTILES + 3):
                    if do_x:
                        if t < XTILES:
                            x_exp(i, t)
                        if 2 <= t < XTILES + 2:
                            x_copy_probs(i, t - 2)
                    if do_a:
                        if t == 0:
                            a_copy_raw(ua, 1)
                        if t == 1:
                            a_copy_v(ua)
                        if t == 4:
                            a_spread(u=ua)
                        if t == 12:
                            a_exp(ua)
                        if 13 <= t < 17:
                            a_copy_probs(ua, t - 13)
                    if do_f:
                        if t == 0:
                            f_exp(uf)
                        if t == 3:
                            f_copy_z(uf)
                        if t in (8, 11):
                            f_relu(uf, (t - 8) // 3)
                if do_x:
                    x_merge(i)

            def a_spread(u):
                if seen(u - 1):
                    act.wait_ge(sem["as_done"], at("as_done", u - 1, 4))
                for n in range(2):
                    act.wait_ge(sem["aq_turned"], at("aq_turned", u, n + 1))
                    for h2 in range(2):
                        rows = slice(h2 * AD, (h2 + 1) * AD)
                        last = go(qz[rows, 8 * n + h2:8 * n + 8:2, :], tiles4(ps_a[1 - n][rows, :]),
                                  ACT.Copy, scale=a_qk[rows, 0:1])
                    last.then_inc(sem["aq_spread"], 1)

            act.wait_ge(sem["consts"], ALL_CONST)
            act.wait_ge(sem["set_dve"], 4)
            act.wait_ge(sem["set_pool"], 2)
            steps(act, step)

        @block.vector
        def _(dve):
            tt, ts, stt = nc.vector.tensor_tensor, nc.vector.tensor_scalar, nc.vector.scalar_tensor_tensor

            def setup():
                dve.wait_ge(sem["consts"], ALL_CONST)
                dve.wait_ge(sem["set_pe"], 1)
                nc.vector.tensor_copy(reltab[:], ps_s[0][0:XH, 0:DIAGS]).then_inc(sem["set_dve"], 1)
                dve.wait_ge(sem["set_pe"], 2)
                ts(f_nbi[:], f_bi[:], -1.0, None, ALU.mult)
                stt(f_bo2[:], f_bo2[:], 2.0, ps_f[:, 0:D], ALU.mult, ALU.add).then_inc(sem["set_dve"], 1)
                tt(a_qk[:], a_qs[:], a_ks[:], ALU.mult).then_inc(sem["set_dve"], 1)
                dve.wait_ge(sem["set_dve"], 3)
                ts(a_qk[:], a_qk[:], 8.0, None, ALU.mult).then_inc(sem["set_dve"], 1)
                dve.wait_ge(sem["set_pool"], 1)
                nc.vector.tensor_reduce(null_len[:, 0:1], null_sq[:], AX, ALU.add)\
                    .then_inc(sem["set_dve"], 1)

            def norm(u, src, dst, st, mv, rs, stats, rstd, k):
                nc.vector.bn_stats(st, src).then_inc(sem[stats], 1)
                dve.wait_ge(sem[stats], lone(dve, stats, u, 2 * k + 1))
                nc.vector.bn_aggr(mv, st).then_inc(sem[stats], 1)
                dve.wait_ge(sem[rstd], at(rstd, u, 2 * k + 2))
                return ts(dst, src, mv[:, 0:1], rs[:, 1:2], ALU.subtract, ALU.mult)

            def x_norm(u):
                dve.wait_ge(sem["x_loaded"], at("x_loaded", u, 16))
                if seen(u - 1):
                    dve.wait_ge(sem["x_turned"], at("x_turned", u - 1, 1))
                norm(u, x_ld[:], x_n[:], x_st[:], x_mv[:], x_rs, "x_stats", "x_rstd", 0)\
                    .then_inc(sem["x_normed"], 1)

            def x_copy_v(u):
                if seen(u - 1):
                    dve.wait_ge(sem["pv_done"], at("pv_done", u - 1, XTILES))
                for n in range(2):
                    dve.wait_ge(sem["v_done"], at("v_done", u, n + 1))
                    nc.vector.tensor_copy(v[:, 2 * n:2 * n + 2, :].rearrange("p t d -> p (t d)"), ps_t[n][:])\
                        .then_inc(sem["v_copied"], 1)

            def x_spread_q(u):
                dve.wait_ge(sem["q_done"], at("q_done", u, 1))
                if seen(u - 1):
                    dve.wait_ge(sem["scores_done"], at("scores_done", u - 1, XTILES))
                for g in range(KD):
                    for b in range(BU):
                        q = ps_o[:, 256 + g * P + b * TQ:256 + g * P + (b + 1) * TQ]
                        last = tt(qbd[:, g, b], q.unsqueeze(1).broadcast_to([P, 8, TQ]),
                                  headmask[:].unsqueeze(2).broadcast_to([P, 8, TQ]), ALU.mult)
                last.then_inc(sem["q_spread"], 1)

            def x_bias(u, t):
                b, pair = t // XPAIRS, t % XPAIRS
                dve.wait_ge(sem["scores_done"], lone(dve, "scores_done", u, t + 1))
                if pair == 0:
                    dve.wait_ge(sem["bias_masked"], lone(dve, "bias_masked", u, b + 1))
                if t < 4:
                    if seen(u - 1):
                        dve.wait_ge(sem["probs_turned"], lone(dve, "probs_turned", u - 1, XTILES - 3 + t))
                else:
                    dve.wait_ge(sem["probs_turned"], lone(dve, "probs_turned", u, t - 3))
                nc.vector.tensor_tensor_reduce(
                    out=S[:, t % 4, :], in0=ps_s[t % 2][:, 0:TK], in1=bm[:, b, pair, :], scale=-1.0,
                    scalar=BIG, op0=ALU.add, op1=ALU.min, accum_out=x_nmx[:, t:t + 1])\
                    .then_inc(sem["biased"], 1)

            def x_scale(u, t):
                dve.wait_ge(sem["exp_done"], at("exp_done", u, t + 1))
                nc.vector.reciprocal(x_inv[:, t:t + 1], x_sum[:, t:t + 1]).then_inc(sem["recip_done"], 1)
                dve.wait_ge(sem["recip_done"], at("recip_done", u, t + 1))
                ts(S[:, t % 4, :], S[:, t % 4, :], x_inv[:, t:t + 1], None, ALU.mult)\
                    .then_inc(sem["probs_ready"], 1)

            def x_merge(u):
                dve.wait_ge(sem["merge_a"], at("merge_a", u, 1))
                if seen(u - 1):
                    dve.wait_ge(sem["xo_done"], at("xo_done", u - 1, 1))
                o = ps_o[:].rearrange("p (g b h q) -> p g b h q", g=KD, b=BU, h=2)
                for g in range(KD):
                    stt(oT[:, g], o[:, g, :, 1, :], parity[:, 1:2], o_half[:, g], ALU.mult, ALU.add)\
                        .then_inc(sem["merge_b"], 1)

            def x_residual(u):
                dve.wait_ge(sem["xo_done"], at("xo_done", u, 1))
                dve.wait_ge(sem["x_kept"], at("x_kept", u, 1))
                if seen(u - 1):
                    dve.wait_ge(sem["a_kept"], at("a_kept", u - 1, 1))
                if seen(u - 1):
                    dve.wait_ge(sem["a_normed"], at("a_normed", u - 1, 1))
                tt(x1[:], ps_o[:, 0:D], x_res[:], ALU.add).then_inc(sem["x1_ready"], 1)

            def a_norm(u, k):
                src, dst = ((x1, a_x), (a_x, a_n))[k]
                if k == 0:
                    dve.wait_ge(sem["x1_ready"], at("x1_ready", u, 1))
                else:
                    dve.wait_ge(sem["a_normed"], at("a_normed", u, 1))
                if seen(u - 1):
                    dve.wait_ge(sem["a_turned"], at("a_turned", u - 1, 1))
                norm(u, src[:], dst[:], a_st[:, k], a_mv[:, k], a_rs[:, k], "a_stats", "a_rstd", k)\
                    .then_inc(sem["a_normed"], 1)

            def a_lengths(u, which):
                dve.wait_ge(sem["a_squared"], at("a_squared", u, which + 1))
                nc.vector.tensor_reduce(a_len[:, which, :], a_sq[:], AX, ALU.add)\
                    .then_inc(sem["a_sumsq"], 1)

            def a_place_keys(u):
                if seen(u - 1):
                    dve.wait_ge(sem["as_done"], at("as_done", u - 1, 4))
                for n in range(2):
                    dve.wait_ge(sem["ak_turned"], at("ak_turned", u, n + 1))
                    nc.vector.tensor_copy(
                        akT[:, 4 * n:4 * n + 4, :, 0:TQ],
                        ps_a[1 - n][:].rearrange("p (j b t) -> p j b t", j=4, b=BU)).then_inc(sem["ak_placed"], 1)

            def a_bias(u, n):
                dve.wait_ge(sem["as_done"], at("as_done", u, n + 1))
                if n == 0:
                    if seen(u - 1):
                        dve.wait_ge(sem["ap_turned"], at("ap_turned", u - 1, 4))
                tt(aS[:, 4 * n:4 * n + 4, :], ps_a[(n + 1) % 2][:, 0:4 * AK].rearrange("p (h k) -> p h k", h=4),
                   alibi[:, 4 * n:4 * n + 4, :], ALU.add).then_inc(sem["as_biased"], 1)

            def a_softmax_top(u):
                dve.wait_ge(sem["as_biased"], at("as_biased", u, 4))
                nc.vector.tensor_reduce(a_mx[:], aS[:], AX, ALU.max).then_inc(sem["a_soft"], 1)
                dve.wait_ge(sem["a_soft"], at("a_soft", u, 1))
                tt(aS[:], aS[:], a_mx[:].unsqueeze(2).broadcast_to([P, AH, AK]), ALU.subtract)\
                    .then_inc(sem["a_soft"], 1)

            def a_softmax_end(u):
                dve.wait_ge(sem["a_exp"], at("a_exp", u, 1))
                nc.vector.tensor_reduce(a_sum[:], aS[:], AX, ALU.add).then_inc(sem["a_soft"], 1)
                dve.wait_ge(sem["a_soft"], at("a_soft", u, 3))
                nc.vector.reciprocal(a_sum[:], a_sum[:]).then_inc(sem["a_soft"], 1)
                dve.wait_ge(sem["a_soft"], at("a_soft", u, 4))
                tt(aS[:], aS[:], a_sum[:].unsqueeze(2).broadcast_to([P, AH, AK]), ALU.mult)\
                    .then_inc(sem["a_soft"], 1)

            def a_copy_pv(u, n):
                dve.wait_ge(sem["apv_done"], at("apv_done", u, n + 1))
                if n == 0:
                    if seen(u - 1):
                        dve.wait_ge(sem["ao_done"], at("ao_done", u - 1, 1))
                nc.vector.tensor_copy(aoT[:, 4 * n:4 * n + 4, :].rearrange("p c t -> p (c t)"), ps_a[1 - n][:])\
                    .then_inc(sem["apv_copied"], 1)

            def a_residual(u):
                dve.wait_ge(sem["ao_done"], at("ao_done", u, 1))
                dve.wait_ge(sem["a_kept"], at("a_kept", u, 1))
                if seen(u - 1):
                    dve.wait_ge(sem["f_kept"], at("f_kept", u - 1, 1))
                if seen(u - 1):
                    dve.wait_ge(sem["f_normed"], at("f_normed", u - 1, 1))
                tt(x2[:], ps_a[1][:, 0:D], a_res[:], ALU.add).then_inc(sem["x2_ready"], 1)

            def f_norm(u):
                dve.wait_ge(sem["x2_ready"], at("x2_ready", u, 1))
                if seen(u - 1):
                    dve.wait_ge(sem["f_turned"], at("f_turned", u - 1, 1))
                norm(u, x2[:], f_n[:], f_st[:], f_mv[:], f_rs, "f_stats", "f_rstd", 0)\
                    .then_inc(sem["f_normed"], 1)

            def f_logits(u):
                dve.wait_ge(sem["z_done"], at("z_done", u, 1))
                if seen(u - 1):
                    dve.wait_ge(sem["z_routed"], at("z_routed", u - 1, 3))
                nc.vector.tensor_copy(z[:, 0:P], ps_f[:, 0:P]).then_inc(sem["z_copied"], 1)
                tt(g_s[:], ps_f[:, P:P + E], f_gb[:], ALU.add).then_inc(sem["route"], 1)
                dve.wait_ge(sem["route"], at("route", u, 1))
                nc.vector.tensor_reduce(g_1[:, 0:1], g_s[:], AX, ALU.max, negate=True)\
                    .then_inc(sem["route"], 1)

            def f_route(u):
                dve.wait_ge(sem["f_exp"], at("f_exp", u, 1))
                nc.vector.reciprocal(g_1[:, 2:3], g_1[:, 1:2]).then_inc(sem["route"], 1)
                dve.wait_ge(sem["route"], at("route", u, 3))
                ts(g_s[:], g_e[:], g_1[:, 2:3], None, ALU.mult).then_inc(sem["route"], 1)
                dve.wait_ge(sem["route"], at("route", u, 4))
                mine = g_s[:].unsqueeze(2).broadcast_to([P, E, E])
                other = g_s[:].unsqueeze(1).broadcast_to([P, E, E])
                tt(g_gt[:], other, mine, ALU.is_gt)
                tt(g_eq[:], other, mine, ALU.is_equal).then_inc(sem["route"], 1)
                dve.wait_ge(sem["route"], at("route", u, 5))
                tt(g_eq[:], g_eq[:], lower[:], ALU.mult).then_inc(sem["route"], 1)
                dve.wait_ge(sem["route"], at("route", u, 6))
                tt(g_gt[:], g_gt[:], g_eq[:], ALU.add).then_inc(sem["route"], 1)
                dve.wait_ge(sem["route"], at("route", u, 7))
                nc.vector.tensor_reduce(g_rank[:], g_gt[:], AX, ALU.add).then_inc(sem["route"], 1)
                dve.wait_ge(sem["route"], at("route", u, 8))
                ts(g_sel[:, 0, :], g_rank[:], 0.0, None, ALU.is_equal)
                ts(g_sel[:, 1, :], g_rank[:], 1.0, None, ALU.is_equal)
                if seen(u - 1):
                    dve.wait_ge(sem["out_ready"], at("out_ready", u - 1, 1))
                stt(g_top[:], g_rank[:], 2.0, g_s[:], ALU.is_lt, ALU.mult, accum_out=g_1[:, 3:4])\
                    .then_inc(sem["route"], 1)
                dve.wait_ge(sem["route"], at("route", u, 9))
                zs = z[:, 0:P].rearrange("p (e r) -> p e r", e=E)
                if seen(u - 1):
                    dve.wait_ge(sem["z_turned"], at("z_turned", u - 1, 1))
                for n in range(2):
                    tt(zr[:, n], zs, g_sel[:, n, :].unsqueeze(2).broadcast_to([P, E, R]), ALU.mult)\
                        .then_inc(sem["z_routed"], 1)
                dve.wait_ge(sem["z_routed"], at("z_routed", u, 2))
                tt(zr[:, 2], zr[:, 1], zr[:, 0], ALU.subtract).then_inc(sem["z_routed"], 1)

            def f_second(u, n):
                dve.wait_ge(sem["hid_second"], at("hid_second", u, n + 1))
                if seen(u - 1):
                    dve.wait_ge(sem["y_done"], at("y_done", u - 1, 1))
                for j in range(4):
                    c = 4 * n + j
                    last = stt(f_h[:, c, :], ps_f[:, j * P:(j + 1) * P], f_nbi[:, c:c + 1], f_r[:, c, :],
                               ALU.max, ALU.add)
                last.then_inc(sem["hid_ready"], 1)

            def f_final(u):
                dve.wait_ge(sem["y_done"], at("y_done", u, 1))
                tt(f_t[:], ps_f[:, 0:D], f_bo2[:], ALU.add).then_inc(sem["y_sum"], 1)
                dve.wait_ge(sem["y_sum"], at("y_sum", u, 1))
                if seen(u - 1):
                    dve.wait_ge(sem["out_stored"], at("out_stored", u - 1, 16))
                dve.wait_ge(sem["f_kept"], at("f_kept", u, 1))
                stt(f_out[:], f_t[:], g_1[:, 3:4], f_res[:], ALU.mult, ALU.add)\
                    .then_inc(sem["out_ready"], 1)

            setup()

            def step(i, do_x, do_a, do_f):
                ua, uf = i - 1, i - 2
                if do_x:
                    x_norm(i)
                if do_a:
                    a_norm(ua, 0)
                if do_f:
                    f_norm(uf)
                if do_a:
                    a_norm(ua, 1)
                if do_x:
                    x_copy_v(i)
                    x_spread_q(i)
                if do_f:
                    f_logits(uf)
                for t in range(XTILES + 3):
                    if do_x:
                        if t < XTILES:
                            x_bias(i, t)
                        if 1 <= t < XTILES + 1:
                            x_scale(i, t - 1)
                    if do_a:
                        if t == 2:
                            a_lengths(ua, 0)
                        if t == 3:
                            a_lengths(ua, 1)
                        if t == 5:
                            a_place_keys(ua)
                        if 6 <= t < 10:
                            a_bias(ua, t - 6)
                        if t == 10:
                            a_softmax_top(ua)
                        if t == 12:
                            a_softmax_end(ua)
                        if t == 17:
                            a_copy_pv(ua, 0)
                            a_copy_pv(ua, 1)
                    if do_f:
                        if t == 1:
                            f_route(uf)
                        if t in (9, 12):
                            f_second(uf, (t - 9) // 3)
                        if t == 15:
                            f_final(uf)
                if do_x:
                    x_merge(i)
                if do_a:
                    a_residual(ua)
                if do_x:
                    x_residual(i)

            steps(dve, step)

        @block.gpsimd
        def _(pool):
            tt, ts = nc.gpsimd.tensor_tensor, nc.gpsimd.tensor_scalar

            def setup():
                pool.memset(half[:], -0.5).then_inc(sem["half"], 1)
                pool.wait_ge(sem["half"], 1)
                pool.wait_ge(sem["consts"], ALL_CONST)
                tt(null_sq[:], nulls[:], nulls[:], ALU.mult).then_inc(sem["set_pool"], 1)
                pool.memset(qz[:], 0.0).then_inc(sem["set_pool"], 1)
                pool.wait_ge(sem["set_dve"], 5)
                ts(null_len[:, 1:2], null_len[:, 0:1], 1e-24, None, ALU.max).then_inc(sem["half"], 1)
                pool.wait_ge(sem["half"], 2)
                tt(null_len[:, 1:2], null_len[:, 1:2], half[0:32, 0:1], ALU.pow).then_inc(sem["half"], 1)
                pool.wait_ge(sem["half"], 3)
                ts(nulls[:], nulls[:], null_len[:, 1:2], None, ALU.mult).then_inc(sem["set_pool"], 1)
                pool.wait_ge(sem["table_loaded"], 32)

            def rstd(u, mv, rs, stats, done, k):
                pool.wait_ge(sem[stats], lone(pool, stats, u, 2 * k + 2))
                ts(rs[:, 0:1], mv[:, 1:2], EPS, None, ALU.add).then_inc(sem[done], 1)
                pool.wait_ge(sem[done], lone(pool, done, u, 2 * k + 1))
                tt(rs[:, 1:2], rs[:, 0:1], half[:, 0:1], ALU.pow).then_inc(sem[done], 1)

            def x_rstd(u):
                if seen(u - 1):
                    pool.wait_ge(sem["x_normed"], lone(pool, "x_normed", u - 1, 1))
                rstd(u, x_mv, x_rs, "x_stats", "x_rstd", 0)

            def x_keep(u):
                pool.wait_ge(sem["x_loaded"], lone(pool, "x_loaded", u, 16))
                if seen(u - 1):
                    pool.wait_ge(sem["x1_ready"], lone(pool, "x1_ready", u - 1, 1))
                pool.tensor_copy(x_res[:], x_ld[:]).then_inc(sem["x_kept"], 1)

            def x_mask(u):
                pool.wait_ge(sem["mask_loaded"], lone(pool, "mask_loaded", u, 16))
                if seen(u - 1):
                    pool.wait_ge(sem["bias_masked"], lone(pool, "bias_masked", u - 1, 2))
                ts(negm[:].rearrange("p b k -> p (b k)"), mask32[:].bitcast(U8), MASKED, -MASKED, ALU.mult, ALU.add).then_inc(sem["mask_scaled"], 1)

            def x_bias(u, b):
                pool.wait_ge(sem["mask_scaled"], lone(pool, "mask_scaled", u, 1))
                if seen(u - 1):
                    pool.wait_ge(sem["biased"], lone(pool, "biased", u - 1, XPAIRS * (b + 1)))
                tt(bm[:, b], bias[:], negm[:, b, :].unsqueeze(1).broadcast_to([P, XPAIRS, TK]), ALU.add)\
                    .then_inc(sem["bias_masked"], 1)

            def a_rstd(u, k):
                if seen(u - 1):
                    pool.wait_ge(sem["a_normed"], lone(pool, "a_normed", u - 1, k + 1))
                rstd(u, a_mv[:, k], a_rs[:, k], "a_stats", "a_rstd", k)

            def a_keep(u):
                pool.wait_ge(sem["x1_ready"], lone(pool, "x1_ready", u, 1))
                if seen(u - 1):
                    pool.wait_ge(sem["x2_ready"], lone(pool, "x2_ready", u - 1, 1))
                pool.tensor_copy(a_res[:], x1[:]).then_inc(sem["a_kept"], 1)

            def a_square(u, which):
                pool.wait_ge(sem["ak_copied" if which else "aq_copied"], lone(pool, "ak_copied" if which else "aq_copied", u, 2))
                if which:
                    pool.wait_ge(sem["a_sumsq"], lone(pool, "a_sumsq", u, 1))
                else:
                    if seen(u - 1):
                        pool.wait_ge(sem["a_sumsq"], lone(pool, "a_sumsq", u - 1, 2))
                tt(a_sq[:], a_raw[:, which], a_raw[:, which], ALU.mult).then_inc(sem["a_squared"], 1)

            def a_unit(u, which):
                pool.wait_ge(sem["a_sumsq"], lone(pool, "a_sumsq", u, which + 1))
                ln = a_len[:, which, :]
                ts(ln, ln, 1e-24, None, ALU.max).then_inc(sem["a_len"], 1)
                pool.wait_ge(sem["a_len"], lone(pool, "a_len", u, 2 * which + 1))
                tt(ln, ln, half[:, 0:AH], ALU.pow).then_inc(sem["a_len"], 1)
                pool.wait_ge(sem["a_len"], lone(pool, "a_len", u, 2 * which + 2))
                tt(a_raw[:, which], a_raw[:, which], ln.unsqueeze(2).broadcast_to([P, AH, AD]), ALU.mult)\
                    .then_inc(sem["a_unit"], 1)

            def f_keep(u):
                pool.wait_ge(sem["x2_ready"], lone(pool, "x2_ready", u, 1))
                if seen(u - 1):
                    pool.wait_ge(sem["out_ready"], lone(pool, "out_ready", u - 1, 1))
                pool.tensor_copy(f_res[:], x2[:]).then_inc(sem["f_kept"], 1)

            def f_rstd(u):
                if seen(u - 1):
                    pool.wait_ge(sem["f_normed"], lone(pool, "f_normed", u - 1, 1))
                rstd(u, f_mv, f_rs, "f_stats", "f_rstd", 0)

            setup()

            def step(i, do_x, do_a, do_f):
                ua, uf = i - 1, i - 2
                if do_x:
                    x_rstd(i)
                if do_a:
                    a_rstd(ua, 0)
                if do_f:
                    f_rstd(uf)
                if do_a:
                    a_rstd(ua, 1)
                if do_x:
                    x_mask(i)
                    x_bias(i, 0)
                    x_keep(i)
                if do_a:
                    a_keep(ua)
                if do_f:
                    f_keep(uf)
                if do_a:
                    a_square(ua, 0)
                    a_square(ua, 1)
                    a_unit(ua, 0)
                    a_unit(ua, 1)
                if do_x:
                    x_bias(i, 1)

            steps(pool, step)


def kernel(**inputs):
    import concourse.bacc as bacc
    from concourse.bass_utils import run_bass_kernel_spmd

    a = {k: np.asarray(val) for k, val in inputs.items()}

    def t(name):
        return a[name].T

    null = a["L0_attn_null_kv"].reshape(AH, NNULL, 2, AD)
    arrays = dict(
        x=a["x"].reshape(B * TQ, D),
        ctxT=a["ctx_1024"].reshape(UNITS, BU, TK, KD, P).transpose(0, 4, 3, 1, 2).reshape(UNITS * P, KD * BU * TK),
        mask=a["mask_Bx1x1xS2_bk0"].reshape(UNITS, BU * TK).view(np.int32),
        wqT=t("L0_xattn_Wq"), wkT=t("L0_xattn_Wk"), wvT=t("L0_xattn_Wv"), woT=t("L0_xattn_Wo"),
        relT=t("L0_xattn_rel_bias"),
        a_g=a["L0_attn_norm_g"].reshape(KD, P).T, a_b=a["L0_attn_norm_b"].reshape(KD, P).T,
        a_wq=a["L0_attn_Wq"], a_wkv=a["L0_attn_Wkv"], a_wo=a["L0_attn_Wout"],
        a_qs=a["L0_attn_q_scale"].reshape(AD, 1), a_ks=a["L0_attn_k_scale"].reshape(AD, 1),
        null_k=null[:, :, 0, :].reshape(AH * NNULL, AD),
        null_v=null[:, :, 1, :].transpose(1, 0, 2).reshape(NNULL, INNER),
        f_wiT=t("L0_ffn_wi"), f_woT=t("L0_ffn_wo"),
        f_bi=a["L0_ffn_bi"].reshape(FC, P).T, f_bo=a["L0_ffn_bo"], f_gb=a["L0_ffn_gate_b"],
        f_loraA=a["L0_ffn_lora_A"].reshape(E * R, D).T,
        f_loraB=a["L0_ffn_lora_B"].transpose(0, 2, 1).reshape(E * R, FF),
        f_gateT=t("L0_ffn_gate_w"),
        **constants(),
    )
    arrays = {k: np.ascontiguousarray(val) for k, val in arrays.items()}
    nc = bacc.Bacc("TRN2", target_bir_lowering=False, num_devices=1)
    io = {k: nc.dram_tensor("in_" + k, val.shape, mybir.dt.from_np(val.dtype), kind="ExternalInput").ap()
          for k, val in arrays.items()}
    out = nc.dram_tensor("out", [B * TQ, D], F32, kind="ExternalOutput").ap()
    build(nc, io, out)
    result = run_bass_kernel_spmd(nc, [{"in_" + k: val for k, val in arrays.items()}], core_ids=[0])
    return result.results[0]["out"].reshape(B, TQ, D)
```

```python
from contextlib import ExitStack

import numpy as np

import concourse.bass as bass
from concourse import mybir

F32, F16 = mybir.dt.float32, mybir.dt.float16
I32, U8 = mybir.dt.int32, mybir.dt.uint8
ALU = mybir.AluOpType
ACT = mybir.ActivationFunctionType
AX = mybir.AxisListType.X

P = 128
B, TQ, TK, D = 64, 64, 256, 256
BU = P // TQ
UNITS = B // BU
KD = D // P
XH, XD = 16, D // 16
XPAIRS = XH // 2
XTILES = BU * XPAIRS
NBUCKET, DIAGS = 32, TQ + TK
AH, AD, NNULL = 16, 64, 2
INNER = AH * AD
AK = TQ + NNULL
APAIRS = AH // 2
FF, E, R = 1024, 8, 16
FC = FF // P
EPS = 1e-5
MASKED = float(2.0 ** 100)
BIG = 3.0e38
UP, DOWN = 2.0 ** 8, 2.0 ** -8
TURN_LAG = 4
PV_LAG = 2
S_BUFS, PT_BUFS = TURN_LAG + 1, PV_LAG + 1

SLOTS = range(-14, 2 * (XTILES + TURN_LAG + PV_LAG))
SLOT = dict(
    pe_x_k=(-13, -11), pe_x_out=(-13,), pe_x_v=(-9, -8), pe_x_turn=(-10,), pe_a_out=(-12,), pe_x_q=(-8,),
    pe_f_turn=(-7,), pe_f_z=(-2,), pe_a_turn=(-9,), pe_a_q=(-6, -5), pe_a_k=(-2, 1), pe_a_v=(1, 7),
    pe_a_turn_q=(8, 8), pe_a_turn_k=(12, 12), pe_a_scores=(13, 15, 18, 19), pe_a_turn_probs=(30, 30, 31, 31),
    pe_a_pv=(40, 40), pe_f_turn_z=(3,), pe_f_first=(18, 24), pe_f_second=(22, 25), pe_f_y=(30,),
    act_x_copy_k=(-14, -1), act_x_copy_turned=(-12,), act_x_copy_v=(0, 2), act_f_copy_turned=(-11,),
    act_a_copy_turned=(-12,), act_a_copy_q=(-10, -8), act_a_copy_k=(-1, 0), act_a_copy_v=(2, 3),
    act_a_spread=(6, 7), act_a_exp=(19, 23), act_a_copy_probs=(28, 28, 30, 36), act_a_copy_pv=(41, 43),
    act_f_exp=(-1,), act_f_copy_z=(1,), act_f_relu=(18, 22), act_f_split_hid=(21, 26), act_x_split_ctx=(0,),
    dve_x_residual=(-12,), dve_x_split_turned=(-8,), dve_a_residual=(-9,), dve_x_spread_q=(-6,),
    dve_f_stats=(-7,), dve_a_stats=(-12, -9), dve_f_norm=(-7,), dve_a_norm=(-11, -9),
    dve_f_split_turned=(-5,), dve_a_split_turned=(-7,), dve_a_lengths=(-1, 3), dve_a_unit=(5, 9),
    dve_a_place_keys=(12, 12), dve_a_bias=(14, 17, 17, 19), dve_a_softmax_top=(17, 23),
    dve_a_softmax_end=(23, 27), dve_a_split_pv=(38, 41), dve_f_logits=(-1,), dve_f_route=(2,),
    dve_f_split_z=(6,), dve_f_second=(22, 25), dve_f_split_hid=(25, 25), dve_f_final=(36,), dve_x_stats=(-5,),
    dve_x_norm=(32,), dve_x_split_ctx=(37,),
    pool_f_rstd=(2,), pool_a_rstd=(1, 1), pool_a_length=(15, 19), pool_x_keep=(4,), pool_a_keep=(27,),
    pool_f_keep=(14,), pool_x_bias_second=(6, 33), pool_x_bias_first=(35, 35), pool_x_rstd=(31,),
    pool_x_mask=(35,),
)

PER_UNIT = dict(
    x_loaded=16, ctx_loaded=16, mask_loaded=16, out_stored=16,
    x_stats=2, x_rstd=2, x_normed=1, x_kept=1, x_turned=1, x_turned_copied=2, ctx_split=2, q_done=1,
    q_spread=1, k_done=2, k_copied=2, v_done=2, v_copied=2, mask_scaled=1, bias_masked=4,
    scores_done=XTILES, biased=XTILES, exp_done=XTILES, recip_done=XTILES, probs_ready=XTILES,
    probs_turned=XTILES, probs_copied=XTILES, pv_done=XTILES, merge_a=1, merge_b=2, merged=2, xo_done=1,
    x1_ready=1,
    a_kept=1, a_stats=4, a_rstd=4, a_normed=2, a_turned=1, a_turned_copied=1, a_turned_split=4, aq_done=2, ak_done=2,
    av_done=2, aq_copied=2, ak_copied=2, av_copied=4, a_squared=4, a_sumsq=2, a_len=4, a_unit=2,
    aq_turned=2, aq_spread=2, ak_turned=2, ak_placed=2, as_done=4, as_biased=4, a_soft=10,
    a_exp=2, ap_turned=4, ap_copied=4, apv_done=2, apv_hi=2, apv_copied=2, ao_done=1, x2_ready=1,
    f_kept=1, f_stats=2, f_rstd=2, f_normed=1, f_turned=1, f_turned_copied=2, z_done=1,
    z_copied=1, f_exp=1, route=9, z_routed=3, z_turned=1, z_turned_copied=2,
    hid_first=2, relu_done=2, hid_second=2, hid_ready=2, hid_hi=2, hid_split=2, y_done=1, y_sum=1, out_ready=1,
)
ONCE = ("consts", "table_stored", "table_loaded", "set_pe", "set_act", "set_dve", "set_pool",
        "half", "staged0", "staged1", "split_hi", "split_lo")


def constants():
    r = np.arange(DIAGS) - (TQ - 1)
    far = 8 + sum((np.abs(r) >= t).astype(np.int64) for t in (12, 16, 23, 32, 46, 64, 91))
    bucket = (r > 0) * 16 + np.where(np.abs(r) < 8, np.abs(r), far)
    onehot = (bucket[None, :] == np.arange(NBUCKET)[:, None]).astype(np.float32)
    start = 2.0 ** (-2.0 ** (-(np.log2(AH) - 3)))
    slopes = np.array([start * start ** i for i in range(AH)], dtype=np.float32)
    q = np.arange(TQ)[:, None]
    col = np.concatenate([NNULL + np.arange(TQ), np.arange(NNULL)])[None, :]
    dist = -np.abs(col - (q + NNULL)).astype(np.float32)
    alibi = slopes[None, :, None] * dist[:, None, :]
    alibi = np.where((col > q + NNULL)[:, None, :], np.float32(-MASKED), alibi)
    alibi = np.tile(alibi, (BU, 1, 1)).astype(np.float32)
    row = np.arange(P)
    headmask = (row[:, None] // XD == np.arange(8)[None, :]).astype(np.float32) * np.float32(DOWN)
    parity = (row[:, None] // XD % 2 == np.arange(2)[None, :]).astype(np.float32)
    lower = np.tile((np.arange(E)[None, :] < np.arange(E)[:, None]).astype(np.float32)[None],
                    (P, 1, 1))
    return dict(c_ident=np.eye(P, dtype=np.float32), c_onehot=onehot, c_alibi=alibi,
                c_headmask=headmask, c_parity=parity, c_lower=lower)


def build(nc, io, out):
    with ExitStack() as ctx:
        def sb(name, shape, dt=F32):
            return ctx.enter_context(nc.sbuf_tensor(name, shape, dt))

        def bank(name):
            return ctx.enter_context(nc.psum_tensor(name, [P, 512], F32))

        sem = {n: ctx.enter_context(nc.semaphore(n)) for n in (*PER_UNIT, *ONCE)}

        def at(name, u, k):
            return u * PER_UNIT[name] + k

        def seen(u):
            return not isinstance(u, int) or u >= 0

        def lone(eng, name, u, k):
            value = at(name, u, k)
            if not isinstance(value, int):
                value = eng.to_reg(value)
                eng.wait_ge(sem["consts"], 16)
            return value

        def split(name, shape):
            return sb(name, [shape[0], 2, *shape[1:]], F16)

        wq, wk, wv, wo = (split(n, [P, KD, D]) for n in ("wq", "wk", "wv", "wo"))
        a_wq, a_wk, a_wv = (split(n, [P, KD, INNER]) for n in ("a_wq", "a_wk", "a_wv"))
        a_wo = split("a_wo", [P, APAIRS, D])
        f_wi, f_wo = split("f_wi", [P, KD, FF]), split("f_wo", [P, FC, D])
        f_loraB, f_zw = split("f_loraB", [P, FF]), split("f_zw", [P, KD, P + E])
        f_bis = split("f_bis", [P, FC])
        f_bi, f_bo2, f_gb = sb("f_bi", [P, FC]), sb("f_bo2", [P, D]), sb("f_gb", [P, E])
        f_bup = sb("f_bup", [P, 2, FC])
        ident, alibi = sb("ident", [P, P]), sb("alibi", [P, AH, AK])
        headmask, parity = sb("headmask", [P, 8]), sb("parity", [P, 2])
        lower = sb("lower", [P, E, E])
        a_g, a_b, a_qs, a_ks = sb("a_g", [P, KD]), sb("a_b", [P, KD]), sb("a_qs", [P, 1]), sb("a_ks", [P, 1])
        relT, onehot = sb("relT", [NBUCKET, XH]), sb("onehot", [NBUCKET, DIAGS])
        reltab = sb("reltab", [XH, DIAGS])
        bias = sb("bias", [P, XPAIRS, TK])
        nulls = sb("nulls", [AH * NNULL, AD])
        null_sq = sb("null_sq", [AH * NNULL, AD])
        null_len, half = sb("null_len", [AH * NNULL, 2]), sb("half", [P, 2 * AH])
        x_ld, x_res, x_n = sb("x_ld", [P, D]), sb("x_res", [P, D]), sb("x_n", [P, D])
        ctxT, mask32, negm = sb("ctxT", [P, KD, BU, TK]), sb("mask32", [P, BU * TK // 4], I32), sb("negm", [P, BU, TK])
        x_st, x_mv, x_rs = sb("x_st", [P, 6]), sb("x_mv", [P, 2]), sb("x_rs", [P, 2])
        ctxS, xnT = split("ctxS", [P, KD, BU * TK]), split("xnT", [P, KD, P])
        qbd = sb("qbd", [P, KD, BU, 8, TQ])
        kT, v = sb("kT", [P, KD, BU, TK]), sb("v", [P, BU * 2, D])
        bm = sb("bm", [P, BU, XPAIRS, TK])
        S = sb("S", [P, S_BUFS, TK])
        x_nmx, x_sum, x_inv = sb("x_nmx", [P, XTILES]), sb("x_sum", [P, XTILES]), sb("x_inv", [P, XTILES])
        pT = sb("pT", [P, PT_BUFS, 2, P])
        o_half, o_sum = sb("o_half", [P, KD, BU, TQ]), sb("o_sum", [P, KD, BU, TQ])
        oT = split("oT", [P, KD, BU, TQ])
        x1 = sb("x1", [P, D])
        a_res, a_x, a_n = sb("a_res", [P, D]), sb("a_x", [P, D]), sb("a_n", [P, D])
        a_st, a_mv, a_rs = sb("a_st", [P, 2, 6]), sb("a_mv", [P, 2, 2]), sb("a_rs", [P, 2, 2])
        aT = split("aT", [P, KD, P])
        a_nT, anT = sb("a_nT", [P, KD, P]), split("anT", [P, KD, P])
        a_raw = sb("a_raw", [P, 2, AH, AD])
        a_work = sb("a_work", [P, 2 * INNER])
        a_sq = a_work[:].rearrange("p (n h d) -> p n h d", n=2, h=AH)
        stage = (a_raw[:].rearrange("p n h d -> p (n h d)"), a_work)
        a_len = sb("a_len", [P, 2, AH])
        a_qk = sb("a_qk", [P, 1])
        qz = sb("qz", [P, AH, P])
        akT = sb("akT", [P, APAIRS, BU, AK])
        av = sb("av", [AK, BU, INNER])
        aS = sb("aS", [P, AH, AK])
        a_mx, a_sum = sb("a_mx", [P, AH]), sb("a_sum", [P, AH])
        apT, aoT = a_work[0:AK, :].rearrange("p (h t) -> p h t", h=AH), split("aoT", [P, APAIRS, P])
        x2 = sb("x2", [P, D])
        f_res, f_n, f_out = (sb(n, [P, D]) for n in ("f_res", "f_n", "f_out"))
        f_st, f_mv, f_rs = sb("f_st", [P, 6]), sb("f_mv", [P, 2]), sb("f_rs", [P, 2])
        fT = split("fT", [P, KD, P])
        z = sb("z", [P, P + E])
        g_e, g_s, g_gt, g_eq = sb("g_e", [P, E]), sb("g_s", [P, E]), sb("g_gt", [P, E, E]), sb("g_eq", [P, E, E])
        g_rank, g_sel, g_1 = sb("g_rank", [P, E]), sb("g_sel", [P, 3, E]), sb("g_1", [P, 4])
        g_top = sb("g_top", [P, E])
        zr, zT = sb("zr", [P, 3, E, R]), split("zT", [P, 2, P])
        f_h = sb("f_h", [P, FC, P])
        hT = split("hT", [P, FC, P])

        ps_s = [bank("ps_s0"), bank("ps_s1")]
        ps_t = [bank("ps_t0"), bank("ps_t1")]
        ps_o = bank("ps_o")
        ps_a = [bank("ps_a0"), bank("ps_a1")]
        ps_f = bank("ps_f")

        table = nc.dram_tensor("table", [XH, TQ, DIAGS], F32)
        table_ap = table.ap()

        block = ctx.enter_context(nc.Block())

        def tiles4(ap):
            return ap.rearrange("p (n c) -> p n c", n=4)

        def due(name, s):
            return [n for n, slot in enumerate(SLOT[name]) if slot == s]

        def last_user(t, bufs):
            return XTILES - 1 - (XTILES - 1 - t) % bufs

        def steps(eng, step):
            for i in range(3):
                step(i, True, i >= 1, i >= 2)
            with eng.Fori(3, UNITS - 1) as i:
                step(i, True, True, True)
            for i in range(UNITS - 1, UNITS + 2):
                step(i, i < UNITS, i - 1 < UNITS, True)

        N_CONST = 18

        pieces = [("wkT", 0, D, wk), ("wvT", 0, D, wv), ("wqT", 0, D, wq), ("woT", 0, D, wo),
                  ("a_wq", 0, INNER, a_wq), ("a_wkv", 0, INNER, a_wk), ("a_wkv", INNER, INNER, a_wv),
                  ("a_wo", 0, D, a_wo), ("f_zwT", 0, P + E, f_zw), ("f_wiT", 0, FF, f_wi),
                  ("f_loraB", 0, FF, f_loraB), ("f_woT", 0, D, f_wo)]
        X_PIECES, A_PIECES = 4, 8

        def staged(n):
            dst = pieces[n][3]
            hi, lo = ((dst[:, k].rearrange("p c n -> p (c n)") if len(dst.shape) == 4 else dst[:, k])
                      for k in range(2))
            return stage[n % 2][:, 0:hi.shape[1]], hi, lo

        @block.sync
        def _(sp):
            def load(u):
                if seen(u - 1):
                    sp.wait_ge(sem["x_normed"], lone(sp, "x_normed", u - 1, 1))
                if seen(u - 1):
                    sp.wait_ge(sem["x_kept"], lone(sp, "x_kept", u - 1, 1))
                sp.dma_start(x_ld[:], io["x"][bass.ts(u, P), :]).then_inc(sem["x_loaded"], 16)
                if seen(u - 1):
                    sp.wait_ge(sem["mask_scaled"], lone(sp, "mask_scaled", u - 1, 1))
                sp.dma_start(mask32[:], io["mask"][bass.ts(u, 1), :].broadcast_to([P, BU * TK // 4])).then_inc(sem["mask_loaded"], 16)
                if seen(u - 1):
                    sp.wait_ge(sem["ctx_split"], lone(sp, "ctx_split", u - 1, 2))
                if seen(u - 1):
                    sp.wait_ge(sem["v_done"], lone(sp, "v_done", u - 1, 2))
                sp.dma_start(ctxT[:].rearrange("p c b k -> p (c b k)"),
                             io["ctxT"][bass.ts(u, P), :]).then_inc(sem["ctx_loaded"], 16)

            def const(dst, src):
                sp.dma_start(dst, src).then_inc(sem["consts"], 16)
                const.n += 1
            const.n = 0

            def piece(n):
                if n >= 2:
                    sp.wait_ge(sem["split_lo"], n - 1)
                name, first, cols, _ = pieces[n]
                src = io[name][:, first:first + cols].rearrange("(c p) n -> p c n", p=P)
                to = staged(n)[0].rearrange("p (c n) -> p c n", n=cols)
                sp.dma_start(to, src).then_inc(sem["staged1" if n % 2 else "staged0"], 16)

            load(0)
            piece(0)
            piece(1)
            const(ident[:], io["c_ident"])
            const(headmask[:], io["c_headmask"])
            const(parity[:], io["c_parity"])
            const(relT[:], io["relT"])
            const(onehot[:], io["c_onehot"])
            const(nulls[:], io["null_k"])
            const(av[TQ:AK, 0, :], io["null_v"])
            const(av[TQ:AK, 1, :], io["null_v"])
            const(alibi[:], io["c_alibi"])
            const(f_bi[:], io["f_bi"])
            const(f_bo2[:], io["f_bo"].partition_broadcast(P))
            const(f_gb[:], io["f_gb"].partition_broadcast(P))
            const(lower[:], io["c_lower"])
            const(a_g[:], io["a_g"])
            const(a_b[:], io["a_b"])
            for h2 in range(2):
                const(a_qs[h2 * AD:(h2 + 1) * AD, :], io["a_qs"])
            const(a_ks[0:AD, :], io["a_ks"])
            assert const.n == N_CONST
            sp.dma_start(a_ks[AD:P, :], io["a_ks"]).then_inc(sem["consts"], 16)
            sp.wait_ge(sem["set_dve"], 1)
            sp.dma_start(table_ap, reltab[:].unsqueeze(1).broadcast_to([XH, TQ, DIAGS]))\
                .then_inc(sem["table_stored"], 16)
            sp.wait_ge(sem["table_stored"], 16)
            for h2 in range(2):
                src = bass.AP(table_ap.tensor, h2 * TQ * DIAGS + TQ - 1,
                              [[DIAGS - 1, TQ], [2 * TQ * DIAGS, XPAIRS], [1, TK]])
                sp.dma_start(bias[h2 * TQ:(h2 + 1) * TQ, :, :], src).then_inc(sem["table_loaded"], 16)

            for n in range(2, X_PIECES):
                piece(n)

            def step(i, do_x, do_a, do_f):
                if do_x and not (isinstance(i, int) and i + 1 >= UNITS):
                    load(i + 1)
                if isinstance(i, int) and i == 0:
                    for n in range(X_PIECES, len(pieces)):
                        piece(n)
                if do_f:
                    u = i - 2
                    sp.wait_ge(sem["out_ready"], lone(sp, "out_ready", u, 1))
                    sp.dma_start(out[bass.ts(u, P), :], f_out[:]).then_inc(sem["out_stored"], 16)

            steps(sp, step)
            sp.wait_ge(sem["out_stored"], 16 * UNITS)

        ALL_CONST = 16 * (N_CONST + 1)

        @block.tensor
        def _(pe):
            mm, turn = nc.tensor.matmul, nc.tensor.transpose

            def mm3(to, left, right, start, stop, **flags):
                mm(to, left(0), right(0), start=start, stop=False, **flags)
                mm(to, left(0), right(1), start=False, stop=False, **flags)
                return mm(to, left(1), right(0), start=False, stop=stop, **flags)

            def setup():
                pe.wait_ge(sem["consts"], ALL_CONST)
                mm(ps_s[0][0:XH, 0:DIAGS], relT[:], onehot[:], start=True, stop=True)\
                    .then_inc(sem["set_pe"], 1)
                pe.wait_ge(sem["set_pool"], 3)
                turn(ps_a[0][0:AD, 0:AH * NNULL], nulls[:], ident[0:32, 0:32])\
                    .then_inc(sem["set_pe"], 1)
                pe.wait_ge(sem["set_dve"], 1)
                pe.wait_ge(sem["set_act"], 1)

            def bias_through():
                pe.wait_ge(sem["set_dve"], 6)
                for c in range(FC):
                    last = mm3(ps_f[:, 0:D], lambda k: f_bis[:, k, c:c + 1].broadcast_to([P, P]),
                               lambda k: f_wo[:, k, c, :], c == 0, c == FC - 1)
                last.then_inc(sem["set_pe"], 1)
                pe.wait_ge(sem["set_dve"], 8)

            def x_k(u, g):
                if g == 0:
                    pe.wait_ge(sem["ctx_split"], at("ctx_split", u, 2))
                if seen(u - 1):
                    pe.wait_ge(sem["biased"], at("biased", u - 1, XTILES - 1 + g))
                for c in range(KD):
                    last = mm3(ps_s[g][:], lambda k: wk[:, k, c, g * P:(g + 1) * P],
                               lambda k: ctxS[:, k, c, :], c == 0, c == KD - 1)
                last.then_inc(sem["k_done"], 1)

            def x_v(u, n):
                if seen(u - 1):
                    pe.wait_ge(sem["probs_copied"], at("probs_copied", u - 1, XTILES - 1 + n))
                for j in range(2):
                    t = 2 * n + j
                    for c in range(KD):
                        last = mm3(ps_t[n][:, j * D:(j + 1) * D],
                                   lambda k: ctxS[:, k, c, t * P:(t + 1) * P],
                                   lambda k: wv[:, k, c, :], c == 0, c == KD - 1)
                last.then_inc(sem["v_done"], 1)

            def x_turn(u):
                pe.wait_ge(sem["x_normed"], at("x_normed", u, 1))
                if seen(u - 1):
                    pe.wait_ge(sem["x1_ready"], at("x1_ready", u - 1, 1))
                for c in range(KD):
                    last = turn(ps_o[:, c * P:(c + 1) * P], x_n[:, c * P:(c + 1) * P], ident[:])
                last.then_inc(sem["x_turned"], 1)

            def x_q(u):
                pe.wait_ge(sem["x_turned_copied"], at("x_turned_copied", u, 2))
                for g in range(KD):
                    for c in range(KD):
                        last = mm3(ps_o[:, 256 + g * P:256 + (g + 1) * P],
                                   lambda k: wq[:, k, c, g * P:(g + 1) * P], lambda k: xnT[:, k, c, :],
                                   c == 0, c == KD - 1)
                last.then_inc(sem["q_done"], 1)

            def x_scores(u, t):
                b, pair = t // XPAIRS, t % XPAIRS
                g, p4 = pair // 4, pair % 4
                if t == 0:
                    pe.wait_ge(sem["q_spread"], at("q_spread", u, 1))
                    pe.wait_ge(sem["k_copied"], at("k_copied", u, 2))
                elif t >= 2:
                    pe.wait_ge(sem["biased"], at("biased", u, t - 1))
                mm(ps_s[t % 2][:, 0:TK], qbd[:, g, b, 2 * p4:2 * p4 + 2, :].rearrange("p h q -> p (h q)"),
                   kT[:, g, b, :], start=True, stop=True).then_inc(sem["scores_done"], 1)

            def x_turn_probs(u, t):
                pe.wait_ge(sem["probs_ready"], at("probs_ready", u, t + 1))
                if t < 2:
                    pe.wait_ge(sem["v_copied"], at("v_copied", u, t + 1))
                else:
                    pe.wait_ge(sem["probs_copied"], at("probs_copied", u, t - 1))
                for c in range(2):
                    last = turn(ps_t[t % 2][:, c * P:(c + 1) * P], S[:, t % S_BUFS, c * P:(c + 1) * P], ident[:])
                last.then_inc(sem["probs_turned"], 1)

            def x_pv(u, t):
                b, pair = t // XPAIRS, t % XPAIRS
                g, p4 = pair // 4, pair % 4
                pe.wait_ge(sem["probs_copied"], at("probs_copied", u, t + 1))
                if t == 0:
                    pe.wait_ge(sem["v_copied"], at("v_copied", u, 2))
                o = ps_o[32 * p4:32 * p4 + 32, (g * BU + b) * P:(g * BU + b + 1) * P]
                for c in range(2):
                    last = mm(o, v[:, 2 * b + c, pair * 32:(pair + 1) * 32], pT[:, t % PT_BUFS, c, :],
                              start=(c == 0), stop=(c == 1))
                last.then_inc(sem["pv_done"], 1)

            def x_out(u):
                pe.wait_ge(sem["merged"], at("merged", u, 2))
                for g in range(KD):
                    last = mm3(ps_o[:, 0:D], lambda k: oT[:, k, g].rearrange("p b q -> p (b q)"),
                               lambda k: wo[:, k, g, :], g == 0, g == KD - 1)
                last.then_inc(sem["xo_done"], 1)

            def a_turn(u):
                pe.wait_ge(sem["a_normed"], at("a_normed", u, 2))
                if seen(u - 1):
                    pe.wait_ge(sem["apv_copied"], at("apv_copied", u - 1, 2))
                for n, src in enumerate((a_x, a_n)):
                    for c in range(KD):
                        last = turn(ps_a[0][:, (n * KD + c) * P:(n * KD + c + 1) * P],
                                    src[:, c * P:(c + 1) * P], ident[:])
                last.then_inc(sem["a_turned"], 1)

            def a_q(u, n):
                if n == 0:
                    pe.wait_ge(sem["a_turned_split"], at("a_turned_split", u, 4))
                    if seen(u - 1):
                        pe.wait_ge(sem["x2_ready"], at("x2_ready", u - 1, 1))
                for c in range(KD):
                    last = mm3(ps_a[1 - n][:], lambda k: anT[:, k, c, :],
                               lambda k: a_wq[:, k, c, n * 512:(n + 1) * 512], c == 0, c == KD - 1)
                last.then_inc(sem["aq_done"], 1)

            def a_k(u, n):
                pe.wait_ge(sem["a_squared"], at("a_squared", u, n + 1))
                for c in range(KD):
                    last = mm3(ps_a[1 - n][:], lambda k: aT[:, k, c, :],
                               lambda k: a_wk[:, k, c, n * 512:(n + 1) * 512], c == 0, c == KD - 1)
                last.then_inc(sem["ak_done"], 1)

            def a_v(u, n):
                pe.wait_ge(sem["a_squared"], at("a_squared", u, n + 3))
                for c in range(KD):
                    last = mm3(ps_a[1 - n][:], lambda k: aT[:, k, c, :],
                               lambda k: a_wv[:, k, c, n * 512:(n + 1) * 512], c == 0, c == KD - 1)
                last.then_inc(sem["av_done"], 1)

            def a_turn_qk(u, which, n):
                if n == 0:
                    pe.wait_ge(sem["a_unit"], at("a_unit", u, which + 1))
                if which == 0:
                    pe.wait_ge(sem["av_copied"], at("av_copied", u, 2 * n + 2))
                else:
                    pe.wait_ge(sem["aq_spread"], at("aq_spread", u, n + 1))
                for j in range(4):
                    pair = 4 * n + j
                    last = turn(ps_a[1 - n][:, j * P:(j + 1) * P],
                                a_raw[:, which, 2 * pair:2 * pair + 2, :].rearrange("p h d -> p (h d)"),
                                ident[:])
                last.then_inc(sem["ak_turned" if which else "aq_turned"], 1)

            def a_scores(u, n):
                if n < 2:
                    pe.wait_ge(sem["ak_placed"], at("ak_placed", u, 2))
                else:
                    pe.wait_ge(sem["as_biased"], at("as_biased", u, n - 1))
                for j in range(4):
                    h = 4 * n + j
                    for b in range(BU):
                        last = mm(ps_a[(n + 1) % 2][b * TQ:(b + 1) * TQ, j * AK:(j + 1) * AK],
                                  qz[:, h, b * TQ:(b + 1) * TQ], akT[:, h // 2, b, :],
                                  start=True, stop=True)
                last.then_inc(sem["as_done"], 1)

            def a_turn_probs(u, n):
                pe.wait_ge(sem["a_soft"], at("a_soft", u, 10 if n >= 2 else 7))
                if n >= 2:
                    pe.wait_ge(sem["ap_copied"], at("ap_copied", u, n - 1))
                for j in range(4):
                    last = turn(ps_a[(n + 1) % 2][0:AK, j * P:(j + 1) * P], aS[:, 4 * n + j, :], ident[:])
                last.then_inc(sem["ap_turned"], 1)

            def a_pv(u, n):
                pe.wait_ge(sem["ap_copied"], at("ap_copied", u, 4))
                for j in range(8):
                    h = 8 * n + j
                    for b in range(BU):
                        last = mm(ps_a[1 - n][(h % 2) * AD:(h % 2 + 1) * AD,
                                              (j // 2) * P + b * TQ:(j // 2) * P + (b + 1) * TQ],
                                  av[:, b, h * AD:(h + 1) * AD], apT[:, h, b * TQ:(b + 1) * TQ],
                                  start=True, stop=True)
                last.then_inc(sem["apv_done"], 1)

            def a_out(u):
                pe.wait_ge(sem["apv_copied"], at("apv_copied", u, 2))
                for c in range(APAIRS):
                    last = mm3(ps_a[1][:, 0:D], lambda k: aoT[:, k, c, :], lambda k: a_wo[:, k, c, :],
                               c == 0, c == APAIRS - 1)
                last.then_inc(sem["ao_done"], 1)

            def f_turn(u):
                pe.wait_ge(sem["f_normed"], at("f_normed", u, 1))
                if seen(u - 1):
                    pe.wait_ge(sem["y_sum"], at("y_sum", u - 1, 1))
                for c in range(KD):
                    last = turn(ps_f[:, c * P:(c + 1) * P], f_n[:, c * P:(c + 1) * P], ident[:])
                last.then_inc(sem["f_turned"], 1)

            def f_z(u):
                pe.wait_ge(sem["f_turned_copied"], at("f_turned_copied", u, 2))
                for c in range(KD):
                    last = mm3(ps_f[:, 0:P + E], lambda k: fT[:, k, c, :], lambda k: f_zw[:, k, c, :],
                               c == 0, c == KD - 1)
                last.then_inc(sem["z_done"], 1)

            def f_turn_z(u):
                pe.wait_ge(sem["z_routed"], at("z_routed", u, 3))
                pe.wait_ge(sem["z_copied"], at("z_copied", u, 1))
                for n, m in enumerate((0, 2)):
                    last = turn(ps_f[:, n * P:(n + 1) * P], zr[:, m].rearrange("p e r -> p (e r)"), ident[:])
                last.then_inc(sem["z_turned"], 1)

            def f_first(u, n):
                if n == 0:
                    pe.wait_ge(sem["z_turned_copied"], at("z_turned_copied", u, 2))
                else:
                    pe.wait_ge(sem["hid_ready"], at("hid_ready", u, 1))
                for j in range(4):
                    f = (4 * n + j) * P
                    for c in range(KD):
                        mm3(ps_f[:, j * P:(j + 1) * P], lambda k: f_wi[:, k, c, f:f + P],
                            lambda k: fT[:, k, c, :], j == 0 and c == 0, False, skip_group_check=True)
                    last = mm3(ps_f[:, j * P:(j + 1) * P], lambda k: f_loraB[:, k, f:f + P],
                               lambda k: zT[:, k, 0, :], False, False, skip_group_check=True)
                last.then_inc(sem["hid_first"], 1)

            def f_second(u, n):
                pe.wait_ge(sem["relu_done"], at("relu_done", u, n + 1))
                for j in range(4):
                    f = (4 * n + j) * P
                    last = mm3(ps_f[:, j * P:(j + 1) * P], lambda k: f_loraB[:, k, f:f + P],
                               lambda k: zT[:, k, 1, :], False, j == 3, skip_group_check=True)
                last.then_inc(sem["hid_second"], 1)

            def f_y(u):
                pe.wait_ge(sem["hid_split"], at("hid_split", u, 2))
                for c in range(FC):
                    last = mm3(ps_f[:, 0:D], lambda k: hT[:, k, c, :], lambda k: f_wo[:, k, c, :],
                               c == 0, c == FC - 1)
                last.then_inc(sem["y_done"], 1)

            setup()

            pe.wait_ge(sem["split_lo"], X_PIECES)

            def step(i, do_x, do_a, do_f):
                ua, uf = i - 1, i - 2
                if isinstance(i, int) and i == 1:
                    pe.wait_ge(sem["split_lo"], len(pieces))
                for s in SLOTS:
                    if do_x:
                        for n in due("pe_x_k", s):
                            x_k(i, n)
                    if do_a:
                        for n in due("pe_x_out", s):
                            x_out(ua)
                    if do_x:
                        for n in due("pe_x_v", s):
                            x_v(i, n)
                        for n in due("pe_x_turn", s):
                            x_turn(i)
                    if do_f:
                        for n in due("pe_a_out", s):
                            a_out(uf)
                    if do_x:
                        for n in due("pe_x_q", s):
                            x_q(i)
                    if do_f:
                        for n in due("pe_f_turn", s):
                            f_turn(uf)
                        for n in due("pe_f_z", s):
                            f_z(uf)
                        for n in due("pe_f_turn_z", s):
                            f_turn_z(uf)
                    if do_a:
                        for n in due("pe_a_turn", s):
                            a_turn(ua)
                        for n in due("pe_a_q", s):
                            a_q(ua, n)
                        for n in due("pe_a_k", s):
                            a_k(ua, n)
                        for n in due("pe_a_v", s):
                            a_v(ua, n)
                        for n in due("pe_a_turn_q", s):
                            a_turn_qk(ua, 0, n)
                        for n in due("pe_a_turn_k", s):
                            a_turn_qk(ua, 1, n)
                        for n in due("pe_a_scores", s):
                            a_scores(ua, n)
                        for n in due("pe_a_turn_probs", s):
                            a_turn_probs(ua, n)
                        for n in due("pe_a_pv", s):
                            a_pv(ua, n)
                    if do_f:
                        for n in due("pe_f_first", s):
                            f_first(uf, n)
                        for n in due("pe_f_second", s):
                            f_second(uf, n)
                        for n in due("pe_f_y", s):
                            f_y(uf)
                    if do_x:
                        t = s // 2
                        if s % 2 == 0 and 0 <= t < XTILES:
                            x_scores(i, t)
                        if s % 2 == 1 and 0 <= t - TURN_LAG < XTILES:
                            x_turn_probs(i, t - TURN_LAG)
                        if s % 2 == 1 and 0 <= t - TURN_LAG - PV_LAG:
                            x_pv(i, t - TURN_LAG - PV_LAG)
                if isinstance(i, int) and i == 1:
                    bias_through()

            steps(pe, step)

        @block.scalar
        def _(act):
            go = nc.scalar.activation

            def setup():
                act.wait_ge(sem["set_pe"], 2)
                src = ps_a[0][0:AD, 0:AH * NNULL].rearrange("d (pair h n) -> d h pair n", h=2, n=NNULL)
                for h2 in range(2):
                    for b in range(BU):
                        last = go(akT[h2 * AD:(h2 + 1) * AD, :, b, TQ:AK], src[:, h2], ACT.Copy)
                last.then_inc(sem["set_act"], 1)

            def split_hi(n):
                act.wait_ge(sem["staged1" if n % 2 else "staged0"], 16 * (n // 2 + 1))
                src, hi, _ = staged(n)
                go(hi, src, ACT.Copy, scale=UP).then_inc(sem["split_hi"], 1)

            def x_split_ctx(u):
                act.wait_ge(sem["ctx_loaded"], at("ctx_loaded", u, 16))
                if seen(u - 1):
                    act.wait_ge(sem["v_done"], at("v_done", u - 1, 2))
                go(ctxS[:, 0].rearrange("p c n -> p (c n)"), ctxT[:].rearrange("p c b k -> p (c b k)"),
                   ACT.Copy).then_inc(sem["ctx_split"], 1)

            def x_copy_turned(u):
                act.wait_ge(sem["x_turned"], at("x_turned", u, 1))
                go(xnT[:, 0].rearrange("p c t -> p (c t)"), ps_o[:, 0:2 * P], ACT.Copy)\
                    .then_inc(sem["x_turned_copied"], 1)

            def x_copy_k(u, g):
                if g == 0:
                    if seen(u - 1):
                        act.wait_ge(sem["scores_done"], at("scores_done", u - 1, XTILES))
                act.wait_ge(sem["k_done"], at("k_done", u, g + 1))
                go(kT[:, g].rearrange("p b k -> p (b k)"), ps_s[g][:], ACT.Copy, scale=DOWN)\
                    .then_inc(sem["k_copied"], 1)

            def x_exp(u, t):
                act.wait_ge(sem["biased"], at("biased", u, t + 1))
                go(S[:, t % S_BUFS, :], S[:, t % S_BUFS, :], ACT.Exp, bias=x_nmx[:, t:t + 1], scale=-1.0,
                   accum_out=x_sum[:, t:t + 1]).then_inc(sem["exp_done"], 1)

            def x_copy_probs(u, t):
                act.wait_ge(sem["probs_turned"], at("probs_turned", u, t + 1))
                if t >= PT_BUFS:
                    act.wait_ge(sem["pv_done"], at("pv_done", u, t - PT_BUFS + 1))
                elif seen(u - 1):
                    act.wait_ge(sem["pv_done"], at("pv_done", u - 1, last_user(t, PT_BUFS) + 1))
                go(pT[:, t % PT_BUFS].rearrange("p c m -> p (c m)"), ps_t[t % 2][:, 0:2 * P], ACT.Copy)\
                    .then_inc(sem["probs_copied"], 1)

            def x_copy_v(u, n):
                if n == 0:
                    if seen(u - 1):
                        act.wait_ge(sem["pv_done"], at("pv_done", u - 1, XTILES))
                act.wait_ge(sem["v_done"], at("v_done", u, n + 1))
                go(v[:, 2 * n:2 * n + 2, :].rearrange("p t d -> p (t d)"), ps_t[n][:], ACT.Copy,
                   scale=DOWN).then_inc(sem["v_copied"], 1)

            def x_merge(u):
                act.wait_ge(sem["pv_done"], at("pv_done", u, XTILES))
                if seen(u - 1):
                    act.wait_ge(sem["merge_b"], at("merge_b", u - 1, 2))
                o = ps_o[:].rearrange("p (g b h q) -> p g b h q", g=KD, b=BU, h=2)
                go(o_half[:].rearrange("p g b q -> p (g b) q"),
                   o.rearrange("p g b h q -> p (g b) h q")[:, :, 0, :],
                   ACT.Copy, scale=parity[:, 0:1]).then_inc(sem["merge_a"], 1)
                act.wait_ge(sem["merge_b"], at("merge_b", u, 2))
                if seen(u - 1):
                    act.wait_ge(sem["xo_done"], at("xo_done", u - 1, 1))
                go(oT[:, 0].rearrange("p g b q -> p (g b q)"), o_sum[:].rearrange("p g b q -> p (g b q)"),
                   ACT.Copy).then_inc(sem["merged"], 1)

            def a_copy_turned(u):
                act.wait_ge(sem["a_turned"], at("a_turned", u, 1))
                if seen(u - 1):
                    act.wait_ge(sem["av_done"], at("av_done", u - 1, 2))
                for c in range(KD):
                    last = go(a_nT[:, c, :], ps_a[0][:, (2 + c) * P:(3 + c) * P], ACT.Identity,
                              bias=a_b[:, c:c + 1], scale=a_g[:, c:c + 1])
                last.then_inc(sem["a_turned_copied"], 1)
                act.wait_ge(sem["a_turned_copied"], at("a_turned_copied", u, 1))
                flat = a_nT[:].rearrange("p c t -> p (c t)")
                go(anT[:, 0].rearrange("p c t -> p (c t)"), flat, ACT.Copy)\
                    .then_inc(sem["a_turned_split"], 1)
                go(aT[:, 0].rearrange("p c t -> p (c t)"), ps_a[0][:, 0:2 * P], ACT.Copy)\
                    .then_inc(sem["a_turned_split"], 1)

            def a_copy_raw(u, which, n):
                done, copied, turned = (("aq_done", "aq_copied", "aq_turned"), ("ak_done", "ak_copied", "ak_turned"))[which]
                if n == 0:
                    if seen(u - 1):
                        act.wait_ge(sem[turned], at(turned, u - 1, 2))
                act.wait_ge(sem[done], at(done, u, n + 1))
                go(a_raw[:, which, 8 * n:8 * n + 8, :].rearrange("p h d -> p (h d)"),
                   ps_a[1 - n][:], ACT.Copy, scale=DOWN).then_inc(sem[copied], 1)
                if seen(u - 1) and n == 0:
                    act.wait_ge(sem["a_sumsq"], at("a_sumsq", u - 1, which + 1))
                go(a_sq[:, which, 8 * n:8 * n + 8, :].rearrange("p h d -> p (h d)"),
                   ps_a[1 - n][:], ACT.Square, scale=DOWN).then_inc(sem["a_squared"], 1)

            def a_copy_v(u, n):
                if n == 0:
                    if seen(u - 1):
                        act.wait_ge(sem["apv_done"], at("apv_done", u - 1, 2))
                act.wait_ge(sem["av_done"], at("av_done", u, n + 1))
                for b in range(BU):
                    go(av[0:TQ, b, n * 512:(n + 1) * 512], ps_a[1 - n][b * TQ:(b + 1) * TQ, :],
                       ACT.Copy, scale=DOWN).then_inc(sem["av_copied"], 1)

            def a_exp(u, half):
                act.wait_ge(sem["a_soft"], at("a_soft", u, 2 * half + 2))
                s = aS[:, 8 * half:8 * half + 8, :].rearrange("p h k -> p (h k)")
                go(s, s, ACT.Exp).then_inc(sem["a_exp"], 1)

            def a_copy_probs(u, n):
                act.wait_ge(sem["ap_turned"], at("ap_turned", u, n + 1))
                if n == 0:
                    if seen(u - 1):
                        act.wait_ge(sem["apv_done"], at("apv_done", u - 1, 2))
                go(apT[:, 4 * n:4 * n + 4, :].rearrange("k h t -> k (h t)"), ps_a[(n + 1) % 2][0:AK, :],
                   ACT.Copy).then_inc(sem["ap_copied"], 1)

            def a_copy_pv(u, n):
                act.wait_ge(sem["apv_done"], at("apv_done", u, n + 1))
                if seen(u - 1):
                    act.wait_ge(sem["ao_done"], at("ao_done", u - 1, 1))
                go(aoT[:, 0, 4 * n:4 * n + 4, :].rearrange("p c t -> p (c t)"), ps_a[1 - n][:], ACT.Copy)\
                    .then_inc(sem["apv_hi"], 1)

            def f_copy_turned(u):
                act.wait_ge(sem["f_turned"], at("f_turned", u, 1))
                if seen(u - 1):
                    act.wait_ge(sem["hid_first"], at("hid_first", u - 1, 2))
                go(fT[:, 0].rearrange("p c t -> p (c t)"), ps_f[:, 0:2 * P], ACT.Copy)\
                    .then_inc(sem["f_turned_copied"], 1)

            def f_exp(u):
                act.wait_ge(sem["route"], at("route", u, 2))
                go(g_e[:], g_s[:], ACT.Exp, bias=g_1[:, 0:1], accum_out=g_1[:, 1:2])\
                    .then_inc(sem["f_exp"], 1)

            def f_copy_z(u):
                act.wait_ge(sem["z_turned"], at("z_turned", u, 1))
                if seen(u - 1):
                    act.wait_ge(sem["hid_second"], at("hid_second", u - 1, 2))
                go(zT[:, 0].rearrange("p n t -> p (n t)"), ps_f[:, 0:2 * P], ACT.Copy)\
                    .then_inc(sem["z_turned_copied"], 1)

            def f_relu(u, n):
                act.wait_ge(sem["hid_first"], at("hid_first", u, n + 1))
                if seen(u - 1):
                    act.wait_ge(sem["hid_split"], at("hid_split", u - 1, n + 1))
                for j in range(4):
                    c = 4 * n + j
                    last = go(f_h[:, c, :], ps_f[:, j * P:(j + 1) * P], ACT.Relu, bias=f_bup[:, 0, c:c + 1])
                last.then_inc(sem["relu_done"], 1)

            def f_split_hid(u, n):
                act.wait_ge(sem["hid_ready"], at("hid_ready", u, n + 1))
                if seen(u - 1):
                    act.wait_ge(sem["y_done"], at("y_done", u - 1, 1))
                go(hT[:, 0, 4 * n:4 * n + 4, :].rearrange("p c t -> p (c t)"),
                   f_h[:, 4 * n:4 * n + 4, :].rearrange("p c t -> p (c t)"), ACT.Copy, scale=DOWN)\
                    .then_inc(sem["hid_hi"], 1)

            def a_spread(u, n):
                if n == 0:
                    if seen(u - 1):
                        act.wait_ge(sem["as_done"], at("as_done", u - 1, 4))
                act.wait_ge(sem["aq_turned"], at("aq_turned", u, n + 1))
                for h2 in range(2):
                    rows = slice(h2 * AD, (h2 + 1) * AD)
                    last = go(qz[rows, 8 * n + h2:8 * n + 8:2, :], tiles4(ps_a[1 - n][rows, :]),
                              ACT.Copy, scale=a_qk[rows, 0:1])
                last.then_inc(sem["aq_spread"], 1)

            def step(i, do_x, do_a, do_f):
                ua, uf = i - 1, i - 2
                ahead = do_x and not (isinstance(i, int) and i + 1 >= UNITS)
                for s in SLOTS:
                    if do_x:
                        for n in due("act_x_copy_k", s):
                            x_copy_k(i, n)
                        for n in due("act_x_copy_turned", s):
                            x_copy_turned(i)
                        for n in due("act_x_copy_v", s):
                            x_copy_v(i, n)
                    if isinstance(i, int) and i == 0 and 2 <= s // 2 < 2 + len(pieces) - X_PIECES and s % 2 == 0:
                        split_hi(X_PIECES + s // 2 - 2)
                    if do_f:
                        for n in due("act_f_copy_turned", s):
                            f_copy_turned(uf)
                        for n in due("act_f_exp", s):
                            f_exp(uf)
                        for n in due("act_f_copy_z", s):
                            f_copy_z(uf)
                    if do_a:
                        for n in due("act_a_copy_turned", s):
                            a_copy_turned(ua)
                        for n in due("act_a_copy_q", s):
                            a_copy_raw(ua, 0, n)
                        for n in due("act_a_copy_k", s):
                            a_copy_raw(ua, 1, n)
                        for n in due("act_a_copy_v", s):
                            a_copy_v(ua, n)
                        for n in due("act_a_spread", s):
                            a_spread(ua, n)
                        for n in due("act_a_exp", s):
                            a_exp(ua, n)
                        for n in due("act_a_copy_probs", s):
                            a_copy_probs(ua, n)
                        for n in due("act_a_copy_pv", s):
                            a_copy_pv(ua, n)
                    if do_f:
                        for n in due("act_f_relu", s):
                            f_relu(uf, n)
                        for n in due("act_f_split_hid", s):
                            f_split_hid(uf, n)
                    if ahead:
                        for n in due("act_x_split_ctx", s):
                            x_split_ctx(i + 1)
                    if do_x:
                        t = s // 2
                        if s % 2 == 0 and 0 <= t < XTILES:
                            x_exp(i, t)
                        if s % 2 == 1 and 0 <= t - TURN_LAG < XTILES:
                            x_copy_probs(i, t - TURN_LAG)
                if do_x:
                    x_merge(i)

            setup()
            for n in range(X_PIECES):
                split_hi(n)
            x_split_ctx(0)
            act.wait_ge(sem["consts"], ALL_CONST)
            act.wait_ge(sem["set_dve"], 5)
            act.wait_ge(sem["set_pool"], 2)
            steps(act, step)

        @block.vector
        def _(dve):
            tt, ts, stt = nc.vector.tensor_tensor, nc.vector.tensor_scalar, nc.vector.scalar_tensor_tensor

            def setup():
                dve.wait_ge(sem["consts"], ALL_CONST)
                dve.wait_ge(sem["set_pe"], 1)
                nc.vector.tensor_copy(reltab[:], ps_s[0][0:XH, 0:DIAGS]).then_inc(sem["set_dve"], 1)
                tt(a_qk[:], a_qs[:], a_ks[:], ALU.mult).then_inc(sem["set_dve"], 1)
                dve.wait_ge(sem["set_dve"], 2)
                ts(a_qk[:], a_qk[:], 8.0, None, ALU.mult).then_inc(sem["set_dve"], 1)
                dve.wait_ge(sem["set_pool"], 1)
                nc.vector.tensor_reduce(null_len[:, 0:1], null_sq[:], AX, ALU.add)\
                    .then_inc(sem["set_dve"], 1)
                for k, by in enumerate((UP, -UP)):
                    ts(f_bup[:, k, :], f_bi[:], by, None, ALU.mult)
                nc.vector.tensor_copy(f_bis[:, 0, :], f_bi[:]).then_inc(sem["set_dve"], 1)
                dve.wait_ge(sem["set_dve"], 5)
                tt(f_bis[:, 1, :], f_bi[:], f_bis[:, 0, :], ALU.subtract).then_inc(sem["set_dve"], 1)

            def bias_out():
                dve.wait_ge(sem["set_pe"], 3)
                ts(f_bo2[:], f_bo2[:], 2.0, None, ALU.mult).then_inc(sem["set_dve"], 1)
                dve.wait_ge(sem["set_dve"], 7)
                stt(f_bo2[:], ps_f[:, 0:D], DOWN, f_bo2[:], ALU.mult, ALU.add).then_inc(sem["set_dve"], 1)

            def split_lo(n):
                dve.wait_ge(sem["split_hi"], n + 1)
                src, hi, lo = staged(n)
                stt(lo, src, UP, hi, ALU.mult, ALU.subtract).then_inc(sem["split_lo"], 1)

            def stats(u, src, st, mv, name, k):
                nc.vector.bn_stats(st, src).then_inc(sem[name], 1)
                dve.wait_ge(sem[name], lone(dve, name, u, 2 * k + 1))
                nc.vector.bn_aggr(mv, st).then_inc(sem[name], 1)

            def norm(src, dst, mv, rs):
                return ts(dst, src, mv[:, 0:1], rs[:, 1:2], ALU.subtract, ALU.mult)

            def x_stats(u):
                dve.wait_ge(sem["x_loaded"], at("x_loaded", u, 16))
                stats(u, x_ld[:], x_st[:], x_mv[:], "x_stats", 0)

            def x_norm(u):
                if seen(u - 1):
                    dve.wait_ge(sem["x_turned"], at("x_turned", u - 1, 1))
                dve.wait_ge(sem["x_rstd"], at("x_rstd", u, 2))
                norm(x_ld[:], x_n[:], x_mv, x_rs).then_inc(sem["x_normed"], 1)

            def x_split_ctx(u):
                dve.wait_ge(sem["ctx_split"], at("ctx_split", u, 1))
                tt(ctxS[:, 1].rearrange("p c n -> p (c n)"), ctxT[:].rearrange("p c b k -> p (c b k)"),
                   ctxS[:, 0].rearrange("p c n -> p (c n)"), ALU.subtract).then_inc(sem["ctx_split"], 1)

            def rest(to, of, less):
                return tt(to, of, less, ALU.subtract)

            def x_split_turned(u):
                dve.wait_ge(sem["x_turned_copied"], at("x_turned_copied", u, 1))
                flat = [xnT[:, k].rearrange("p c t -> p (c t)") for k in range(2)]
                rest(flat[1], ps_o[:, 0:2 * P], flat[0]).then_inc(sem["x_turned_copied"], 1)

            def x_spread_q(u):
                dve.wait_ge(sem["q_done"], at("q_done", u, 1))
                if seen(u - 1):
                    dve.wait_ge(sem["scores_done"], at("scores_done", u - 1, XTILES))
                for g in range(KD):
                    for b in range(BU):
                        q = ps_o[:, 256 + g * P + b * TQ:256 + g * P + (b + 1) * TQ]
                        last = tt(qbd[:, g, b], q.unsqueeze(1).broadcast_to([P, 8, TQ]),
                                  headmask[:].unsqueeze(2).broadcast_to([P, 8, TQ]), ALU.mult)
                last.then_inc(sem["q_spread"], 1)

            def x_bias(u, t):
                b, pair = t // XPAIRS, t % XPAIRS
                dve.wait_ge(sem["scores_done"], lone(dve, "scores_done", u, t + 1))
                if pair % (XPAIRS // 2) == 0:
                    dve.wait_ge(sem["bias_masked"], lone(dve, "bias_masked", u, t // (XPAIRS // 2) + 1))
                if t >= S_BUFS:
                    dve.wait_ge(sem["probs_turned"], lone(dve, "probs_turned", u, t - S_BUFS + 1))
                elif seen(u - 1):
                    dve.wait_ge(sem["probs_turned"], lone(dve, "probs_turned", u - 1, last_user(t, S_BUFS) + 1))
                nc.vector.tensor_tensor_reduce(
                    out=S[:, t % S_BUFS, :], in0=ps_s[t % 2][:, 0:TK], in1=bm[:, b, pair, :], scale=-1.0,
                    scalar=BIG, op0=ALU.add, op1=ALU.min, accum_out=x_nmx[:, t:t + 1])\
                    .then_inc(sem["biased"], 1)

            def x_scale(u, t):
                dve.wait_ge(sem["exp_done"], at("exp_done", u, t + 1))
                nc.vector.reciprocal(x_inv[:, t:t + 1], x_sum[:, t:t + 1]).then_inc(sem["recip_done"], 1)
                dve.wait_ge(sem["recip_done"], at("recip_done", u, t + 1))
                ts(S[:, t % S_BUFS, :], S[:, t % S_BUFS, :], x_inv[:, t:t + 1], None, ALU.mult)\
                    .then_inc(sem["probs_ready"], 1)

            def x_merge(u):
                dve.wait_ge(sem["merge_a"], at("merge_a", u, 1))
                o = ps_o[:].rearrange("p (g b h q) -> p g b h q", g=KD, b=BU, h=2)
                for g in range(KD):
                    stt(o_sum[:, g], o[:, g, :, 1, :], parity[:, 1:2], o_half[:, g], ALU.mult, ALU.add)\
                        .then_inc(sem["merge_b"], 1)
                dve.wait_ge(sem["merged"], at("merged", u, 1))
                rest(oT[:, 1], o_sum[:], oT[:, 0]).then_inc(sem["merged"], 1)

            def x_residual(u):
                dve.wait_ge(sem["xo_done"], at("xo_done", u, 1))
                dve.wait_ge(sem["x_kept"], at("x_kept", u, 1))
                if seen(u - 1):
                    dve.wait_ge(sem["a_kept"], at("a_kept", u - 1, 1))
                if seen(u - 1):
                    dve.wait_ge(sem["a_normed"], at("a_normed", u - 1, 1))
                stt(x1[:], ps_o[:, 0:D], DOWN, x_res[:], ALU.mult, ALU.add).then_inc(sem["x1_ready"], 1)

            def a_stats(u, k):
                src = (x1, a_x)[k]
                if k == 0:
                    dve.wait_ge(sem["x1_ready"], at("x1_ready", u, 1))
                else:
                    dve.wait_ge(sem["a_normed"], at("a_normed", u, 1))
                stats(u, src[:], a_st[:, k], a_mv[:, k], "a_stats", k)

            def a_norm(u, k):
                src, dst = ((x1, a_x), (a_x, a_n))[k]
                if seen(u - 1):
                    dve.wait_ge(sem["a_turned"], at("a_turned", u - 1, 1))
                dve.wait_ge(sem["a_rstd"], at("a_rstd", u, 2 * k + 2))
                norm(src[:], dst[:], a_mv[:, k], a_rs[:, k]).then_inc(sem["a_normed"], 1)

            def a_split_turned(u):
                dve.wait_ge(sem["a_turned_split"], at("a_turned_split", u, 2))
                rest(anT[:, 1], a_nT[:], anT[:, 0]).then_inc(sem["a_turned_split"], 1)
                rest(aT[:, 1].rearrange("p c t -> p (c t)"), ps_a[0][:, 0:2 * P],
                     aT[:, 0].rearrange("p c t -> p (c t)")).then_inc(sem["a_turned_split"], 1)

            def a_lengths(u, which):
                dve.wait_ge(sem["a_squared"], at("a_squared", u, 2 * which + 2))
                nc.vector.tensor_reduce(a_len[:, which, :], a_sq[:, which], AX, ALU.add)\
                    .then_inc(sem["a_sumsq"], 1)

            def a_unit(u, which):
                dve.wait_ge(sem["a_len"], at("a_len", u, 2 * which + 2))
                tt(a_raw[:, which], a_raw[:, which],
                   a_len[:, which, :].unsqueeze(2).broadcast_to([P, AH, AD]), ALU.mult)\
                    .then_inc(sem["a_unit"], 1)

            def a_place_keys(u, n):
                if n == 0:
                    if seen(u - 1):
                        dve.wait_ge(sem["as_done"], at("as_done", u - 1, 4))
                dve.wait_ge(sem["ak_turned"], at("ak_turned", u, n + 1))
                nc.vector.tensor_copy(
                    akT[:, 4 * n:4 * n + 4, :, 0:TQ],
                    ps_a[1 - n][:].rearrange("p (j b t) -> p j b t", j=4, b=BU)).then_inc(sem["ak_placed"], 1)

            def a_bias(u, n):
                dve.wait_ge(sem["as_done"], at("as_done", u, n + 1))
                if n == 0:
                    if seen(u - 1):
                        dve.wait_ge(sem["ap_turned"], at("ap_turned", u - 1, 4))
                tt(aS[:, 4 * n:4 * n + 4, :], ps_a[(n + 1) % 2][:, 0:4 * AK].rearrange("p (h k) -> p h k", h=4),
                   alibi[:, 4 * n:4 * n + 4, :], ALU.add).then_inc(sem["as_biased"], 1)

            def a_softmax_top(u, part):
                h = slice(8 * part, 8 * part + 8)
                dve.wait_ge(sem["as_biased"], at("as_biased", u, 2 * part + 2))
                nc.vector.tensor_reduce(a_mx[:, h], aS[:, h, :], AX, ALU.max).then_inc(sem["a_soft"], 1)
                dve.wait_ge(sem["a_soft"], at("a_soft", u, 2 * part + 1))
                tt(aS[:, h, :], aS[:, h, :], a_mx[:, h].unsqueeze(2).broadcast_to([P, 8, AK]), ALU.subtract)\
                    .then_inc(sem["a_soft"], 1)

            def a_softmax_end(u, part):
                h = slice(8 * part, 8 * part + 8)
                dve.wait_ge(sem["a_exp"], at("a_exp", u, part + 1))
                nc.vector.tensor_reduce(a_sum[:, h], aS[:, h, :], AX, ALU.add).then_inc(sem["a_soft"], 1)
                dve.wait_ge(sem["a_soft"], at("a_soft", u, 4 + 3 * part + 1))
                nc.vector.reciprocal(a_sum[:, h], a_sum[:, h]).then_inc(sem["a_soft"], 1)
                dve.wait_ge(sem["a_soft"], at("a_soft", u, 4 + 3 * part + 2))
                tt(aS[:, h, :], aS[:, h, :], a_sum[:, h].unsqueeze(2).broadcast_to([P, 8, AK]), ALU.mult)\
                    .then_inc(sem["a_soft"], 1)

            def a_split_pv(u, n):
                dve.wait_ge(sem["apv_hi"], at("apv_hi", u, n + 1))
                hi, lo = (aoT[:, k, 4 * n:4 * n + 4, :].rearrange("p c t -> p (c t)") for k in range(2))
                rest(lo, ps_a[1 - n][:], hi).then_inc(sem["apv_copied"], 1)

            def a_residual(u):
                dve.wait_ge(sem["ao_done"], at("ao_done", u, 1))
                dve.wait_ge(sem["a_kept"], at("a_kept", u, 1))
                if seen(u - 1):
                    dve.wait_ge(sem["f_kept"], at("f_kept", u - 1, 1))
                if seen(u - 1):
                    dve.wait_ge(sem["f_normed"], at("f_normed", u - 1, 1))
                stt(x2[:], ps_a[1][:, 0:D], DOWN, a_res[:], ALU.mult, ALU.add).then_inc(sem["x2_ready"], 1)

            def f_stats(u):
                dve.wait_ge(sem["x2_ready"], at("x2_ready", u, 1))
                stats(u, x2[:], f_st[:], f_mv[:], "f_stats", 0)

            def f_norm(u):
                if seen(u - 1):
                    dve.wait_ge(sem["f_turned"], at("f_turned", u - 1, 1))
                dve.wait_ge(sem["f_rstd"], at("f_rstd", u, 2))
                norm(x2[:], f_n[:], f_mv, f_rs).then_inc(sem["f_normed"], 1)

            def f_split_turned(u):
                dve.wait_ge(sem["f_turned_copied"], at("f_turned_copied", u, 1))
                flat = [fT[:, k].rearrange("p c t -> p (c t)") for k in range(2)]
                rest(flat[1], ps_f[:, 0:2 * P], flat[0]).then_inc(sem["f_turned_copied"], 1)

            def f_split_z(u):
                dve.wait_ge(sem["z_turned_copied"], at("z_turned_copied", u, 1))
                flat = [zT[:, k].rearrange("p n t -> p (n t)") for k in range(2)]
                rest(flat[1], ps_f[:, 0:2 * P], flat[0]).then_inc(sem["z_turned_copied"], 1)

            def f_logits(u):
                dve.wait_ge(sem["z_done"], at("z_done", u, 1))
                if seen(u - 1):
                    dve.wait_ge(sem["z_routed"], at("z_routed", u - 1, 3))
                ts(z[:, 0:P], ps_f[:, 0:P], DOWN, None, ALU.mult).then_inc(sem["z_copied"], 1)
                stt(g_s[:], ps_f[:, P:P + E], DOWN, f_gb[:], ALU.mult, ALU.add).then_inc(sem["route"], 1)
                dve.wait_ge(sem["route"], at("route", u, 1))
                nc.vector.tensor_reduce(g_1[:, 0:1], g_s[:], AX, ALU.max, negate=True)\
                    .then_inc(sem["route"], 1)

            def f_route(u):
                dve.wait_ge(sem["f_exp"], at("f_exp", u, 1))
                nc.vector.reciprocal(g_1[:, 2:3], g_1[:, 1:2]).then_inc(sem["route"], 1)
                dve.wait_ge(sem["route"], at("route", u, 3))
                ts(g_s[:], g_e[:], g_1[:, 2:3], None, ALU.mult).then_inc(sem["route"], 1)
                dve.wait_ge(sem["route"], at("route", u, 4))
                mine = g_s[:].unsqueeze(2).broadcast_to([P, E, E])
                other = g_s[:].unsqueeze(1).broadcast_to([P, E, E])
                tt(g_gt[:], other, mine, ALU.is_gt)
                tt(g_eq[:], other, mine, ALU.is_equal).then_inc(sem["route"], 1)
                dve.wait_ge(sem["route"], at("route", u, 5))
                tt(g_eq[:], g_eq[:], lower[:], ALU.mult).then_inc(sem["route"], 1)
                dve.wait_ge(sem["route"], at("route", u, 6))
                tt(g_gt[:], g_gt[:], g_eq[:], ALU.add).then_inc(sem["route"], 1)
                dve.wait_ge(sem["route"], at("route", u, 7))
                nc.vector.tensor_reduce(g_rank[:], g_gt[:], AX, ALU.add).then_inc(sem["route"], 1)
                dve.wait_ge(sem["route"], at("route", u, 8))
                ts(g_sel[:, 0, :], g_rank[:], 0.0, None, ALU.is_equal)
                ts(g_sel[:, 1, :], g_rank[:], 1.0, None, ALU.is_equal)
                if seen(u - 1):
                    dve.wait_ge(sem["out_ready"], at("out_ready", u - 1, 1))
                stt(g_top[:], g_rank[:], 2.0, g_s[:], ALU.is_lt, ALU.mult, accum_out=g_1[:, 3:4])\
                    .then_inc(sem["route"], 1)
                dve.wait_ge(sem["route"], at("route", u, 9))
                zs = z[:, 0:P].rearrange("p (e r) -> p e r", e=E)
                if seen(u - 1):
                    dve.wait_ge(sem["z_turned"], at("z_turned", u - 1, 1))
                for n in range(2):
                    tt(zr[:, n], zs, g_sel[:, n, :].unsqueeze(2).broadcast_to([P, E, R]), ALU.mult)\
                        .then_inc(sem["z_routed"], 1)
                dve.wait_ge(sem["z_routed"], at("z_routed", u, 2))
                tt(zr[:, 2], zr[:, 1], zr[:, 0], ALU.subtract).then_inc(sem["z_routed"], 1)

            def f_second(u, n):
                dve.wait_ge(sem["hid_second"], at("hid_second", u, n + 1))
                for j in range(4):
                    c = 4 * n + j
                    last = stt(f_h[:, c, :], ps_f[:, j * P:(j + 1) * P], f_bup[:, 1, c:c + 1], f_h[:, c, :],
                               ALU.max, ALU.add)
                last.then_inc(sem["hid_ready"], 1)

            def f_split_hid(u, n):
                dve.wait_ge(sem["hid_hi"], at("hid_hi", u, n + 1))
                c = slice(4 * n, 4 * n + 4)
                stt(hT[:, 1, c, :], f_h[:, c, :], DOWN, hT[:, 0, c, :], ALU.mult, ALU.subtract)\
                    .then_inc(sem["hid_split"], 1)

            def f_final(u):
                dve.wait_ge(sem["y_done"], at("y_done", u, 1))
                if seen(u - 1):
                    dve.wait_ge(sem["out_stored"], at("out_stored", u - 1, 16))
                stt(f_out[:], ps_f[:, 0:D], DOWN, f_bo2[:], ALU.mult, ALU.add).then_inc(sem["y_sum"], 1)
                dve.wait_ge(sem["y_sum"], at("y_sum", u, 1))
                dve.wait_ge(sem["f_kept"], at("f_kept", u, 1))
                stt(f_out[:], f_out[:], g_1[:, 3:4], f_res[:], ALU.mult, ALU.add)\
                    .then_inc(sem["out_ready"], 1)

            setup()
            for n in range(X_PIECES):
                split_lo(n)
            x_stats(0)
            x_norm(0)
            x_split_ctx(0)

            def step(i, do_x, do_a, do_f):
                ua, uf = i - 1, i - 2
                ahead = do_x and not (isinstance(i, int) and i + 1 >= UNITS)
                for s in SLOTS:
                    if do_a:
                        for n in due("dve_x_residual", s):
                            x_residual(ua)
                    if do_x:
                        for n in due("dve_x_split_turned", s):
                            x_split_turned(i)
                        for n in due("dve_x_spread_q", s):
                            x_spread_q(i)
                    if do_f:
                        for n in due("dve_a_residual", s):
                            a_residual(uf)
                        for n in due("dve_f_stats", s):
                            f_stats(uf)
                    if do_a:
                        for n in due("dve_a_stats", s):
                            a_stats(ua, n)
                    if do_f:
                        for n in due("dve_f_norm", s):
                            f_norm(uf)
                    if do_a:
                        for n in due("dve_a_norm", s):
                            a_norm(ua, n)
                    if do_f:
                        for n in due("dve_f_split_turned", s):
                            f_split_turned(uf)
                        for n in due("dve_f_logits", s):
                            f_logits(uf)
                        for n in due("dve_f_route", s):
                            f_route(uf)
                        for n in due("dve_f_split_z", s):
                            f_split_z(uf)
                    if isinstance(i, int) and i == 0 and 2 <= s // 2 < 2 + len(pieces) - X_PIECES and s % 2 == 1:
                        split_lo(X_PIECES + s // 2 - 2)
                    if do_a:
                        for n in due("dve_a_split_turned", s):
                            a_split_turned(ua)
                        for n in due("dve_a_lengths", s):
                            a_lengths(ua, n)
                        for n in due("dve_a_unit", s):
                            a_unit(ua, n)
                        for n in due("dve_a_place_keys", s):
                            a_place_keys(ua, n)
                        for n in due("dve_a_bias", s):
                            a_bias(ua, n)
                        for n in due("dve_a_softmax_top", s):
                            a_softmax_top(ua, n)
                        for n in due("dve_a_softmax_end", s):
                            a_softmax_end(ua, n)
                        for n in due("dve_a_split_pv", s):
                            a_split_pv(ua, n)
                    if do_f:
                        for n in due("dve_f_second", s):
                            f_second(uf, n)
                        for n in due("dve_f_split_hid", s):
                            f_split_hid(uf, n)
                        for n in due("dve_f_final", s):
                            f_final(uf)
                    if ahead:
                        for n in due("dve_x_stats", s):
                            x_stats(i + 1)
                        for n in due("dve_x_norm", s):
                            x_norm(i + 1)
                        for n in due("dve_x_split_ctx", s):
                            x_split_ctx(i + 1)
                    if do_x:
                        t = s // 2
                        if s % 2 == 0 and 0 <= t < XTILES:
                            x_bias(i, t)
                        if s % 2 == 1 and 0 <= t - 1 < XTILES:
                            x_scale(i, t - 1)
                if isinstance(i, int) and i == 1:
                    bias_out()
                if do_x:
                    x_merge(i)

            steps(dve, step)

        @block.gpsimd
        def _(pool):
            tt, ts = nc.gpsimd.tensor_tensor, nc.gpsimd.tensor_scalar

            def setup():
                pool.memset(half[:], -0.5).then_inc(sem["half"], 1)
                pool.wait_ge(sem["half"], 1)
                pool.wait_ge(sem["consts"], ALL_CONST)
                tt(null_sq[:], nulls[:], nulls[:], ALU.mult).then_inc(sem["set_pool"], 1)
                pool.memset(qz[:], 0.0).then_inc(sem["set_pool"], 1)
                pool.wait_ge(sem["set_dve"], 4)
                ts(null_len[:, 1:2], null_len[:, 0:1], 1e-24, None, ALU.max).then_inc(sem["half"], 1)
                pool.wait_ge(sem["half"], 2)
                tt(null_len[:, 1:2], null_len[:, 1:2], half[0:32, 0:1], ALU.pow).then_inc(sem["half"], 1)
                pool.wait_ge(sem["half"], 3)
                ts(nulls[:], nulls[:], null_len[:, 1:2], None, ALU.mult).then_inc(sem["set_pool"], 1)
                pool.wait_ge(sem["table_loaded"], 32)

            def rstd(u, mv, rs, stats, done, k):
                pool.wait_ge(sem[stats], lone(pool, stats, u, 2 * k + 2))
                ts(rs[:, 0:1], mv[:, 1:2], EPS, None, ALU.add).then_inc(sem[done], 1)
                pool.wait_ge(sem[done], lone(pool, done, u, 2 * k + 1))
                tt(rs[:, 1:2], rs[:, 0:1], half[:, 0:1], ALU.pow).then_inc(sem[done], 1)

            def x_rstd(u):
                if seen(u - 1):
                    pool.wait_ge(sem["x_normed"], lone(pool, "x_normed", u - 1, 1))
                rstd(u, x_mv, x_rs, "x_stats", "x_rstd", 0)

            def x_keep(u):
                pool.wait_ge(sem["x_loaded"], lone(pool, "x_loaded", u, 16))
                if seen(u - 1):
                    pool.wait_ge(sem["x1_ready"], lone(pool, "x1_ready", u - 1, 1))
                pool.tensor_copy(x_res[:], x_ld[:]).then_inc(sem["x_kept"], 1)

            def x_mask(u):
                pool.wait_ge(sem["mask_loaded"], lone(pool, "mask_loaded", u, 16))
                if seen(u - 1):
                    pool.wait_ge(sem["bias_masked"], lone(pool, "bias_masked", u - 1, 4))
                ts(negm[:].rearrange("p b k -> p (b k)"), mask32[:].bitcast(U8), MASKED, -MASKED, ALU.mult, ALU.add).then_inc(sem["mask_scaled"], 1)

            def x_bias(u, n):
                half_pairs = XPAIRS // 2
                b, pairs = n // 2, slice(n % 2 * half_pairs, (n % 2 + 1) * half_pairs)
                if n == 0:
                    pool.wait_ge(sem["mask_scaled"], lone(pool, "mask_scaled", u, 1))
                if seen(u - 1):
                    pool.wait_ge(sem["biased"], lone(pool, "biased", u - 1, half_pairs * (n + 1)))
                tt(bm[:, b, pairs], bias[:, pairs], negm[:, b, :].unsqueeze(1).broadcast_to([P, half_pairs, TK]),
                   ALU.add).then_inc(sem["bias_masked"], 1)

            def a_rstd(u, k):
                if seen(u - 1):
                    pool.wait_ge(sem["a_normed"], lone(pool, "a_normed", u - 1, k + 1))
                rstd(u, a_mv[:, k], a_rs[:, k], "a_stats", "a_rstd", k)

            def a_keep(u):
                pool.wait_ge(sem["x1_ready"], lone(pool, "x1_ready", u, 1))
                if seen(u - 1):
                    pool.wait_ge(sem["x2_ready"], lone(pool, "x2_ready", u - 1, 1))
                pool.tensor_copy(a_res[:], x1[:]).then_inc(sem["a_kept"], 1)

            def a_length(u, which):
                pool.wait_ge(sem["a_sumsq"], lone(pool, "a_sumsq", u, which + 1))
                if seen(u - 1):
                    pool.wait_ge(sem["a_unit"], lone(pool, "a_unit", u - 1, which + 1))
                ln = a_len[:, which, :]
                ts(ln, ln, 1e-24, None, ALU.max).then_inc(sem["a_len"], 1)
                pool.wait_ge(sem["a_len"], lone(pool, "a_len", u, 2 * which + 1))
                tt(ln, ln, half[:, 0:AH], ALU.pow).then_inc(sem["a_len"], 1)

            def f_keep(u):
                pool.wait_ge(sem["x2_ready"], lone(pool, "x2_ready", u, 1))
                if seen(u - 1):
                    pool.wait_ge(sem["out_ready"], lone(pool, "out_ready", u - 1, 1))
                pool.tensor_copy(f_res[:], x2[:]).then_inc(sem["f_kept"], 1)

            def f_rstd(u):
                if seen(u - 1):
                    pool.wait_ge(sem["f_normed"], lone(pool, "f_normed", u - 1, 1))
                rstd(u, f_mv, f_rs, "f_stats", "f_rstd", 0)

            setup()
            x_rstd(0)
            x_mask(0)
            x_bias(0, 0)
            x_bias(0, 1)

            def step(i, do_x, do_a, do_f):
                ua, uf = i - 1, i - 2
                ahead = do_x and not (isinstance(i, int) and i + 1 >= UNITS)
                for s in SLOTS:
                    if do_f:
                        for n in due("pool_f_rstd", s):
                            f_rstd(uf)
                    if do_a:
                        for n in due("pool_a_rstd", s):
                            a_rstd(ua, n)
                        for n in due("pool_a_length", s):
                            a_length(ua, n)
                    if do_x:
                        for n in due("pool_x_keep", s):
                            x_keep(i)
                    if do_a:
                        for n in due("pool_a_keep", s):
                            a_keep(ua)
                    if do_f:
                        for n in due("pool_f_keep", s):
                            f_keep(uf)
                    if do_x:
                        for n in due("pool_x_bias_second", s):
                            x_bias(i, 2 + n)
                    if ahead:
                        for n in due("pool_x_rstd", s):
                            x_rstd(i + 1)
                        for n in due("pool_x_mask", s):
                            x_mask(i + 1)
                        for n in due("pool_x_bias_first", s):
                            x_bias(i + 1, n)

            steps(pool, step)


def kernel(**inputs):
    import concourse.bacc as bacc
    from concourse.bass_utils import run_bass_kernel_spmd

    a = {k: np.asarray(val) for k, val in inputs.items()}

    def t(name):
        return a[name].T

    null = a["L0_attn_null_kv"].reshape(AH, NNULL, 2, AD)
    arrays = dict(
        x=a["x"].reshape(B * TQ, D),
        ctxT=a["ctx_1024"].reshape(UNITS, BU, TK, KD, P).transpose(0, 4, 3, 1, 2).reshape(UNITS * P, KD * BU * TK),
        mask=a["mask_Bx1x1xS2_bk0"].reshape(UNITS, BU * TK).view(np.int32),
        wqT=t("L0_xattn_Wq"), wkT=t("L0_xattn_Wk"), wvT=t("L0_xattn_Wv"), woT=t("L0_xattn_Wo"),
        relT=t("L0_xattn_rel_bias"),
        a_g=a["L0_attn_norm_g"].reshape(KD, P).T, a_b=a["L0_attn_norm_b"].reshape(KD, P).T,
        a_wq=a["L0_attn_Wq"], a_wkv=a["L0_attn_Wkv"], a_wo=a["L0_attn_Wout"],
        a_qs=a["L0_attn_q_scale"].reshape(AD, 1), a_ks=a["L0_attn_k_scale"].reshape(AD, 1),
        null_k=null[:, :, 0, :].reshape(AH * NNULL, AD),
        null_v=null[:, :, 1, :].transpose(1, 0, 2).reshape(NNULL, INNER),
        f_wiT=t("L0_ffn_wi"), f_woT=t("L0_ffn_wo"),
        f_bi=a["L0_ffn_bi"].reshape(FC, P).T, f_bo=a["L0_ffn_bo"], f_gb=a["L0_ffn_gate_b"],
        f_zwT=np.concatenate([a["L0_ffn_lora_A"].reshape(E * R, D), a["L0_ffn_gate_w"]], axis=0).T,
        f_loraB=a["L0_ffn_lora_B"].transpose(0, 2, 1).reshape(E * R, FF),
        **constants(),
    )
    arrays = {k: np.ascontiguousarray(val) for k, val in arrays.items()}
    nc = bacc.Bacc("TRN2", target_bir_lowering=False, num_devices=1)
    io = {k: nc.dram_tensor("in_" + k, val.shape, mybir.dt.from_np(val.dtype), kind="ExternalInput").ap()
          for k, val in arrays.items()}
    out = nc.dram_tensor("out", [B * TQ, D], F32, kind="ExternalOutput").ap()
    build(nc, io, out)
    result = run_bass_kernel_spmd(nc, [{"in_" + k: val for k, val in arrays.items()}], core_ids=[0])
    return result.results[0]["out"].reshape(B, TQ, D)
```

```python
from contextlib import ExitStack

import numpy as np

import concourse.bass as bass
from concourse import mybir

F32, F16 = mybir.dt.float32, mybir.dt.float16
I32, U8 = mybir.dt.int32, mybir.dt.uint8
ALU = mybir.AluOpType
ACT = mybir.ActivationFunctionType
AX = mybir.AxisListType.X

P = 128
B, TQ, TK, D = 64, 64, 256, 256
BU = P // TQ
UNITS = B // BU
KD = D // P
XH, XD = 16, D // 16
XPAIRS = XH // 2
XTILES = BU * XPAIRS
NBUCKET, DIAGS = 32, TQ + TK
AH, AD, NNULL = 16, 64, 2
INNER = AH * AD
AK = TQ + NNULL
APAIRS = AH // 2
FF, E, R = 1024, 8, 16
FC = FF // P
BIAS_ROWS = 36
EPS = 1e-5
MASKED = float(2.0 ** 100)
BIG = 3.0e38
UP, DOWN = 2.0 ** 8, 2.0 ** -8
TURN_LAG = 3
PV_LAG = 2
S_BUFS, PT_BUFS = TURN_LAG + 1, PV_LAG + 1

SLOTS = range(-14, 2 * (XTILES + TURN_LAG + PV_LAG))
SLOT = dict(
    pe_x_k=(-14, -14), pe_x_out=(-14,), pe_x_v=(-14, -6), pe_x_turn=(-14,), pe_a_out=(-10,), pe_x_q=(-7,),
    pe_f_turn=(-1,), pe_f_z=(2,), pe_a_turn=(-8, -6), pe_a_k=(-3, -1), pe_a_q=(3, 3), pe_a_v=(3, 6),
    pe_a_turn_k=(10, 11), pe_a_turn_q=(13, 14), pe_a_scores=(17, 17, 18, 18),
    pe_a_turn_probs=(25, 25, 25, 25), pe_a_pv=(27, 33), pe_f_turn_z=(7,), pe_f_first=(9, 21),
    pe_f_second=(15, 24), pe_f_y=(41,),
    act_x_copy_k=(-14, -14), act_x_copy_turned=(-13,), act_x_spread_q=(-10,), act_x_copy_v=(-3, 6),
    act_f_copy_turned=(-9,), act_a_copy_turned=(-13, -10), act_a_copy_k=(-7, -7), act_a_copy_q=(-1, -1),
    act_a_copy_v=(5, 7), act_a_spread=(12, 12), act_a_exp=(17, 21), act_a_copy_probs=(22, 22, 22, 22),
    act_a_copy_pv=(38, 38), act_f_exp=(-3,), act_f_copy_z=(4,), act_f_relu=(8, 19), act_f_split_hid=(21, 28),
    act_x_split_ctx=(17,),
    dve_x_residual=(-12,), dve_x_split_turned=(-9,), dve_a_residual=(-9,), dve_x_split_k=(-13, -3),
    dve_x_spread_q=(-5,), dve_f_stats=(-7,), dve_a_stats=(-11, -10), dve_f_norm=(-6,), dve_a_norm=(-11, -8),
    dve_f_split_turned=(-3,), dve_a_split_turned=(-8, 0), dve_a_lengths=(2, 4), dve_a_unit=(8, 10),
    dve_a_place_keys=(10, 12), dve_a_bias=(17, 17, 18, 20), dve_a_softmax_top=(17, 21),
    dve_a_softmax_end=(21, 21), dve_a_split_pv=(38, 41), dve_f_logits=(2,), dve_f_route=(3,),
    dve_f_split_z=(6,), dve_f_second=(15, 21), dve_f_split_hid=(27, 36), dve_f_final=(41,), dve_x_stats=(-7,),
    dve_x_norm=(33,),
    pool_f_rstd=(6,), pool_a_rstd=(-1, 0), pool_a_length=(22, 29), pool_x_keep=(-5,), pool_a_keep=(16,),
    pool_f_keep=(1,), pool_x_bias_second=(6, 6), pool_x_bias_first=(31, 39), pool_x_rstd=(35,),
    pool_x_mask=(16,), pool_x_split_ctx=(40,),
)

PER_UNIT = dict(
    x_loaded=16, ctx_loaded=16, mask_loaded=16, out_stored=16,
    x_stats=2, x_rstd=2, x_normed=1, x_kept=1, x_turned=1, x_turned_copied=2, ctx_split=2, q_done=1,
    q_hi=1, q_spread=1, k_done=2, k_hi=2, k_copied=2, v_done=2, v_copied=2, mask_scaled=1, bias_masked=4,
    scores_done=XTILES, biased=XTILES, exp_done=XTILES, recip_done=XTILES, probs_ready=XTILES,
    probs_turned=XTILES, probs_copied=XTILES, pv_done=XTILES, merge_a=1, merge_b=2, merged=2, xo_done=1,
    x1_ready=1,
    a_kept=1, a_stats=4, a_rstd=4, a_normed=2, a_turned=2, a_turned_copied=1, ax_split=2, an_split=2, aq_done=2, ak_done=2,
    av_done=2, aq_copied=2, ak_copied=2, av_copied=4, a_squared=4, a_sumsq=2, a_len=4, a_unit=2,
    aq_turned=2, aq_spread=2, ak_turned=2, ak_placed=2, as_done=4, as_biased=4, a_soft=10,
    a_exp=2, ap_turned=4, ap_copied=4, apv_done=2, apv_hi=2, apv_copied=2, ao_done=1, x2_ready=1,
    f_kept=1, f_stats=2, f_rstd=2, f_normed=1, f_turned=1, f_turned_copied=2, z_done=1,
    z_copied=1, f_exp=1, route=9, z_routed=3, z_turned=1, z_turned_copied=2,
    hid_first=2, relu_done=2, hid_second=2, hid_ready=2, hid_hi=2, hid_split=2, y_done=1, y_sum=1, out_ready=1,
)
ONCE = ("consts", "rel_loaded", "first_consts", "table_stored", "table_loaded", "set_pe", "set_act", "set_dve", "set_pool",
        "half", "staged0", "staged1", "split_hi", "split_lo")


def constants():
    r = np.arange(DIAGS) - (TQ - 1)
    far = 8 + sum((np.abs(r) >= t).astype(np.int64) for t in (12, 16, 23, 32, 46, 64, 91))
    bucket = (r > 0) * 16 + np.where(np.abs(r) < 8, np.abs(r), far)
    onehot = (bucket[None, :] == np.arange(NBUCKET)[:, None]).astype(np.float32)
    start = 2.0 ** (-2.0 ** (-(np.log2(AH) - 3)))
    slopes = np.array([start * start ** i for i in range(AH)], dtype=np.float32)
    q = np.arange(TQ)[:, None]
    col = np.concatenate([NNULL + np.arange(TQ), np.arange(NNULL)])[None, :]
    dist = -np.abs(col - (q + NNULL)).astype(np.float32)
    alibi = slopes[None, :, None] * dist[:, None, :]
    alibi = np.where((col > q + NNULL)[:, None, :], np.float32(-MASKED), alibi)
    alibi = np.tile(alibi, (BU, 1, 1)).astype(np.float32)
    row = np.arange(P)
    parity = (row[:, None] // XD % 2 == np.arange(2)[None, :]).astype(np.float32)
    parity_down = parity * np.float32(DOWN)
    lower = np.tile((np.arange(E)[None, :] < np.arange(E)[:, None]).astype(np.float32)[None],
                    (P, 1, 1))
    chunk = np.zeros((BIAS_ROWS, 4, P), dtype=np.float16)
    for j in range(4):
        chunk[[j, 32 + j], j, :] = 1
    return dict(c_chunk=chunk, c_ident=np.eye(P, dtype=np.float32), c_onehot=onehot, c_alibi=alibi,
                c_parity_down=parity_down, c_parity=parity, c_lower=lower)


def build(nc, io, out):
    with ExitStack() as ctx:
        def sb(name, shape, dt=F32):
            return ctx.enter_context(nc.sbuf_tensor(name, shape, dt))

        def bank(name):
            return ctx.enter_context(nc.psum_tensor(name, [P, 512], F32))

        sem = {n: ctx.enter_context(nc.semaphore(n)) for n in (*PER_UNIT, *ONCE)}

        def at(name, u, k):
            return u * PER_UNIT[name] + k

        def seen(u):
            return not isinstance(u, int) or u >= 0

        def lone(eng, name, u, k):
            value = at(name, u, k)
            if not isinstance(value, int):
                value = eng.to_reg(value)
                eng.wait_ge(sem["consts"], 16)
            return value

        def split(name, shape):
            return sb(name, [shape[0], 2, *shape[1:]], F16)

        wq, wk, wv, wo = (split(n, [P, KD, D]) for n in ("wq", "wk", "wv", "wo"))
        a_wq, a_wk, a_wv = (split(n, [P, KD, INNER]) for n in ("a_wq", "a_wk", "a_wv"))
        a_wo = split("a_wo", [P, APAIRS, D])
        f_wi, f_wo = split("f_wi", [P, KD, FF]), split("f_wo", [P, FC, D])
        f_loraB, f_zw = split("f_loraB", [P, FF]), split("f_zw", [P, KD, P + E])
        f_bi, f_bis = sb("f_bi", [BIAS_ROWS, 2 * P]), sb("f_bis", [BIAS_ROWS, 2 * P], F16)
        f_chunk = sb("f_chunk", [BIAS_ROWS, 4, P], F16)
        f_bo2, f_gb = sb("f_bo2", [P, D]), sb("f_gb", [P, E])
        ident, alibi = sb("ident", [P, P]), sb("alibi", [P, AH, AK])
        parity_down, parity = sb("parity_down", [P, 2]), sb("parity", [P, 2])
        lower = sb("lower", [P, E, E])
        a_g, a_b, a_qs, a_ks = sb("a_g", [P, KD]), sb("a_b", [P, KD]), sb("a_qs", [P, 1]), sb("a_ks", [P, 1])
        relT, onehot = sb("relT", [NBUCKET, XH]), sb("onehot", [NBUCKET, DIAGS])
        reltab = sb("reltab", [XH, DIAGS])
        bias = sb("bias", [P, XPAIRS, TK])
        nulls = sb("nulls", [AH * NNULL, AD])
        null_sq = sb("null_sq", [AH * NNULL, AD])
        null_len, half = sb("null_len", [AH * NNULL, 2]), sb("half", [P, 2 * AH])
        x_ld, x_res, x_n = sb("x_ld", [P, D]), sb("x_res", [P, D]), sb("x_n", [P, D])
        ctxT, mask32, negm = sb("ctxT", [P, KD, BU, TK]), sb("mask32", [P, BU * TK // 4], I32), sb("negm", [P, BU, TK])
        x_st, x_mv, x_rs = sb("x_st", [P, 6]), sb("x_mv", [P, 2]), sb("x_rs", [P, 2])
        ctxS, xnT = split("ctxS", [P, KD, BU * TK]), split("xnT", [P, KD, P])
        qT = split("qT", [P, KD, BU, 2, TQ])
        kT, v = split("kT", [P, KD, BU, TK]), sb("v", [P, BU * 2, D])
        bm = sb("bm", [P, BU, XPAIRS, TK])
        S = sb("S", [P, S_BUFS, TK])
        x_nmx, x_sum, x_inv = sb("x_nmx", [P, XTILES]), sb("x_sum", [P, XTILES]), sb("x_inv", [P, XTILES])
        pT = sb("pT", [P, PT_BUFS, 2, P])
        o_half, o_sum = sb("o_half", [P, KD, BU, TQ]), sb("o_sum", [P, KD, BU, TQ])
        oT = split("oT", [P, KD, BU, TQ])
        x1 = sb("x1", [P, D])
        a_res, a_x, a_n = sb("a_res", [P, D]), sb("a_x", [P, D]), sb("a_n", [P, D])
        a_st, a_mv, a_rs = sb("a_st", [P, 2, 6]), sb("a_mv", [P, 2, 2]), sb("a_rs", [P, 2, 2])
        aT = split("aT", [P, KD, P])
        a_nT, anT = sb("a_nT", [P, KD, P]), split("anT", [P, KD, P])
        a_raw = sb("a_raw", [P, 2, AH, AD])
        a_work = sb("a_work", [P, 2 * INNER])
        a_sq = a_work[:].rearrange("p (n h d) -> p n h d", n=2, h=AH)
        stage = (a_raw[:].rearrange("p n h d -> p (n h d)"), a_work)
        a_len = sb("a_len", [P, 2, AH])
        a_qk = sb("a_qk", [P, 1])
        qz = sb("qz", [P, AH, P])
        akT = sb("akT", [P, APAIRS, BU, AK])
        av = sb("av", [AK, BU, INNER])
        aS = sb("aS", [P, AH, AK])
        a_mx, a_sum = sb("a_mx", [P, AH]), sb("a_sum", [P, AH])
        apT, aoT = a_work[0:AK, :].rearrange("p (h t) -> p h t", h=AH), split("aoT", [P, APAIRS, P])
        x2 = sb("x2", [P, D])
        f_res, f_n, f_out = (sb(n, [P, D]) for n in ("f_res", "f_n", "f_out"))
        f_st, f_mv, f_rs = sb("f_st", [P, 6]), sb("f_mv", [P, 2]), sb("f_rs", [P, 2])
        fT = split("fT", [P, KD, P])
        z = sb("z", [P, P + E])
        g_e, g_s, g_gt, g_eq = sb("g_e", [P, E]), sb("g_s", [P, E]), sb("g_gt", [P, E, E]), sb("g_eq", [P, E, E])
        g_rank, g_sel, g_1 = sb("g_rank", [P, E]), sb("g_sel", [P, 3, E]), sb("g_1", [P, 4])
        g_top = sb("g_top", [P, E])
        zr, zT = sb("zr", [P, 3, E, R]), split("zT", [P, 2, P])
        f_h = sb("f_h", [P, FC, P])
        hT = split("hT", [P, FC, P])

        ps_s = [bank("ps_s0"), bank("ps_s1")]
        ps_t = [bank("ps_t0"), bank("ps_t1")]
        ps_o = bank("ps_o")
        ps_a = [bank("ps_a0"), bank("ps_a1")]
        ps_f = bank("ps_f")

        table = nc.dram_tensor("table", [XH, TQ, DIAGS], F32)
        table_ap = table.ap()

        block = ctx.enter_context(nc.Block())

        def tiles4(ap):
            return ap.rearrange("p (n c) -> p n c", n=4)

        def due(name, s):
            return [n for n, slot in enumerate(SLOT[name]) if slot == s]

        def last_user(t, bufs):
            return XTILES - 1 - (XTILES - 1 - t) % bufs

        def steps(eng, step):
            for i in range(3):
                step(i, True, i >= 1, i >= 2)
            with eng.Fori(3, UNITS - 1) as i:
                step(i, True, True, True)
            for i in range(UNITS - 1, UNITS + 2):
                step(i, i < UNITS, i - 1 < UNITS, True)

        N_CONST = 16

        pieces = [("wkT", 0, D, wk), ("wvT", 0, D, wv), ("wqT", 0, D, wq), ("woT", 0, D, wo),
                  ("a_wq", 0, INNER, a_wq), ("a_wkv", 0, INNER, a_wk), ("a_wkv", INNER, INNER, a_wv),
                  ("a_wo", 0, D, a_wo), ("f_zwT", 0, P + E, f_zw), ("f_wiT", 0, FF, f_wi),
                  ("f_loraB", 0, FF, f_loraB), ("f_woT", 0, D, f_wo)]
        X_PIECES, A_PIECES = 4, 8

        def staged(n):
            dst = pieces[n][3]
            hi, lo = ((dst[:, k].rearrange("p c n -> p (c n)") if len(dst.shape) == 4 else dst[:, k])
                      for k in range(2))
            return stage[n % 2][:, 0:hi.shape[1]], hi, lo

        @block.sync
        def _(sp):
            def load(u):
                if seen(u - 1):
                    sp.wait_ge(sem["x_normed"], lone(sp, "x_normed", u - 1, 1))
                if seen(u - 1):
                    sp.wait_ge(sem["x_kept"], lone(sp, "x_kept", u - 1, 1))
                sp.dma_start(x_ld[:], io["x"][bass.ts(u, P), :]).then_inc(sem["x_loaded"], 16)
                if seen(u - 1):
                    sp.wait_ge(sem["mask_scaled"], lone(sp, "mask_scaled", u - 1, 1))
                sp.dma_start(mask32[:], io["mask"][bass.ts(u, 1), :].broadcast_to([P, BU * TK // 4])).then_inc(sem["mask_loaded"], 16)
                if seen(u - 1):
                    sp.wait_ge(sem["ctx_split"], lone(sp, "ctx_split", u - 1, 2))
                if seen(u - 1):
                    sp.wait_ge(sem["v_done"], lone(sp, "v_done", u - 1, 2))
                sp.dma_start(ctxT[:].rearrange("p c b k -> p (c b k)"),
                             io["ctxT"][bass.ts(u, P), :]).then_inc(sem["ctx_loaded"], 16)

            def const(dst, src):
                sp.dma_start(dst, src).then_inc(sem["consts"], 16)
                const.n += 1
            const.n = 0

            def piece(n):
                if n >= 2:
                    sp.wait_ge(sem["split_lo"], n - 1)
                name, first, cols, _ = pieces[n]
                src = io[name][:, first:first + cols].rearrange("(c p) n -> p c n", p=P)
                to = staged(n)[0].rearrange("p (c n) -> p c n", n=cols)
                sp.dma_start(to, src).then_inc(sem["staged1" if n % 2 else "staged0"], 16)

            sp.dma_start(relT[:], io["relT"]).then_inc(sem["rel_loaded"], 16)
            sp.dma_start(onehot[:], io["c_onehot"]).then_inc(sem["rel_loaded"], 16)
            load(0)
            piece(0)
            piece(1)
            sp.dma_start(ident[:], io["c_ident"]).then_inc(sem["first_consts"], 16)
            sp.dma_start(parity_down[:], io["c_parity_down"]).then_inc(sem["first_consts"], 16)
            sp.dma_start(parity[:], io["c_parity"]).then_inc(sem["first_consts"], 16)
            sp.wait_ge(sem["set_dve"], 1)
            sp.dma_start(table_ap, reltab[:].unsqueeze(1).broadcast_to([XH, TQ, DIAGS]))\
                .then_inc(sem["table_stored"], 16)
            for n in range(2, X_PIECES):
                piece(n)
            sp.wait_ge(sem["table_stored"], 16)
            for h2 in range(2):
                src = bass.AP(table_ap.tensor, h2 * TQ * DIAGS + TQ - 1,
                              [[DIAGS - 1, TQ], [2 * TQ * DIAGS, XPAIRS], [1, TK]])
                sp.dma_start(bias[h2 * TQ:(h2 + 1) * TQ, :, :], src).then_inc(sem["table_loaded"], 16)
            const(nulls[:], io["null_k"])
            const(av[TQ:AK, 0, :], io["null_v"])
            const(av[TQ:AK, 1, :], io["null_v"])
            sp.wait_ge(sem["half"], 2)
            const(f_bi[0:4, :], io["f_bi"])
            const(f_bi[32:BIAS_ROWS, :], io["f_bi"])
            const(f_chunk[:], io["c_chunk"])
            const(f_bo2[:], io["f_bo"].partition_broadcast(P))
            const(f_gb[:], io["f_gb"].partition_broadcast(P))
            const(lower[:], io["c_lower"])
            const(a_g[:], io["a_g"])
            const(a_b[:], io["a_b"])
            for h2 in range(2):
                const(a_qs[h2 * AD:(h2 + 1) * AD, :], io["a_qs"])
                const(a_ks[h2 * AD:(h2 + 1) * AD, :], io["a_ks"])
            const(alibi[:], io["c_alibi"])
            assert const.n == N_CONST

            def step(i, do_x, do_a, do_f):
                if do_x and not (isinstance(i, int) and i + 1 >= UNITS):
                    load(i + 1)
                if isinstance(i, int) and i == 0:
                    for n in range(X_PIECES, len(pieces)):
                        piece(n)
                if do_f:
                    u = i - 2
                    sp.wait_ge(sem["out_ready"], lone(sp, "out_ready", u, 1))
                    sp.dma_start(out[bass.ts(u, P), :], f_out[:]).then_inc(sem["out_stored"], 16)

            steps(sp, step)
            sp.wait_ge(sem["out_stored"], 16 * UNITS)

        ALL_CONST = 16 * N_CONST

        @block.tensor
        def _(pe):
            mm, turn = nc.tensor.matmul, nc.tensor.transpose

            def mm3(to, left, right, start, stop, **flags):
                mm(to, left(0), right(0), start=start, stop=False, **flags)
                mm(to, left(0), right(1), start=False, stop=False, **flags)
                return mm(to, left(1), right(0), start=False, stop=stop, **flags)

            def setup_table():
                pe.wait_ge(sem["rel_loaded"], 32)
                mm(ps_s[0][0:XH, 0:DIAGS], relT[:], onehot[:], start=True, stop=True)\
                    .then_inc(sem["set_pe"], 1)
                pe.wait_ge(sem["set_dve"], 1)

            def setup_nulls():
                pe.wait_ge(sem["consts"], ALL_CONST)
                pe.wait_ge(sem["set_pool"], 3)
                turn(ps_a[0][0:AD, 0:AH * NNULL], nulls[:], ident[0:32, 0:32])\
                    .then_inc(sem["set_pe"], 1)
                pe.wait_ge(sem["set_act"], 1)

            def x_k(u, g):
                if isinstance(u, int) and u == 0:
                    pe.wait_ge(sem["split_lo"], 1)
                if g == 0:
                    pe.wait_ge(sem["ctx_split"], at("ctx_split", u, 2))
                if seen(u - 1):
                    pe.wait_ge(sem["biased"], at("biased", u - 1, XTILES - 1 + g))
                for c in range(KD):
                    last = mm3(ps_s[g][:], lambda k: wk[:, k, c, g * P:(g + 1) * P],
                               lambda k: ctxS[:, k, c, :], c == 0, c == KD - 1)
                last.then_inc(sem["k_done"], 1)

            def x_v(u, n):
                if isinstance(u, int) and u == 0:
                    pe.wait_ge(sem["split_lo"], 2)
                if seen(u - 1):
                    pe.wait_ge(sem["probs_copied"], at("probs_copied", u - 1, XTILES - 1 + n))
                for j in range(2):
                    t = 2 * n + j
                    for c in range(KD):
                        last = mm3(ps_t[n][:, j * D:(j + 1) * D],
                                   lambda k: ctxS[:, k, c, t * P:(t + 1) * P],
                                   lambda k: wv[:, k, c, :], c == 0, c == KD - 1)
                last.then_inc(sem["v_done"], 1)

            def x_turn(u):
                pe.wait_ge(sem["x_normed"], at("x_normed", u, 1))
                if seen(u - 1):
                    pe.wait_ge(sem["x1_ready"], at("x1_ready", u - 1, 1))
                for c in range(KD):
                    last = turn(ps_o[:, c * P:(c + 1) * P], x_n[:, c * P:(c + 1) * P], ident[:])
                last.then_inc(sem["x_turned"], 1)

            def x_q(u):
                if isinstance(u, int) and u == 0:
                    pe.wait_ge(sem["split_lo"], 3)
                pe.wait_ge(sem["x_turned_copied"], at("x_turned_copied", u, 2))
                for g in range(KD):
                    for c in range(KD):
                        last = mm3(ps_o[:, 256 + g * P:256 + (g + 1) * P],
                                   lambda k: wq[:, k, c, g * P:(g + 1) * P], lambda k: xnT[:, k, c, :],
                                   c == 0, c == KD - 1)
                last.then_inc(sem["q_done"], 1)

            def x_scores(u, t):
                b, pair = t // XPAIRS, t % XPAIRS
                g, p4 = pair // 4, pair % 4
                if t == 0:
                    pe.wait_ge(sem["q_spread"], at("q_spread", u, 1))
                    pe.wait_ge(sem["k_copied"], at("k_copied", u, 2))
                elif t >= 2:
                    pe.wait_ge(sem["biased"], at("biased", u, t - 1))
                rows = slice(32 * p4, 32 * p4 + 32)
                mm3(ps_s[t % 2][:, 0:TK], lambda k: qT[rows, k, g, b].rearrange("p h q -> p (h q)"),
                    lambda k: kT[rows, k, g, b, :], True, True).then_inc(sem["scores_done"], 1)

            def x_turn_probs(u, t):
                pe.wait_ge(sem["probs_ready"], at("probs_ready", u, t + 1))
                if t < 2:
                    pe.wait_ge(sem["v_copied"], at("v_copied", u, t + 1))
                else:
                    pe.wait_ge(sem["probs_copied"], at("probs_copied", u, t - 1))
                for c in range(2):
                    last = turn(ps_t[t % 2][:, c * P:(c + 1) * P], S[:, t % S_BUFS, c * P:(c + 1) * P], ident[:])
                last.then_inc(sem["probs_turned"], 1)

            def x_pv(u, t):
                b, pair = t // XPAIRS, t % XPAIRS
                g, p4 = pair // 4, pair % 4
                pe.wait_ge(sem["probs_copied"], at("probs_copied", u, t + 1))
                if t == 0:
                    pe.wait_ge(sem["v_copied"], at("v_copied", u, 2))
                o = ps_o[32 * p4:32 * p4 + 32, (g * BU + b) * P:(g * BU + b + 1) * P]
                for c in range(2):
                    last = mm(o, v[:, 2 * b + c, pair * 32:(pair + 1) * 32], pT[:, t % PT_BUFS, c, :],
                              start=(c == 0), stop=(c == 1))
                last.then_inc(sem["pv_done"], 1)

            def x_out(u):
                pe.wait_ge(sem["merged"], at("merged", u, 2))
                for g in range(KD):
                    last = mm3(ps_o[:, 0:D], lambda k: oT[:, k, g].rearrange("p b q -> p (b q)"),
                               lambda k: wo[:, k, g, :], g == 0, g == KD - 1)
                last.then_inc(sem["xo_done"], 1)

            def a_turn(u, n):
                pe.wait_ge(sem["a_normed"], at("a_normed", u, n + 1))
                if n == 0:
                    if seen(u - 1):
                        pe.wait_ge(sem["apv_copied"], at("apv_copied", u - 1, 2))
                else:
                    pe.wait_ge(sem["ax_split"], at("ax_split", u, 2))
                src = (a_x, a_n)[n]
                for c in range(KD):
                    last = turn(ps_a[0][:, (n * KD + c) * P:(n * KD + c + 1) * P],
                                src[:, c * P:(c + 1) * P], ident[:])
                last.then_inc(sem["a_turned"], 1)

            def a_k(u, n):
                if n == 0:
                    pe.wait_ge(sem["ax_split"], at("ax_split", u, 2))
                    if seen(u - 1):
                        pe.wait_ge(sem["x2_ready"], at("x2_ready", u - 1, 1))
                else:
                    pe.wait_ge(sem["a_turned_copied"], at("a_turned_copied", u, 1))
                for c in range(KD):
                    last = mm3(ps_a[1 - n][:], lambda k: aT[:, k, c, :],
                               lambda k: a_wk[:, k, c, n * 512:(n + 1) * 512], c == 0, c == KD - 1)
                last.then_inc(sem["ak_done"], 1)

            def a_q(u, n):
                pe.wait_ge(sem["a_squared"], at("a_squared", u, n + 1))
                if n == 0:
                    pe.wait_ge(sem["an_split"], at("an_split", u, 2))
                for c in range(KD):
                    last = mm3(ps_a[1 - n][:], lambda k: anT[:, k, c, :],
                               lambda k: a_wq[:, k, c, n * 512:(n + 1) * 512], c == 0, c == KD - 1)
                last.then_inc(sem["aq_done"], 1)

            def a_v(u, n):
                pe.wait_ge(sem["a_squared"], at("a_squared", u, n + 3))
                for c in range(KD):
                    last = mm3(ps_a[1 - n][:], lambda k: aT[:, k, c, :],
                               lambda k: a_wv[:, k, c, n * 512:(n + 1) * 512], c == 0, c == KD - 1)
                last.then_inc(sem["av_done"], 1)

            def a_turn_kq(u, which, n):
                if n == 0:
                    pe.wait_ge(sem["a_unit"], at("a_unit", u, which + 1))
                if which == 0:
                    pe.wait_ge(sem["av_copied"], at("av_copied", u, 2 * n + 2))
                else:
                    pe.wait_ge(sem["ak_placed"], at("ak_placed", u, n + 1))
                for j in range(4):
                    pair = 4 * n + j
                    last = turn(ps_a[1 - n][:, j * P:(j + 1) * P],
                                a_raw[:, which, 2 * pair:2 * pair + 2, :].rearrange("p h d -> p (h d)"),
                                ident[:])
                last.then_inc(sem["aq_turned" if which else "ak_turned"], 1)

            def a_scores(u, n):
                if n < 2:
                    pe.wait_ge(sem["aq_spread"], at("aq_spread", u, 2))
                else:
                    pe.wait_ge(sem["as_biased"], at("as_biased", u, n - 1))
                for j in range(4):
                    h = 4 * n + j
                    for b in range(BU):
                        last = mm(ps_a[(n + 1) % 2][b * TQ:(b + 1) * TQ, j * AK:(j + 1) * AK],
                                  qz[:, h, b * TQ:(b + 1) * TQ], akT[:, h // 2, b, :],
                                  start=True, stop=True)
                last.then_inc(sem["as_done"], 1)

            def a_turn_probs(u, n):
                pe.wait_ge(sem["a_soft"], at("a_soft", u, 10 if n >= 2 else 7))
                if n >= 2:
                    pe.wait_ge(sem["ap_copied"], at("ap_copied", u, n - 1))
                for j in range(4):
                    last = turn(ps_a[(n + 1) % 2][0:AK, j * P:(j + 1) * P], aS[:, 4 * n + j, :], ident[:])
                last.then_inc(sem["ap_turned"], 1)

            def a_pv(u, n):
                pe.wait_ge(sem["ap_copied"], at("ap_copied", u, 4))
                for j in range(8):
                    h = 8 * n + j
                    for b in range(BU):
                        last = mm(ps_a[1 - n][(h % 2) * AD:(h % 2 + 1) * AD,
                                              (j // 2) * P + b * TQ:(j // 2) * P + (b + 1) * TQ],
                                  av[:, b, h * AD:(h + 1) * AD], apT[:, h, b * TQ:(b + 1) * TQ],
                                  start=True, stop=True)
                last.then_inc(sem["apv_done"], 1)

            def a_out(u):
                pe.wait_ge(sem["apv_copied"], at("apv_copied", u, 2))
                for c in range(APAIRS):
                    last = mm3(ps_a[1][:, 0:D], lambda k: aoT[:, k, c, :], lambda k: a_wo[:, k, c, :],
                               c == 0, c == APAIRS - 1)
                last.then_inc(sem["ao_done"], 1)

            def f_turn(u):
                pe.wait_ge(sem["f_normed"], at("f_normed", u, 1))
                if seen(u - 1):
                    pe.wait_ge(sem["y_sum"], at("y_sum", u - 1, 1))
                for c in range(KD):
                    last = turn(ps_f[:, c * P:(c + 1) * P], f_n[:, c * P:(c + 1) * P], ident[:])
                last.then_inc(sem["f_turned"], 1)

            def f_z(u):
                pe.wait_ge(sem["f_turned_copied"], at("f_turned_copied", u, 2))
                for c in range(KD):
                    last = mm3(ps_f[:, 0:P + E], lambda k: fT[:, k, c, :], lambda k: f_zw[:, k, c, :],
                               c == 0, c == KD - 1)
                last.then_inc(sem["z_done"], 1)

            def f_turn_z(u):
                pe.wait_ge(sem["z_routed"], at("z_routed", u, 3))
                pe.wait_ge(sem["z_copied"], at("z_copied", u, 1))
                for n, m in enumerate((0, 2)):
                    last = turn(ps_f[:, n * P:(n + 1) * P], zr[:, m].rearrange("p e r -> p (e r)"), ident[:])
                last.then_inc(sem["z_turned"], 1)

            def f_first(u, n):
                if n == 0:
                    pe.wait_ge(sem["z_turned_copied"], at("z_turned_copied", u, 2))
                else:
                    pe.wait_ge(sem["hid_ready"], at("hid_ready", u, 1))
                mm(ps_f[:], f_bis[:, n * P:(n + 1) * P], f_chunk[:].rearrange("k j t -> k (j t)"),
                   start=True, stop=False, skip_group_check=True)
                for j in range(4):
                    f = (4 * n + j) * P
                    for c in range(KD):
                        mm3(ps_f[:, j * P:(j + 1) * P], lambda k: f_wi[:, k, c, f:f + P],
                            lambda k: fT[:, k, c, :], False, False, skip_group_check=True)
                    last = mm3(ps_f[:, j * P:(j + 1) * P], lambda k: f_loraB[:, k, f:f + P],
                               lambda k: zT[:, k, 0, :], False, False, skip_group_check=True)
                last.then_inc(sem["hid_first"], 1)

            def f_second(u, n):
                pe.wait_ge(sem["relu_done"], at("relu_done", u, n + 1))
                for j in range(4):
                    f = (4 * n + j) * P
                    last = mm3(ps_f[:, j * P:(j + 1) * P], lambda k: f_loraB[:, k, f:f + P],
                               lambda k: zT[:, k, 1, :], False, j == 3, skip_group_check=True)
                last.then_inc(sem["hid_second"], 1)

            def f_y(u):
                pe.wait_ge(sem["hid_split"], at("hid_split", u, 2))
                for c in range(FC):
                    last = mm3(ps_f[:, 0:D], lambda k: hT[:, k, c, :], lambda k: f_wo[:, k, c, :],
                               c == 0, c == FC - 1)
                last.then_inc(sem["y_done"], 1)

            setup_table()
            pe.wait_ge(sem["first_consts"], 48)

            def step(i, do_x, do_a, do_f):
                ua, uf = i - 1, i - 2
                if isinstance(i, int) and i == 1:
                    setup_nulls()
                    pe.wait_ge(sem["split_lo"], len(pieces))
                    pe.wait_ge(sem["set_dve"], 7)
                for s in SLOTS:
                    if do_x:
                        for n in due("pe_x_k", s):
                            x_k(i, n)
                    if do_a:
                        for n in due("pe_x_out", s):
                            x_out(ua)
                    if do_x:
                        for n in due("pe_x_v", s):
                            x_v(i, n)
                        for n in due("pe_x_turn", s):
                            x_turn(i)
                    if do_f:
                        for n in due("pe_a_out", s):
                            a_out(uf)
                    if do_x:
                        for n in due("pe_x_q", s):
                            x_q(i)
                    if do_f:
                        for n in due("pe_f_turn", s):
                            f_turn(uf)
                        for n in due("pe_f_z", s):
                            f_z(uf)
                        for n in due("pe_f_turn_z", s):
                            f_turn_z(uf)
                    if do_a:
                        for n in due("pe_a_turn", s):
                            a_turn(ua, n)
                        for n in due("pe_a_k", s):
                            a_k(ua, n)
                        for n in due("pe_a_q", s):
                            a_q(ua, n)
                        for n in due("pe_a_v", s):
                            a_v(ua, n)
                        for n in due("pe_a_turn_k", s):
                            a_turn_kq(ua, 0, n)
                        for n in due("pe_a_turn_q", s):
                            a_turn_kq(ua, 1, n)
                        for n in due("pe_a_scores", s):
                            a_scores(ua, n)
                        for n in due("pe_a_turn_probs", s):
                            a_turn_probs(ua, n)
                        for n in due("pe_a_pv", s):
                            a_pv(ua, n)
                    if do_f:
                        for n in due("pe_f_first", s):
                            f_first(uf, n)
                        for n in due("pe_f_second", s):
                            f_second(uf, n)
                        for n in due("pe_f_y", s):
                            f_y(uf)
                    if do_x:
                        t = s // 2
                        if s % 2 == 0 and 0 <= t < XTILES:
                            x_scores(i, t)
                        if s % 2 == 1 and 0 <= t - TURN_LAG < XTILES:
                            x_turn_probs(i, t - TURN_LAG)
                        if s % 2 == 1 and 0 <= t - TURN_LAG - PV_LAG:
                            x_pv(i, t - TURN_LAG - PV_LAG)

            steps(pe, step)

        @block.scalar
        def _(act):
            go = nc.scalar.activation

            def setup_nulls():
                act.wait_ge(sem["consts"], ALL_CONST)
                act.wait_ge(sem["set_pe"], 2)
                src = ps_a[0][0:AD, 0:AH * NNULL].rearrange("d (pair h n) -> d h pair n", h=2, n=NNULL)
                for h2 in range(2):
                    for b in range(BU):
                        last = go(akT[h2 * AD:(h2 + 1) * AD, :, b, TQ:AK], src[:, h2], ACT.Copy)
                last.then_inc(sem["set_act"], 1)

            def split_hi(n):
                act.wait_ge(sem["staged1" if n % 2 else "staged0"], 16 * (n // 2 + 1))
                src, hi, _ = staged(n)
                go(hi, src, ACT.Copy, scale=UP).then_inc(sem["split_hi"], 1)

            def x_split_ctx(u):
                act.wait_ge(sem["ctx_loaded"], at("ctx_loaded", u, 16))
                if seen(u - 1):
                    act.wait_ge(sem["v_done"], at("v_done", u - 1, 2))
                go(ctxS[:, 0].rearrange("p c n -> p (c n)"), ctxT[:].rearrange("p c b k -> p (c b k)"),
                   ACT.Copy).then_inc(sem["ctx_split"], 1)

            def x_copy_turned(u):
                act.wait_ge(sem["x_turned"], at("x_turned", u, 1))
                go(xnT[:, 0].rearrange("p c t -> p (c t)"), ps_o[:, 0:2 * P], ACT.Copy)\
                    .then_inc(sem["x_turned_copied"], 1)

            def x_copy_k(u, g):
                if g == 0:
                    if seen(u - 1):
                        act.wait_ge(sem["scores_done"], at("scores_done", u - 1, XTILES))
                act.wait_ge(sem["k_done"], at("k_done", u, g + 1))
                go(kT[:, 0, g].rearrange("p b k -> p (b k)"), ps_s[g][:], ACT.Copy, scale=DOWN)\
                    .then_inc(sem["k_hi"], 1)

            def x_spread_q(u):
                act.wait_ge(sem["q_done"], at("q_done", u, 1))
                if seen(u - 1):
                    act.wait_ge(sem["scores_done"], at("scores_done", u - 1, XTILES))
                q = ps_o[:, 256:512].rearrange("p (n q) -> p n q", q=TQ)
                for h2 in range(2):
                    last = go(qT[:, 0, :, :, h2].rearrange("p g b q -> p (g b) q"), q, ACT.Copy,
                              scale=parity_down[:, h2:h2 + 1])
                last.then_inc(sem["q_hi"], 1)

            def x_exp(u, t):
                act.wait_ge(sem["biased"], at("biased", u, t + 1))
                go(S[:, t % S_BUFS, :], S[:, t % S_BUFS, :], ACT.Exp, bias=x_nmx[:, t:t + 1], scale=-1.0,
                   accum_out=x_sum[:, t:t + 1]).then_inc(sem["exp_done"], 1)

            def x_copy_probs(u, t):
                act.wait_ge(sem["probs_turned"], at("probs_turned", u, t + 1))
                if t >= PT_BUFS:
                    act.wait_ge(sem["pv_done"], at("pv_done", u, t - PT_BUFS + 1))
                elif seen(u - 1):
                    act.wait_ge(sem["pv_done"], at("pv_done", u - 1, last_user(t, PT_BUFS) + 1))
                go(pT[:, t % PT_BUFS].rearrange("p c m -> p (c m)"), ps_t[t % 2][:, 0:2 * P], ACT.Copy)\
                    .then_inc(sem["probs_copied"], 1)

            def x_copy_v(u, n):
                if n == 0:
                    if seen(u - 1):
                        act.wait_ge(sem["pv_done"], at("pv_done", u - 1, XTILES))
                act.wait_ge(sem["v_done"], at("v_done", u, n + 1))
                go(v[:, 2 * n:2 * n + 2, :].rearrange("p t d -> p (t d)"), ps_t[n][:], ACT.Copy,
                   scale=DOWN).then_inc(sem["v_copied"], 1)

            def x_merge(u):
                act.wait_ge(sem["pv_done"], at("pv_done", u, XTILES))
                if seen(u - 1):
                    act.wait_ge(sem["merge_b"], at("merge_b", u - 1, 2))
                o = ps_o[:].rearrange("p (g b h q) -> p g b h q", g=KD, b=BU, h=2)
                go(o_half[:].rearrange("p g b q -> p (g b) q"),
                   o.rearrange("p g b h q -> p (g b) h q")[:, :, 0, :],
                   ACT.Copy, scale=parity[:, 0:1]).then_inc(sem["merge_a"], 1)
                act.wait_ge(sem["merge_b"], at("merge_b", u, 2))
                if seen(u - 1):
                    act.wait_ge(sem["xo_done"], at("xo_done", u - 1, 1))
                go(oT[:, 0].rearrange("p g b q -> p (g b q)"), o_sum[:].rearrange("p g b q -> p (g b q)"),
                   ACT.Copy).then_inc(sem["merged"], 1)

            def a_copy_turned(u, n):
                act.wait_ge(sem["a_turned"], at("a_turned", u, n + 1))
                if n == 0:
                    if seen(u - 1):
                        act.wait_ge(sem["av_done"], at("av_done", u - 1, 2))
                    go(aT[:, 0].rearrange("p c t -> p (c t)"), ps_a[0][:, 0:2 * P], ACT.Copy)\
                        .then_inc(sem["ax_split"], 1)
                else:
                    if seen(u - 1):
                        act.wait_ge(sem["aq_done"], at("aq_done", u - 1, 2))
                    for c in range(KD):
                        last = go(a_nT[:, c, :], ps_a[0][:, (2 + c) * P:(3 + c) * P], ACT.Identity,
                                  bias=a_b[:, c:c + 1], scale=a_g[:, c:c + 1])
                    last.then_inc(sem["a_turned_copied"], 1)
                    act.wait_ge(sem["a_turned_copied"], at("a_turned_copied", u, 1))
                    go(anT[:, 0].rearrange("p c t -> p (c t)"), a_nT[:].rearrange("p c t -> p (c t)"), ACT.Copy)\
                        .then_inc(sem["an_split"], 1)

            def a_copy_raw(u, which, n):
                done, copied, turned = (("ak_done", "ak_copied", "ak_turned"), ("aq_done", "aq_copied", "aq_turned"))[which]
                if n == 0:
                    if seen(u - 1):
                        act.wait_ge(sem[turned], at(turned, u - 1, 2))
                act.wait_ge(sem[done], at(done, u, n + 1))
                go(a_raw[:, which, 8 * n:8 * n + 8, :].rearrange("p h d -> p (h d)"),
                   ps_a[1 - n][:], ACT.Copy, scale=DOWN).then_inc(sem[copied], 1)
                if seen(u - 1) and n == 0:
                    act.wait_ge(sem["a_sumsq"], at("a_sumsq", u - 1, which + 1))
                go(a_sq[:, which, 8 * n:8 * n + 8, :].rearrange("p h d -> p (h d)"),
                   ps_a[1 - n][:], ACT.Square, scale=DOWN).then_inc(sem["a_squared"], 1)

            def a_copy_v(u, n):
                if n == 0:
                    if seen(u - 1):
                        act.wait_ge(sem["apv_done"], at("apv_done", u - 1, 2))
                act.wait_ge(sem["av_done"], at("av_done", u, n + 1))
                for b in range(BU):
                    go(av[0:TQ, b, n * 512:(n + 1) * 512], ps_a[1 - n][b * TQ:(b + 1) * TQ, :],
                       ACT.Copy, scale=DOWN).then_inc(sem["av_copied"], 1)

            def a_exp(u, half):
                act.wait_ge(sem["a_soft"], at("a_soft", u, 2 * half + 2))
                s = aS[:, 8 * half:8 * half + 8, :].rearrange("p h k -> p (h k)")
                go(s, s, ACT.Exp).then_inc(sem["a_exp"], 1)

            def a_copy_probs(u, n):
                act.wait_ge(sem["ap_turned"], at("ap_turned", u, n + 1))
                if n == 0:
                    if seen(u - 1):
                        act.wait_ge(sem["apv_done"], at("apv_done", u - 1, 2))
                go(apT[:, 4 * n:4 * n + 4, :].rearrange("k h t -> k (h t)"), ps_a[(n + 1) % 2][0:AK, :],
                   ACT.Copy).then_inc(sem["ap_copied"], 1)

            def a_copy_pv(u, n):
                act.wait_ge(sem["apv_done"], at("apv_done", u, n + 1))
                if seen(u - 1):
                    act.wait_ge(sem["ao_done"], at("ao_done", u - 1, 1))
                go(aoT[:, 0, 4 * n:4 * n + 4, :].rearrange("p c t -> p (c t)"), ps_a[1 - n][:], ACT.Copy)\
                    .then_inc(sem["apv_hi"], 1)

            def f_copy_turned(u):
                act.wait_ge(sem["f_turned"], at("f_turned", u, 1))
                if seen(u - 1):
                    act.wait_ge(sem["hid_first"], at("hid_first", u - 1, 2))
                go(fT[:, 0].rearrange("p c t -> p (c t)"), ps_f[:, 0:2 * P], ACT.Copy)\
                    .then_inc(sem["f_turned_copied"], 1)

            def f_exp(u):
                act.wait_ge(sem["route"], at("route", u, 2))
                go(g_e[:], g_s[:], ACT.Exp, bias=g_1[:, 0:1], accum_out=g_1[:, 1:2])\
                    .then_inc(sem["f_exp"], 1)

            def f_copy_z(u):
                act.wait_ge(sem["z_turned"], at("z_turned", u, 1))
                if seen(u - 1):
                    act.wait_ge(sem["hid_second"], at("hid_second", u - 1, 2))
                go(zT[:, 0].rearrange("p n t -> p (n t)"), ps_f[:, 0:2 * P], ACT.Copy)\
                    .then_inc(sem["z_turned_copied"], 1)

            def f_relu(u, n):
                act.wait_ge(sem["hid_first"], at("hid_first", u, n + 1))
                if seen(u - 1):
                    act.wait_ge(sem["hid_split"], at("hid_split", u - 1, n + 1))
                go(f_h[:, 4 * n:4 * n + 4, :].rearrange("p c t -> p (c t)"), ps_f[:], ACT.Relu)\
                    .then_inc(sem["relu_done"], 1)

            def f_split_hid(u, n):
                act.wait_ge(sem["hid_ready"], at("hid_ready", u, n + 1))
                if seen(u - 1):
                    act.wait_ge(sem["y_done"], at("y_done", u - 1, 1))
                go(hT[:, 0, 4 * n:4 * n + 4, :].rearrange("p c t -> p (c t)"),
                   f_h[:, 4 * n:4 * n + 4, :].rearrange("p c t -> p (c t)"), ACT.Copy, scale=DOWN)\
                    .then_inc(sem["hid_hi"], 1)

            def a_spread(u, n):
                if n == 0:
                    if seen(u - 1):
                        act.wait_ge(sem["as_done"], at("as_done", u - 1, 4))
                act.wait_ge(sem["aq_turned"], at("aq_turned", u, n + 1))
                for h2 in range(2):
                    rows = slice(h2 * AD, (h2 + 1) * AD)
                    last = go(qz[rows, 8 * n + h2:8 * n + 8:2, :], tiles4(ps_a[1 - n][rows, :]),
                              ACT.Copy, scale=a_qk[rows, 0:1])
                last.then_inc(sem["aq_spread"], 1)

            def step(i, do_x, do_a, do_f):
                ua, uf = i - 1, i - 2
                ahead = do_x and not (isinstance(i, int) and i + 1 >= UNITS)
                if isinstance(i, int) and i == 1:
                    setup_nulls()
                    act.wait_ge(sem["set_dve"], 3)
                    act.wait_ge(sem["set_pool"], 2)
                for s in SLOTS:
                    if do_x:
                        for n in due("act_x_copy_k", s):
                            x_copy_k(i, n)
                        for n in due("act_x_copy_turned", s):
                            x_copy_turned(i)
                        for n in due("act_x_spread_q", s):
                            x_spread_q(i)
                        for n in due("act_x_copy_v", s):
                            x_copy_v(i, n)
                    if isinstance(i, int) and i == 0 and 2 <= s // 2 < 2 + len(pieces) - X_PIECES and s % 2 == 0:
                        split_hi(X_PIECES + s // 2 - 2)
                    if do_f:
                        for n in due("act_f_copy_turned", s):
                            f_copy_turned(uf)
                        for n in due("act_f_exp", s):
                            f_exp(uf)
                        for n in due("act_f_copy_z", s):
                            f_copy_z(uf)
                    if do_a:
                        for n in due("act_a_copy_turned", s):
                            a_copy_turned(ua, n)
                        for n in due("act_a_copy_k", s):
                            a_copy_raw(ua, 0, n)
                        for n in due("act_a_copy_q", s):
                            a_copy_raw(ua, 1, n)
                        for n in due("act_a_copy_v", s):
                            a_copy_v(ua, n)
                        for n in due("act_a_spread", s):
                            a_spread(ua, n)
                        for n in due("act_a_exp", s):
                            a_exp(ua, n)
                        for n in due("act_a_copy_probs", s):
                            a_copy_probs(ua, n)
                        for n in due("act_a_copy_pv", s):
                            a_copy_pv(ua, n)
                    if do_f:
                        for n in due("act_f_relu", s):
                            f_relu(uf, n)
                        for n in due("act_f_split_hid", s):
                            f_split_hid(uf, n)
                    if ahead:
                        for n in due("act_x_split_ctx", s):
                            x_split_ctx(i + 1)
                    if do_x:
                        t = s // 2
                        if s % 2 == 0 and 0 <= t < XTILES:
                            x_exp(i, t)
                        if s % 2 == 1 and 0 <= t - TURN_LAG < XTILES:
                            x_copy_probs(i, t - TURN_LAG)
                if do_x:
                    x_merge(i)

            split_hi(0)
            x_split_ctx(0)
            for n in range(1, X_PIECES):
                split_hi(n)
            act.wait_ge(sem["first_consts"], 48)
            steps(act, step)

        @block.vector
        def _(dve):
            tt, ts, stt = nc.vector.tensor_tensor, nc.vector.tensor_scalar, nc.vector.scalar_tensor_tensor

            def setup_table():
                dve.wait_ge(sem["set_pe"], 1)
                nc.vector.tensor_copy(reltab[:], ps_s[0][0:XH, 0:DIAGS]).then_inc(sem["set_dve"], 1)

            def setup():
                dve.wait_ge(sem["consts"], ALL_CONST)
                tt(a_qk[:], a_qs[:], a_ks[:], ALU.mult).then_inc(sem["set_dve"], 1)
                dve.wait_ge(sem["set_dve"], 2)
                ts(a_qk[:], a_qk[:], 8.0, None, ALU.mult).then_inc(sem["set_dve"], 1)
                dve.wait_ge(sem["set_pool"], 1)
                nc.vector.tensor_reduce(null_len[:, 0:1], null_sq[:], AX, ALU.add)\
                    .then_inc(sem["set_dve"], 1)
                ts(f_bo2[:], f_bo2[:], 2.0, None, ALU.mult).then_inc(sem["set_dve"], 1)
                ts(f_bis[:], f_bi[:], UP, None, ALU.mult).then_inc(sem["set_dve"], 1)
                dve.wait_ge(sem["set_dve"], 6)
                stt(f_bis[32:BIAS_ROWS, :], f_bi[32:BIAS_ROWS, :], UP, f_bis[32:BIAS_ROWS, :], ALU.mult, ALU.subtract)\
                    .then_inc(sem["set_dve"], 1)

            def split_lo(n):
                dve.wait_ge(sem["split_hi"], n + 1)
                src, hi, lo = staged(n)
                stt(lo, src, UP, hi, ALU.mult, ALU.subtract).then_inc(sem["split_lo"], 1)

            def stats(u, src, st, mv, name, k):
                nc.vector.bn_stats(st, src).then_inc(sem[name], 1)
                dve.wait_ge(sem[name], lone(dve, name, u, 2 * k + 1))
                nc.vector.bn_aggr(mv, st).then_inc(sem[name], 1)

            def norm(src, dst, mv, rs):
                return ts(dst, src, mv[:, 0:1], rs[:, 1:2], ALU.subtract, ALU.mult)

            def x_stats(u):
                dve.wait_ge(sem["x_loaded"], at("x_loaded", u, 16))
                stats(u, x_ld[:], x_st[:], x_mv[:], "x_stats", 0)

            def x_norm(u):
                if seen(u - 1):
                    dve.wait_ge(sem["x_turned"], at("x_turned", u - 1, 1))
                dve.wait_ge(sem["x_rstd"], at("x_rstd", u, 2))
                norm(x_ld[:], x_n[:], x_mv, x_rs).then_inc(sem["x_normed"], 1)

            def rest(to, of, less):
                return tt(to, of, less, ALU.subtract)

            def x_split_turned(u):
                dve.wait_ge(sem["x_turned_copied"], at("x_turned_copied", u, 1))
                flat = [xnT[:, k].rearrange("p c t -> p (c t)") for k in range(2)]
                rest(flat[1], ps_o[:, 0:2 * P], flat[0]).then_inc(sem["x_turned_copied"], 1)

            def x_spread_q(u):
                dve.wait_ge(sem["q_hi"], at("q_hi", u, 1))
                q = ps_o[:, 256:512].rearrange("p (n q) -> p n q", q=TQ)
                for h2 in range(2):
                    hi, lo = (qT[:, k, :, :, h2].rearrange("p g b q -> p (g b) q") for k in range(2))
                    last = stt(lo, q, parity_down[:, h2:h2 + 1], hi, ALU.mult, ALU.subtract)
                last.then_inc(sem["q_spread"], 1)

            def x_split_k(u, g):
                dve.wait_ge(sem["k_hi"], at("k_hi", u, g + 1))
                hi, lo = (kT[:, k, g].rearrange("p b k -> p (b k)") for k in range(2))
                stt(lo, ps_s[g][:], DOWN, hi, ALU.mult, ALU.subtract).then_inc(sem["k_copied"], 1)

            def x_bias(u, t):
                b, pair = t // XPAIRS, t % XPAIRS
                dve.wait_ge(sem["scores_done"], lone(dve, "scores_done", u, t + 1))
                if pair % (XPAIRS // 2) == 0:
                    dve.wait_ge(sem["bias_masked"], lone(dve, "bias_masked", u, t // (XPAIRS // 2) + 1))
                if t >= S_BUFS:
                    dve.wait_ge(sem["probs_turned"], lone(dve, "probs_turned", u, t - S_BUFS + 1))
                elif seen(u - 1):
                    dve.wait_ge(sem["probs_turned"], lone(dve, "probs_turned", u - 1, last_user(t, S_BUFS) + 1))
                nc.vector.tensor_tensor_reduce(
                    out=S[:, t % S_BUFS, :], in0=ps_s[t % 2][:, 0:TK], in1=bm[:, b, pair, :], scale=-1.0,
                    scalar=BIG, op0=ALU.add, op1=ALU.min, accum_out=x_nmx[:, t:t + 1])\
                    .then_inc(sem["biased"], 1)

            def x_scale(u, t):
                dve.wait_ge(sem["exp_done"], at("exp_done", u, t + 1))
                nc.vector.reciprocal(x_inv[:, t:t + 1], x_sum[:, t:t + 1]).then_inc(sem["recip_done"], 1)
                dve.wait_ge(sem["recip_done"], at("recip_done", u, t + 1))
                ts(S[:, t % S_BUFS, :], S[:, t % S_BUFS, :], x_inv[:, t:t + 1], None, ALU.mult)\
                    .then_inc(sem["probs_ready"], 1)

            def x_merge(u):
                dve.wait_ge(sem["merge_a"], at("merge_a", u, 1))
                o = ps_o[:].rearrange("p (g b h q) -> p g b h q", g=KD, b=BU, h=2)
                for g in range(KD):
                    stt(o_sum[:, g], o[:, g, :, 1, :], parity[:, 1:2], o_half[:, g], ALU.mult, ALU.add)\
                        .then_inc(sem["merge_b"], 1)
                dve.wait_ge(sem["merged"], at("merged", u, 1))
                rest(oT[:, 1], o_sum[:], oT[:, 0]).then_inc(sem["merged"], 1)

            def x_residual(u):
                dve.wait_ge(sem["xo_done"], at("xo_done", u, 1))
                dve.wait_ge(sem["x_kept"], at("x_kept", u, 1))
                if seen(u - 1):
                    dve.wait_ge(sem["a_kept"], at("a_kept", u - 1, 1))
                if seen(u - 1):
                    dve.wait_ge(sem["a_normed"], at("a_normed", u - 1, 1))
                stt(x1[:], ps_o[:, 0:D], DOWN, x_res[:], ALU.mult, ALU.add).then_inc(sem["x1_ready"], 1)

            def a_stats(u, k):
                src = (x1, a_x)[k]
                if k == 0:
                    dve.wait_ge(sem["x1_ready"], at("x1_ready", u, 1))
                else:
                    dve.wait_ge(sem["a_normed"], at("a_normed", u, 1))
                stats(u, src[:], a_st[:, k], a_mv[:, k], "a_stats", k)

            def a_norm(u, k):
                src, dst = ((x1, a_x), (a_x, a_n))[k]
                if seen(u - 1):
                    dve.wait_ge(sem["a_turned"], at("a_turned", u - 1, 1))
                dve.wait_ge(sem["a_rstd"], at("a_rstd", u, 2 * k + 2))
                norm(src[:], dst[:], a_mv[:, k], a_rs[:, k]).then_inc(sem["a_normed"], 1)

            def a_split_turned(u, n):
                if n == 0:
                    dve.wait_ge(sem["ax_split"], at("ax_split", u, 1))
                    rest(aT[:, 1].rearrange("p c t -> p (c t)"), ps_a[0][:, 0:2 * P],
                         aT[:, 0].rearrange("p c t -> p (c t)")).then_inc(sem["ax_split"], 1)
                else:
                    dve.wait_ge(sem["an_split"], at("an_split", u, 1))
                    rest(anT[:, 1], a_nT[:], anT[:, 0]).then_inc(sem["an_split"], 1)

            def a_lengths(u, which):
                dve.wait_ge(sem["a_squared"], at("a_squared", u, 2 * which + 2))
                nc.vector.tensor_reduce(a_len[:, which, :], a_sq[:, which], AX, ALU.add)\
                    .then_inc(sem["a_sumsq"], 1)

            def a_unit(u, which):
                dve.wait_ge(sem["a_len"], at("a_len", u, 2 * which + 2))
                tt(a_raw[:, which], a_raw[:, which],
                   a_len[:, which, :].unsqueeze(2).broadcast_to([P, AH, AD]), ALU.mult)\
                    .then_inc(sem["a_unit"], 1)

            def a_place_keys(u, n):
                if n == 0:
                    if seen(u - 1):
                        dve.wait_ge(sem["as_done"], at("as_done", u - 1, 4))
                dve.wait_ge(sem["ak_turned"], at("ak_turned", u, n + 1))
                nc.vector.tensor_copy(
                    akT[:, 4 * n:4 * n + 4, :, 0:TQ],
                    ps_a[1 - n][:].rearrange("p (j b t) -> p j b t", j=4, b=BU)).then_inc(sem["ak_placed"], 1)

            def a_bias(u, n):
                dve.wait_ge(sem["as_done"], at("as_done", u, n + 1))
                if n == 0:
                    if seen(u - 1):
                        dve.wait_ge(sem["ap_turned"], at("ap_turned", u - 1, 4))
                tt(aS[:, 4 * n:4 * n + 4, :], ps_a[(n + 1) % 2][:, 0:4 * AK].rearrange("p (h k) -> p h k", h=4),
                   alibi[:, 4 * n:4 * n + 4, :], ALU.add).then_inc(sem["as_biased"], 1)

            def a_softmax_top(u, part):
                h = slice(8 * part, 8 * part + 8)
                dve.wait_ge(sem["as_biased"], at("as_biased", u, 2 * part + 2))
                nc.vector.tensor_reduce(a_mx[:, h], aS[:, h, :], AX, ALU.max).then_inc(sem["a_soft"], 1)
                dve.wait_ge(sem["a_soft"], at("a_soft", u, 2 * part + 1))
                tt(aS[:, h, :], aS[:, h, :], a_mx[:, h].unsqueeze(2).broadcast_to([P, 8, AK]), ALU.subtract)\
                    .then_inc(sem["a_soft"], 1)

            def a_softmax_end(u, part):
                h = slice(8 * part, 8 * part + 8)
                dve.wait_ge(sem["a_exp"], at("a_exp", u, part + 1))
                nc.vector.tensor_reduce(a_sum[:, h], aS[:, h, :], AX, ALU.add).then_inc(sem["a_soft"], 1)
                dve.wait_ge(sem["a_soft"], at("a_soft", u, 4 + 3 * part + 1))
                nc.vector.reciprocal(a_sum[:, h], a_sum[:, h]).then_inc(sem["a_soft"], 1)
                dve.wait_ge(sem["a_soft"], at("a_soft", u, 4 + 3 * part + 2))
                tt(aS[:, h, :], aS[:, h, :], a_sum[:, h].unsqueeze(2).broadcast_to([P, 8, AK]), ALU.mult)\
                    .then_inc(sem["a_soft"], 1)

            def a_split_pv(u, n):
                dve.wait_ge(sem["apv_hi"], at("apv_hi", u, n + 1))
                hi, lo = (aoT[:, k, 4 * n:4 * n + 4, :].rearrange("p c t -> p (c t)") for k in range(2))
                rest(lo, ps_a[1 - n][:], hi).then_inc(sem["apv_copied"], 1)

            def a_residual(u):
                dve.wait_ge(sem["ao_done"], at("ao_done", u, 1))
                dve.wait_ge(sem["a_kept"], at("a_kept", u, 1))
                if seen(u - 1):
                    dve.wait_ge(sem["f_kept"], at("f_kept", u - 1, 1))
                if seen(u - 1):
                    dve.wait_ge(sem["f_normed"], at("f_normed", u - 1, 1))
                stt(x2[:], ps_a[1][:, 0:D], DOWN, a_res[:], ALU.mult, ALU.add).then_inc(sem["x2_ready"], 1)

            def f_stats(u):
                dve.wait_ge(sem["x2_ready"], at("x2_ready", u, 1))
                stats(u, x2[:], f_st[:], f_mv[:], "f_stats", 0)

            def f_norm(u):
                if seen(u - 1):
                    dve.wait_ge(sem["f_turned"], at("f_turned", u - 1, 1))
                dve.wait_ge(sem["f_rstd"], at("f_rstd", u, 2))
                norm(x2[:], f_n[:], f_mv, f_rs).then_inc(sem["f_normed"], 1)

            def f_split_turned(u):
                dve.wait_ge(sem["f_turned_copied"], at("f_turned_copied", u, 1))
                flat = [fT[:, k].rearrange("p c t -> p (c t)") for k in range(2)]
                rest(flat[1], ps_f[:, 0:2 * P], flat[0]).then_inc(sem["f_turned_copied"], 1)

            def f_split_z(u):
                dve.wait_ge(sem["z_turned_copied"], at("z_turned_copied", u, 1))
                flat = [zT[:, k].rearrange("p n t -> p (n t)") for k in range(2)]
                rest(flat[1], ps_f[:, 0:2 * P], flat[0]).then_inc(sem["z_turned_copied"], 1)

            def f_logits(u):
                dve.wait_ge(sem["z_done"], at("z_done", u, 1))
                if seen(u - 1):
                    dve.wait_ge(sem["z_routed"], at("z_routed", u - 1, 3))
                ts(z[:, 0:P], ps_f[:, 0:P], DOWN, None, ALU.mult).then_inc(sem["z_copied"], 1)
                stt(g_s[:], ps_f[:, P:P + E], DOWN, f_gb[:], ALU.mult, ALU.add).then_inc(sem["route"], 1)
                dve.wait_ge(sem["route"], at("route", u, 1))
                nc.vector.tensor_reduce(g_1[:, 0:1], g_s[:], AX, ALU.max, negate=True)\
                    .then_inc(sem["route"], 1)

            def f_route(u):
                dve.wait_ge(sem["f_exp"], at("f_exp", u, 1))
                nc.vector.reciprocal(g_1[:, 2:3], g_1[:, 1:2]).then_inc(sem["route"], 1)
                dve.wait_ge(sem["route"], at("route", u, 3))
                ts(g_s[:], g_e[:], g_1[:, 2:3], None, ALU.mult).then_inc(sem["route"], 1)
                dve.wait_ge(sem["route"], at("route", u, 4))
                mine = g_s[:].unsqueeze(2).broadcast_to([P, E, E])
                other = g_s[:].unsqueeze(1).broadcast_to([P, E, E])
                tt(g_gt[:], other, mine, ALU.is_gt)
                tt(g_eq[:], other, mine, ALU.is_equal).then_inc(sem["route"], 1)
                dve.wait_ge(sem["route"], at("route", u, 5))
                tt(g_eq[:], g_eq[:], lower[:], ALU.mult).then_inc(sem["route"], 1)
                dve.wait_ge(sem["route"], at("route", u, 6))
                tt(g_gt[:], g_gt[:], g_eq[:], ALU.add).then_inc(sem["route"], 1)
                dve.wait_ge(sem["route"], at("route", u, 7))
                nc.vector.tensor_reduce(g_rank[:], g_gt[:], AX, ALU.add).then_inc(sem["route"], 1)
                dve.wait_ge(sem["route"], at("route", u, 8))
                ts(g_sel[:, 0, :], g_rank[:], 0.0, None, ALU.is_equal)
                ts(g_sel[:, 1, :], g_rank[:], 1.0, None, ALU.is_equal)
                if seen(u - 1):
                    dve.wait_ge(sem["out_ready"], at("out_ready", u - 1, 1))
                stt(g_top[:], g_rank[:], 2.0, g_s[:], ALU.is_lt, ALU.mult, accum_out=g_1[:, 3:4])\
                    .then_inc(sem["route"], 1)
                dve.wait_ge(sem["route"], at("route", u, 9))
                zs = z[:, 0:P].rearrange("p (e r) -> p e r", e=E)
                if seen(u - 1):
                    dve.wait_ge(sem["z_turned"], at("z_turned", u - 1, 1))
                for n in range(2):
                    tt(zr[:, n], zs, g_sel[:, n, :].unsqueeze(2).broadcast_to([P, E, R]), ALU.mult)\
                        .then_inc(sem["z_routed"], 1)
                dve.wait_ge(sem["z_routed"], at("z_routed", u, 2))
                tt(zr[:, 2], zr[:, 1], zr[:, 0], ALU.subtract).then_inc(sem["z_routed"], 1)

            def f_second(u, n):
                dve.wait_ge(sem["hid_second"], at("hid_second", u, n + 1))
                h = f_h[:, 4 * n:4 * n + 4, :].rearrange("p c t -> p (c t)")
                stt(h, ps_f[:], 0.0, h, ALU.max, ALU.add).then_inc(sem["hid_ready"], 1)

            def f_split_hid(u, n):
                dve.wait_ge(sem["hid_hi"], at("hid_hi", u, n + 1))
                c = slice(4 * n, 4 * n + 4)
                stt(hT[:, 1, c, :], f_h[:, c, :], DOWN, hT[:, 0, c, :], ALU.mult, ALU.subtract)\
                    .then_inc(sem["hid_split"], 1)

            def f_final(u):
                dve.wait_ge(sem["y_done"], at("y_done", u, 1))
                if seen(u - 1):
                    dve.wait_ge(sem["out_stored"], at("out_stored", u - 1, 16))
                stt(f_out[:], ps_f[:, 0:D], DOWN, f_bo2[:], ALU.mult, ALU.add).then_inc(sem["y_sum"], 1)
                dve.wait_ge(sem["y_sum"], at("y_sum", u, 1))
                dve.wait_ge(sem["f_kept"], at("f_kept", u, 1))
                stt(f_out[:], f_out[:], g_1[:, 3:4], f_res[:], ALU.mult, ALU.add)\
                    .then_inc(sem["out_ready"], 1)

            setup_table()
            x_stats(0)
            split_lo(0)
            x_norm(0)
            for n in range(1, X_PIECES):
                split_lo(n)
            dve.wait_ge(sem["first_consts"], 48)

            def step(i, do_x, do_a, do_f):
                ua, uf = i - 1, i - 2
                ahead = do_x and not (isinstance(i, int) and i + 1 >= UNITS)
                for s in SLOTS:
                    if do_a:
                        for n in due("dve_x_residual", s):
                            x_residual(ua)
                    if do_x:
                        for n in due("dve_x_split_turned", s):
                            x_split_turned(i)
                        for n in due("dve_x_split_k", s):
                            x_split_k(i, n)
                        for n in due("dve_x_spread_q", s):
                            x_spread_q(i)
                    if do_f:
                        for n in due("dve_a_residual", s):
                            a_residual(uf)
                        for n in due("dve_f_stats", s):
                            f_stats(uf)
                    if do_a:
                        for n in due("dve_a_stats", s):
                            a_stats(ua, n)
                    if do_f:
                        for n in due("dve_f_norm", s):
                            f_norm(uf)
                    if do_a:
                        for n in due("dve_a_norm", s):
                            a_norm(ua, n)
                    if do_f:
                        for n in due("dve_f_split_turned", s):
                            f_split_turned(uf)
                        for n in due("dve_f_logits", s):
                            f_logits(uf)
                        for n in due("dve_f_route", s):
                            f_route(uf)
                        for n in due("dve_f_split_z", s):
                            f_split_z(uf)
                    if isinstance(i, int) and i == 0 and 2 <= s // 2 < 2 + len(pieces) - X_PIECES and s % 2 == 1:
                        split_lo(X_PIECES + s // 2 - 2)
                    if do_a:
                        for n in due("dve_a_split_turned", s):
                            a_split_turned(ua, n)
                        for n in due("dve_a_lengths", s):
                            a_lengths(ua, n)
                        for n in due("dve_a_unit", s):
                            a_unit(ua, n)
                        for n in due("dve_a_place_keys", s):
                            a_place_keys(ua, n)
                        for n in due("dve_a_bias", s):
                            a_bias(ua, n)
                        for n in due("dve_a_softmax_top", s):
                            a_softmax_top(ua, n)
                        for n in due("dve_a_softmax_end", s):
                            a_softmax_end(ua, n)
                        for n in due("dve_a_split_pv", s):
                            a_split_pv(ua, n)
                    if do_f:
                        for n in due("dve_f_second", s):
                            f_second(uf, n)
                        for n in due("dve_f_split_hid", s):
                            f_split_hid(uf, n)
                        for n in due("dve_f_final", s):
                            f_final(uf)
                    if ahead:
                        for n in due("dve_x_stats", s):
                            x_stats(i + 1)
                        for n in due("dve_x_norm", s):
                            x_norm(i + 1)
                    if do_x:
                        t = s // 2
                        if s % 2 == 0 and 0 <= t < XTILES:
                            x_bias(i, t)
                        if s % 2 == 1 and 0 <= t - 1 < XTILES:
                            x_scale(i, t - 1)
                if isinstance(i, int) and i == 0:
                    setup()
                if do_x:
                    x_merge(i)

            steps(dve, step)

        @block.gpsimd
        def _(pool):
            tt, ts = nc.gpsimd.tensor_tensor, nc.gpsimd.tensor_scalar

            def setup():
                pool.memset(half[:], -0.5).then_inc(sem["half"], 1)
                pool.memset(f_bi[:], 0.0).then_inc(sem["half"], 1)
                pool.wait_ge(sem["half"], 2)

            def setup_nulls():
                pool.wait_ge(sem["consts"], ALL_CONST)
                tt(null_sq[:], nulls[:], nulls[:], ALU.mult).then_inc(sem["set_pool"], 1)
                pool.memset(qz[:], 0.0).then_inc(sem["set_pool"], 1)
                pool.wait_ge(sem["set_dve"], 4)
                ts(null_len[:, 1:2], null_len[:, 0:1], 1e-24, None, ALU.max).then_inc(sem["half"], 1)
                pool.wait_ge(sem["half"], 3)
                tt(null_len[:, 1:2], null_len[:, 1:2], half[0:32, 0:1], ALU.pow).then_inc(sem["half"], 1)
                pool.wait_ge(sem["half"], 4)
                ts(nulls[:], nulls[:], null_len[:, 1:2], None, ALU.mult).then_inc(sem["set_pool"], 1)

            def rstd(u, mv, rs, stats, done, k):
                pool.wait_ge(sem[stats], lone(pool, stats, u, 2 * k + 2))
                ts(rs[:, 0:1], mv[:, 1:2], EPS, None, ALU.add).then_inc(sem[done], 1)
                pool.wait_ge(sem[done], lone(pool, done, u, 2 * k + 1))
                tt(rs[:, 1:2], rs[:, 0:1], half[:, 0:1], ALU.pow).then_inc(sem[done], 1)

            def x_rstd(u):
                if seen(u - 1):
                    pool.wait_ge(sem["x_normed"], lone(pool, "x_normed", u - 1, 1))
                rstd(u, x_mv, x_rs, "x_stats", "x_rstd", 0)

            def x_split_ctx(u):
                pool.wait_ge(sem["ctx_split"], lone(pool, "ctx_split", u, 1))
                tt(ctxS[:, 1].rearrange("p c n -> p (c n)"), ctxT[:].rearrange("p c b k -> p (c b k)"),
                   ctxS[:, 0].rearrange("p c n -> p (c n)"), ALU.subtract).then_inc(sem["ctx_split"], 1)

            def x_keep(u):
                pool.wait_ge(sem["x_loaded"], lone(pool, "x_loaded", u, 16))
                if seen(u - 1):
                    pool.wait_ge(sem["x1_ready"], lone(pool, "x1_ready", u - 1, 1))
                pool.tensor_copy(x_res[:], x_ld[:]).then_inc(sem["x_kept"], 1)

            def x_mask(u):
                pool.wait_ge(sem["mask_loaded"], lone(pool, "mask_loaded", u, 16))
                if seen(u - 1):
                    pool.wait_ge(sem["bias_masked"], lone(pool, "bias_masked", u - 1, 4))
                ts(negm[:].rearrange("p b k -> p (b k)"), mask32[:].bitcast(U8), MASKED, -MASKED, ALU.mult, ALU.add).then_inc(sem["mask_scaled"], 1)

            def x_bias(u, n):
                half_pairs = XPAIRS // 2
                b, pairs = n // 2, slice(n % 2 * half_pairs, (n % 2 + 1) * half_pairs)
                if n == 0:
                    pool.wait_ge(sem["mask_scaled"], lone(pool, "mask_scaled", u, 1))
                if seen(u - 1):
                    pool.wait_ge(sem["biased"], lone(pool, "biased", u - 1, half_pairs * (n + 1)))
                tt(bm[:, b, pairs], bias[:, pairs], negm[:, b, :].unsqueeze(1).broadcast_to([P, half_pairs, TK]),
                   ALU.add).then_inc(sem["bias_masked"], 1)

            def a_rstd(u, k):
                if seen(u - 1):
                    pool.wait_ge(sem["a_normed"], lone(pool, "a_normed", u - 1, k + 1))
                rstd(u, a_mv[:, k], a_rs[:, k], "a_stats", "a_rstd", k)

            def a_keep(u):
                pool.wait_ge(sem["x1_ready"], lone(pool, "x1_ready", u, 1))
                if seen(u - 1):
                    pool.wait_ge(sem["x2_ready"], lone(pool, "x2_ready", u - 1, 1))
                pool.tensor_copy(a_res[:], x1[:]).then_inc(sem["a_kept"], 1)

            def a_length(u, which):
                pool.wait_ge(sem["a_sumsq"], lone(pool, "a_sumsq", u, which + 1))
                if seen(u - 1):
                    pool.wait_ge(sem["a_unit"], lone(pool, "a_unit", u - 1, which + 1))
                ln = a_len[:, which, :]
                ts(ln, ln, 1e-24, None, ALU.max).then_inc(sem["a_len"], 1)
                pool.wait_ge(sem["a_len"], lone(pool, "a_len", u, 2 * which + 1))
                tt(ln, ln, half[:, 0:AH], ALU.pow).then_inc(sem["a_len"], 1)

            def f_keep(u):
                pool.wait_ge(sem["x2_ready"], lone(pool, "x2_ready", u, 1))
                if seen(u - 1):
                    pool.wait_ge(sem["out_ready"], lone(pool, "out_ready", u - 1, 1))
                pool.tensor_copy(f_res[:], x2[:]).then_inc(sem["f_kept"], 1)

            def f_rstd(u):
                if seen(u - 1):
                    pool.wait_ge(sem["f_normed"], lone(pool, "f_normed", u - 1, 1))
                rstd(u, f_mv, f_rs, "f_stats", "f_rstd", 0)

            setup()
            x_rstd(0)
            x_split_ctx(0)
            x_keep(0)
            x_mask(0)
            pool.wait_ge(sem["table_loaded"], 32)
            x_bias(0, 0)
            x_bias(0, 1)

            def step(i, do_x, do_a, do_f):
                ua, uf = i - 1, i - 2
                ahead = do_x and not (isinstance(i, int) and i + 1 >= UNITS)
                for s in SLOTS:
                    if do_f:
                        for n in due("pool_f_rstd", s):
                            f_rstd(uf)
                    if do_a:
                        for n in due("pool_a_rstd", s):
                            a_rstd(ua, n)
                        for n in due("pool_a_length", s):
                            a_length(ua, n)
                    if do_x:
                        for n in due("pool_x_keep", s):
                            if not (isinstance(i, int) and i == 0):
                                x_keep(i)
                    if do_a:
                        for n in due("pool_a_keep", s):
                            a_keep(ua)
                    if do_f:
                        for n in due("pool_f_keep", s):
                            f_keep(uf)
                    if do_x:
                        for n in due("pool_x_bias_second", s):
                            x_bias(i, 2 + n)
                    if ahead:
                        for n in due("pool_x_rstd", s):
                            x_rstd(i + 1)
                        for n in due("pool_x_mask", s):
                            x_mask(i + 1)
                        for n in due("pool_x_split_ctx", s):
                            x_split_ctx(i + 1)
                        for n in due("pool_x_bias_first", s):
                            x_bias(i + 1, n)
                if isinstance(i, int) and i == 0:
                    setup_nulls()

            steps(pool, step)


def kernel(**inputs):
    import concourse.bacc as bacc
    from concourse.bass_utils import run_bass_kernel_spmd

    a = {k: np.asarray(val) for k, val in inputs.items()}

    def t(name):
        return a[name].T

    null = a["L0_attn_null_kv"].reshape(AH, NNULL, 2, AD)
    arrays = dict(
        x=a["x"].reshape(B * TQ, D),
        ctxT=a["ctx_1024"].reshape(UNITS, BU, TK, KD, P).transpose(0, 4, 3, 1, 2).reshape(UNITS * P, KD * BU * TK),
        mask=a["mask_Bx1x1xS2_bk0"].reshape(UNITS, BU * TK).view(np.int32),
        wqT=t("L0_xattn_Wq"), wkT=t("L0_xattn_Wk"), wvT=t("L0_xattn_Wv"), woT=t("L0_xattn_Wo"),
        relT=t("L0_xattn_rel_bias"),
        a_g=a["L0_attn_norm_g"].reshape(KD, P).T, a_b=a["L0_attn_norm_b"].reshape(KD, P).T,
        a_wq=a["L0_attn_Wq"], a_wkv=a["L0_attn_Wkv"], a_wo=a["L0_attn_Wout"],
        a_qs=a["L0_attn_q_scale"].reshape(AD, 1), a_ks=a["L0_attn_k_scale"].reshape(AD, 1),
        null_k=null[:, :, 0, :].reshape(AH * NNULL, AD),
        null_v=null[:, :, 1, :].transpose(1, 0, 2).reshape(NNULL, INNER),
        f_wiT=t("L0_ffn_wi"), f_woT=t("L0_ffn_wo"),
        f_bi=a["L0_ffn_bi"].reshape(2, 4, P).transpose(1, 0, 2).reshape(4, 2 * P), f_bo=a["L0_ffn_bo"], f_gb=a["L0_ffn_gate_b"],
        f_zwT=np.concatenate([a["L0_ffn_lora_A"].reshape(E * R, D), a["L0_ffn_gate_w"]], axis=0).T,
        f_loraB=a["L0_ffn_lora_B"].transpose(0, 2, 1).reshape(E * R, FF),
        **constants(),
    )
    arrays = {k: np.ascontiguousarray(val) for k, val in arrays.items()}
    nc = bacc.Bacc("TRN2", target_bir_lowering=False, num_devices=1)
    io = {k: nc.dram_tensor("in_" + k, val.shape, mybir.dt.from_np(val.dtype), kind="ExternalInput").ap()
          for k, val in arrays.items()}
    out = nc.dram_tensor("out", [B * TQ, D], F32, kind="ExternalOutput").ap()
    build(nc, io, out)
    result = run_bass_kernel_spmd(nc, [{"in_" + k: val for k, val in arrays.items()}], core_ids=[0])
    return result.results[0]["out"].reshape(B, TQ, D)
```
